# Optimizing a Trainium2 kernel written in Bass

```python
import numpy as np
import jax
import jax.numpy as jnp

def _softmax(x, axis=-1):
    return jax.nn.softmax(x, axis=axis)

def _gelu(x):
    return jax.nn.gelu(x, approximate=True)

def _silu(x):
    return jax.nn.silu(x)

def _sigmoid(x):
    return jax.nn.sigmoid(x)

def _layernorm(x, axis=-1, eps=1e-05):
    m = jnp.mean(x, axis=axis, keepdims=True)
    v = jnp.var(x, axis=axis, keepdims=True)
    return (x - m) / jnp.sqrt(v + eps)

def _scatter_add(tgt, idx, src, axis=0):
    return tgt.at[idx].add(src)

def _segment_sum(src, seg, n):
    return jax.ops.segment_sum(src, seg, n)
kernel_name = 'mk_flamingo_gated_d1_seqx_r8_4a3276'

def setup_inputs(seed: int=0):
    np.random.seed(seed)
    _w = jnp.asarray

    def _rec_inputs():
        import jax
        import jax.numpy as jnp
        _rk = jax.random.key(seed)
        x = -0.0003929 + 0.9999 * jax.random.normal(jax.random.fold_in(_rk, 1), (8, 128, 256), jnp.float32)
        _lenS = 128 - jax.random.randint(jax.random.fold_in(_rk, 7), (8,), 0, max(1, 128 // 4) + 1, jnp.int32)
        _lenS2 = 128 - jax.random.randint(jax.random.fold_in(_rk, 8), (8,), 0, max(1, 128 // 4) + 1, jnp.int32)
        _ctx_2048P = jax.random.normal(jax.random.fold_in(_rk, 11), (8, 16, 256), jnp.float32)
        _ctx_2048c = jax.random.dirichlet(jax.random.fold_in(_rk, 511), 0.3 * jnp.ones((16,), jnp.float32), (8, 128))
        _ctx_2048t = jnp.einsum('bsk,bkd->bsd', _ctx_2048c, _ctx_2048P)
        _ctx_2048t = _ctx_2048t * jax.lax.rsqrt(jnp.mean(jnp.square(_ctx_2048t)) + 1e-12) * 0.953939
        ctx_2048 = -0.000514642 + 1.00011 * (_ctx_2048t + 0.3 * jax.random.normal(jax.random.fold_in(_rk, 611), (8, 128, 256), jnp.float32))
        _g = jax.random.normal(jax.random.fold_in(_rk, 9001), (2, 1), jnp.float32)
        _g = jnp.sign(_g) * jnp.maximum(jnp.abs(_g), 1.0) + (_g == 0) * 1.0
        g_xattn = _g[0]
        g_ffn = _g[1]
        return (x, ctx_2048, g_xattn, g_ffn)
    x, ctx_2048, g_xattn, g_ffn = _rec_inputs()

    def _L0_xattn_setup():
        import jax, jax.numpy as jnp
        import numpy as np
        NUM_HEADS = 16

        def _qdq(x):
            s = jnp.maximum(jnp.max(jnp.abs(x), axis=-1, keepdims=True) / 127.0, 1e-08)
            return jnp.clip(jnp.round(x / s), -127.0, 127.0) * s
        key = jax.random.key(seed)
        ks = jax.random.split(key, 8)
        B, N, M, D = (2, 512, 64, 256)
        w_std = 0.02
        return {'x': jax.random.normal(ks[0], (B, N, D), jnp.float32), 'cond': jax.random.normal(ks[1], (B, M, D), jnp.float32), 'wq': jax.random.normal(ks[2], (D, D), jnp.float32) * w_std, 'bq': jax.random.normal(ks[3], (D,), jnp.float32) * w_std, 'wkv': jax.random.normal(ks[4], (2 * D, D), jnp.float32) * w_std, 'bkv': jax.random.normal(ks[5], (2 * D,), jnp.float32) * w_std, 'wp': jax.random.normal(ks[6], (D, D), jnp.float32) * w_std, 'bp': jax.random.normal(ks[7], (D,), jnp.float32) * w_std}
    _L0_xattn_all = _L0_xattn_setup()
    _L0_xattn_in = {k: v for k, v in _L0_xattn_all.items() if k in ('wq', 'bq', 'wkv', 'bkv', 'wp', 'bp')}
    del _L0_xattn_all

    def _L0_ffn_setup():
        import jax, jax.numpy as jnp
        import numpy as np
        TOP_K = 6
        N_GROUP = 8
        TOPK_GROUP = 3
        CAPACITY = 96
        RSF = 1.0
        key = jax.random.key(seed)
        ks = jax.random.split(key, 8)
        B, S, H = (1, 512, 256)
        E, M = (64, 176)
        MS = 352
        sc = 0.02
        return {'hidden_states': jax.random.normal(ks[0], (B, S, H), jnp.float32), 'gate_weight': jax.random.normal(ks[1], (E, H), jnp.float32) * sc, 'Wg': jax.random.normal(ks[2], (E, M, H), jnp.float32) * sc, 'Wu': jax.random.normal(ks[3], (E, M, H), jnp.float32) * sc, 'Wd': jax.random.normal(ks[4], (E, H, M), jnp.float32) * sc, 'Sg': jax.random.normal(ks[5], (MS, H), jnp.float32) * sc, 'Su': jax.random.normal(ks[6], (MS, H), jnp.float32) * sc, 'Sd': jax.random.normal(ks[7], (H, MS), jnp.float32) * sc}
    _L0_ffn_all = _L0_ffn_setup()
    _L0_ffn_in = {k: v for k, v in _L0_ffn_all.items() if k in ('gate_weight', 'Wg', 'Wu', 'Wd', 'Sg', 'Su', 'Sd')}
    del _L0_ffn_all
    return {'x': x, 'ctx_2048': ctx_2048, 'g_xattn': g_xattn, 'g_ffn': g_ffn, 'L0_xattn_wq': _L0_xattn_in['wq'], 'L0_xattn_bq': _L0_xattn_in['bq'], 'L0_xattn_wkv': _L0_xattn_in['wkv'], 'L0_xattn_bkv': _L0_xattn_in['bkv'], 'L0_xattn_wp': _L0_xattn_in['wp'], 'L0_xattn_bp': _L0_xattn_in['bp'], 'L0_ffn_gate_weight': _L0_ffn_in['gate_weight'], 'L0_ffn_Wg': _L0_ffn_in['Wg'], 'L0_ffn_Wu': _L0_ffn_in['Wu'], 'L0_ffn_Wd': _L0_ffn_in['Wd'], 'L0_ffn_Sg': _L0_ffn_in['Sg'], 'L0_ffn_Su': _L0_ffn_in['Su'], 'L0_ffn_Sd': _L0_ffn_in['Sd']}

def reference(x, ctx_2048, g_xattn, g_ffn, L0_xattn_wq, L0_xattn_bq, L0_xattn_wkv, L0_xattn_bkv, L0_xattn_wp, L0_xattn_bp, L0_ffn_gate_weight, L0_ffn_Wg, L0_ffn_Wu, L0_ffn_Wd, L0_ffn_Sg, L0_ffn_Su, L0_ffn_Sd):
    import jax
    import jax.numpy as jnp

    def _L0_xattn_ref(x, cond, wq, bq, wkv, bkv, wp, bp):
        import jax, jax.numpy as jnp
        import numpy as np
        NUM_HEADS = 16

        def _qdq(x):
            s = jnp.maximum(jnp.max(jnp.abs(x), axis=-1, keepdims=True) / 127.0, 1e-08)
            return jnp.clip(jnp.round(x / s), -127.0, 127.0) * s
        B, N, C = x.shape
        M = cond.shape[1]
        H = NUM_HEADS
        Dh = C // H
        q = _qdq(x) @ _qdq(wq).T + bq
        kv = cond @ wkv.T + bkv
        k, v = jnp.split(kv, 2, axis=-1)
        q = q.reshape(B, N, H, Dh)
        k = k.reshape(B, M, H, Dh)
        v = v.reshape(B, M, H, Dh)
        scale = 1.0 / np.sqrt(Dh)
        attn = jax.nn.softmax(jnp.einsum('bnhd,bmhd->bhnm', q, k) * scale, axis=-1)
        o = jnp.einsum('bhnm,bmhd->bnhd', attn, v).reshape(B, N, C)
        out = _qdq(o) @ _qdq(wp).T + bp
        return out

    def _L0_ffn_ref(hidden_states, gate_weight, Wg, Wu, Wd, Sg, Su, Sd):
        import jax, jax.numpy as jnp
        import numpy as np
        TOP_K = 6
        N_GROUP = 8
        TOPK_GROUP = 3
        CAPACITY = 96
        RSF = 1.0
        B, S, H = hidden_states.shape
        E, M, _ = Wg.shape
        K, NG, TG, C = (TOP_K, N_GROUP, TOPK_GROUP, CAPACITY)
        x = hidden_states.reshape(-1, H)
        T = x.shape[0]
        logits = x.astype(jnp.float32) @ gate_weight.astype(jnp.float32).T
        scores = jax.nn.softmax(logits, axis=-1)
        group_scores = scores.reshape(T, NG, E // NG).max(axis=-1)
        _, gidx = jax.lax.top_k(group_scores, TG)
        gmask = jnp.zeros((T, NG), scores.dtype).at[jnp.arange(T)[:, None], gidx].set(1.0)
        smask = jnp.repeat(gmask, E // NG, axis=1)
        tmp_scores = jnp.where(smask > 0, scores, 0.0)
        topk_w, topk_i = jax.lax.top_k(tmp_scores, K)
        topk_w = topk_w * RSF
        flat = topk_i.reshape(-1)
        oh = jax.nn.one_hot(flat, E, dtype=jnp.int32)
        pos = jnp.sum(jnp.cumsum(oh, axis=0) * oh, axis=-1) - 1
        slot = flat * C + jnp.minimum(pos, C - 1)
        tok = jnp.arange(T * K) // K
        buf = jnp.zeros((E * C, H), x.dtype).at[slot].set(x[tok]).reshape(E, C, H)
        g = jnp.einsum('ech,emh->ecm', buf, Wg)
        u = jnp.einsum('ech,emh->ecm', buf, Wu)
        out = jnp.einsum('ecm,ehm->ech', jax.nn.silu(g) * u, Wd).reshape(E * C, H)
        yk = out[slot].reshape(T, K, H)
        y = jnp.sum(yk * topk_w[..., None].astype(yk.dtype), axis=1)
        shared = jax.nn.silu(x @ Sg.T) * (x @ Su.T) @ Sd.T
        return (y + shared).reshape(B, S, H)
    x = x + jnp.tanh(g_xattn[0]) * _L0_xattn_ref(_layernorm(x, axis=-1), ctx_2048, L0_xattn_wq, L0_xattn_bq, L0_xattn_wkv, L0_xattn_bkv, L0_xattn_wp, L0_xattn_bp)
    x = x + jnp.tanh(g_ffn[0]) * _L0_ffn_ref(_layernorm(x, axis=-1), L0_ffn_gate_weight, L0_ffn_Wg, L0_ffn_Wu, L0_ffn_Wd, L0_ffn_Sg, L0_ffn_Su, L0_ffn_Sd)
    return x

_drawn_inputs = setup_inputs


def setup_inputs(seed=0):
    import zlib

    import numpy as np

    out = dict(_drawn_inputs(seed))
    spreads = {}
    factors = {'L0_xattn_wq': 8.0,
     'L0_xattn_bq': 8.0,
     'L0_xattn_bkv': 8.0,
     'L0_xattn_bp': 3.658,
     'L0_ffn_gate_weight': 8.0,
     'L0_ffn_Wg': 8.0,
     'L0_ffn_Wu': 8.0,
     'L0_ffn_Wd': 8.0,
     'L0_ffn_Sg': 3.063,
     'L0_ffn_Su': 3.028,
     'L0_ffn_Sd': 3.034}
    for name, (base, spread) in spreads.items():
        noise = np.random.default_rng([zlib.crc32(name.encode()), seed]).standard_normal(out[name].shape)
        drawn = base * np.exp(spread * noise) if base else spread * noise
        out[name] = jnp.asarray(drawn.astype(out[name].dtype))
    for name, factor in factors.items():
        out[name] = (out[name] * factor).astype(out[name].dtype)
    return out
```

```python
import concourse.bass as bass
from concourse import mybir
from contextlib import ExitStack
import numpy as np

P = 128
TILES, TOK, D = 8, 128, 256
T = TILES * TOK
KC = D // P
HEADS, DH = 16, 16
VW = 32
PARTS = 3
Q_PART = [0, 0, 1, 0, 2, 1, 1, 2]
K_PART = [0, 1, 0, 2, 0, 1, 2, 1]
EXPERTS, GROUPS, TOPG, TOPK = 64, 8, 3, 6
GSIZE = EXPERTS // GROUPS
CAP = 96
M, MC = 176, 2
MH = M // MC
MS = 352
SCH = [(0, 128), (128, 128), (256, 96)]
ROW = D + EXPERTS
SPARE = T
LASTROW = T + CAP
ROWS = T + 2 * P
LAPS = TILES // 2 - 2
RING = 16
GBUF = 8
OBUF = 4
EPS = 1e-5
ROUND = 12582912.0
LOWEST = -87.33
MARK, CHOSEN = 1.0, 2.0
SCALE = 1.0 / float(np.sqrt(DH))


def gated_block(nc, a, out):
    f32, bf16, u32 = mybir.dt.float32, mybir.dt.bfloat16, mybir.dt.uint32
    ALU, ACT, AX = mybir.AluOpType, mybir.ActivationFunctionType, mybir.AxisListType
    ctx = ExitStack()
    with ctx:
        def sb(name, shape, dt=f32):
            return ctx.enter_context(nc.sbuf_tensor(name, shape, dt))

        def sem(name):
            return ctx.enter_context(nc.semaphore(name))

        def dram(name, shape, dt=f32):
            return nc.dram_tensor(name, shape, dt, kind="Internal").ap()

        q_parts = dram("q_parts", (PARTS, D, T), bf16)
        k_parts = dram("k_parts", (PARTS, D, T), bf16)
        table = dram("table", (ROWS, ROW))
        acc = [dram(f"acc{i}", (ROWS, D)) for i in range(2)]

        def carver(arena):
            at = [0]

            def cut(n, parts=P):
                at[0] += n
                return arena[0:parts, at[0] - n:at[0]]
            return cut

        stream = sb("stream", [P, 20 * T])
        cut = carver(stream)
        qs, ks = [cut(HEADS * T // 2).bitcast(bf16) for _ in range(2)]
        probs = [cut(HEADS * TOK) for _ in range(2)]
        cut = carver(stream)
        wgu, wdn = [], []
        for _ in range(RING):
            wgu.append(cut(KC * 2 * M).rearrange("p (k i m) -> p k i m", k=KC, i=2))
            wdn.append(cut(MC * D, MH).rearrange("p (c h) -> p c h", c=MC))
        scratch = sb("scratch", [P, 10880])
        cut = carver(scratch)
        xqT = cut(KC * T).rearrange("p (k t) -> p k t", k=KC)
        w_rows, w_fix = [cut(4 * D).rearrange("p (c h) -> p c h", c=4) for _ in range(2)]
        wkv = cut(KC * 2 * D).rearrange("p (k h) -> p k h", k=KC)
        part = [cut(PARTS * 256).bitcast(bf16).rearrange("p (r t) -> p r t", r=PARTS) for _ in range(2)]
        exact, rest = [[cut(512) for _ in range(2)] for _ in range(2)]
        values = cut(TILES * D)
        cut = carver(scratch)
        sact = cut(3 * T)
        sgate = [cut(512) for _ in range(2)]
        key, key2, overT = [cut(T, EXPERTS) for _ in range(3)]
        logit, pexp, over = [cut(TILES * EXPERTS).rearrange("p (b e) -> p b e", b=TILES) for _ in range(3)]
        eout = cut(TILES * (EXPERTS + 8 - TOPK)).rearrange("p (b e) -> p b e", b=TILES)
        cut = carver(scratch)
        gx = [cut(ROW, CAP) for _ in range(GBUF)]
        orow = [cut(D, CAP) for _ in range(OBUF)]
        gxT = [cut(KC * CAP).rearrange("p (k t) -> p k t", k=KC) for _ in range(2)]
        silu, hid = [[cut(MC * CAP, MH).rearrange("p (c t) -> p c t", c=MC) for _ in range(2)] for _ in range(2)]
        lastrow = cut(3 * D, EXPERTS).rearrange("p (i h) -> p i h", i=3)
        x = sb("x", [P, TILES, D])
        xn = sb("xn", [P, TILES, D])
        xq = sb("xq", [P, TILES, D])
        ctxT = sb("ctxT", [P, KC, T])
        hT = ctxT
        wp_int = sb("wp_int", [P, 2, D], bf16)
        wqT = sb("wqT", [P, KC, D])
        wpT = sb("wpT", [P, KC, D], bf16)
        bqk = sb("bqk", [P, 4])
        bvp = sb("bvp", [P, 2, D])
        gates = sb("gates", [P, 2])
        tg = sb("tg", [P, 2])
        rowmax = sb("rowmax", [P, 2, HEADS])
        negmax = sb("negmax", [P, 2, 2 * HEADS], bf16)
        negmaxT = [sb(f"negmaxT{i}", [P, TOK], bf16) for i in range(2)]
        pick = sb("pick", [P, HEADS, P], bf16)
        rden = sb("rden", [P, 2, HEADS])
        ident = sb("ident", [P, P])
        identb = sb("identb", [P, P], bf16)
        before = sb("before", [P, P])
        beforeb = sb("beforeb", [P, P], bf16)
        onesb = sb("onesb", [P, P], bf16)
        onesf = sb("onesf", [P, P])
        slotc = sb("slotc", [P, 2 + EXPERTS])
        tokv = xn[0:EXPERTS].rearrange("p b h -> p (b h)").rearrange("p (i t) -> p i t", i=2)
        zeros = sb("zeros", [P, 2 * ROW])
        stat = sb("stat", [P, TILES, 6])
        mv = sb("mv", [P, TILES, 2])
        veps = sb("veps", [P, TILES])
        neghalf = sb("neghalf", [P, TILES])
        rstd = sb("rstd", [P, TILES])
        nmr = sb("nmr", [P, TILES])
        amax = sb("amax", [P, TILES])
        qsc = sb("qsc", [P, TILES])
        qrs = sb("qrs", [P, TILES])
        oamax = sb("oamax", [P, TILES])
        osc = sb("osc", [P, TILES])
        ors = sb("ors", [P, TILES])
        wamax = sb("wamax", [P, 4])
        wsc = sb("wsc", [P, 4])
        wrs = sb("wrs", [P, 4])
        wdiag = sb("wdiag", [P, 2, P])
        wscale = sb("wscale", [P, D])
        oq = sb("oq", [P, TILES, D], bf16)
        oT = [sb(f"oT{i}", [P, KC, 2 * P], bf16) for i in range(2)]
        rows = sb("rows", [P, TILES, ROW])
        cut = carver(rows[:].rearrange("p b r -> p (b r)"))
        vpad = [cut(HEADS * VW) for _ in range(2)]
        headsT = [cut(4 * TOK) for _ in range(2)]
        gateT = sb("gateT", [P, KC, EXPERTS])
        lmax = sb("lmax", [P, TILES])
        total = sb("total", [P, TILES])
        rtotal = sb("rtotal", [P, TILES])
        gbest = sb("gbest", [P, TILES, GROUPS + 8 - TOPG])
        gtop = sb("gtop", [P, TILES, 8])
        g8 = sb("g8", [P, TILES, 8])
        e8 = sb("e8", [P, TILES, 8])
        gout = sb("gout", [P, TILES, GROUPS + 8 - TOPG])
        gcap = sb("gcap", [P, TILES, GROUPS])
        cand = sb("cand", [P, TILES, EXPERTS + 8 - TOPK])
        etop = sb("etop", [P, TILES, 8])
        sel = sb("sel", [P, TILES, EXPERTS], bf16)
        last = sb("last", [EXPERTS, 4])
        order = sb("order", [EXPERTS, CAP])
        slotv = sb("slotv", [CAP, 2, EXPERTS])
        empty = sb("empty", [CAP, EXPERTS])
        gidx = sb("gidx", [CAP, EXPERTS], u32)
        sidx = sb("sidx", [CAP, EXPERTS], u32)
        sgu = sb("sgu", [P, KC, 2, MS])
        sdn = sb("sdn", [P, 3, D])
        gcol = [sb(f"gcol{i}", [CAP, 1], u32) for i in range(GBUF)]
        scol = [sb(f"scol{i}", [CAP, 1], u32) for i in range(OBUF)]
        gw = [sb(f"gw{i}", [CAP, 1]) for i in range(2)]
        bank = [ctx.enter_context(nc.psum_tensor(f"bank{i}", [P, 512], f32)) for i in range(8)]

        got_x, got_w, got_ctx, got_kv, got_small, got_const, got_gate, got_tokv, got_shared = [
            sem(n) for n in ("got_x", "got_w", "got_ctx", "got_kv", "got_small", "got_const", "got_gate",
                             "got_tokv", "got_shared")]
        got_expert = [sem(f"got_expert{r}") for r in range(RING)]
        got_rows = [sem(f"got_rows{i}") for i in range(GBUF)]
        parts_out = [sem(f"parts_out{i}") for i in range(2)]
        got_k, got_q = sem("got_k"), sem("got_q")
        table_out = sem("table_out")
        acc_in = [sem(f"acc_in{i}") for i in range(2)]
        got_last = sem("got_last")
        got_acc = [sem(f"got_acc{i}") for i in range(4)]
        stored = sem("stored")
        pool_set, dve_chain, act_chain, pool_chain = sem("pool_set"), sem("dve_chain"), sem("act_chain"), sem("pool_chain")
        tanh_done, tbp_done, xp_done = sem("tanh_done"), sem("tbp_done"), sem("xp_done")
        consts_b = sem("consts_b")
        bn_done, bn2_done, veps_done, rstd_done, nmr_done, xn_done = [
            sem(n) for n in ("bn_done", "bn2_done", "veps_done", "rstd_done", "nmr_done", "xn_done")]
        xq_done, xqT_psum, xqT_done = sem("xq_done"), sem("xqT_psum"), sem("xqT_done")
        w_done, w_psum, wT_done = sem("w_done"), sem("w_psum"), sem("wT_done")
        unit_psum, unit_act, unit_rest, unit_mid, unit_lo = [
            sem(n) for n in ("unit_psum", "unit_act", "unit_rest", "unit_mid", "unit_lo")]
        v_psum, v_done = sem("v_psum"), sem("v_done")
        vpad_done, headsT_done, heads_psum = sem("vpad_done"), sem("headsT_done"), sem("heads_psum")
        s_psum, max_done, split_done, nm_psum, nm_done, st_psum, exp_done, pv_psum, norm_done, oq_done, att_chain = [
            sem(n) for n in ("s_psum", "max_done", "split_done", "nm_psum", "nm_done", "st_psum", "exp_done",
                             "pv_psum", "norm_done", "oq_done", "att_chain")]
        oT_psum, oT_done, y_psum, y1_done, x2_done = [
            sem(n) for n in ("oT_psum", "oT_done", "y_psum", "y1_done", "x2_done")]
        h_done, hT_psum, hT_done, logit_psum, shift_done, pexp_done = [
            sem(n) for n in ("h_done", "hT_psum", "hT_done", "logit_psum", "shift_done", "pexp_done")]
        wrow_done, sel_done, selT_psum, key_done, pos_psum, over_done, overT_psum, overT_done = [
            sem(n) for n in ("wrow_done", "sel_done", "selT_psum", "key_done", "pos_psum", "over_done",
                             "overT_psum", "overT_done")]
        order_done, slot_psum, idx_done = sem("order_done"), sem("slot_psum"), sem("idx_done")
        sg_psum, sgate_done, sact_done, sd_psum, base_done = [
            sem(n) for n in ("sg_psum", "sgate_done", "sact_done", "sd_psum", "base_done")]
        gT_psum, gxT_done, up_psum, silu_done, hid_done, down_psum, gw_done, orow_done, gcol_done, scol_done = [
            sem(n) for n in ("gT_psum", "gxT_done", "up_psum", "silu_done", "hid_done", "down_psum", "gw_done",
                             "orow_done", "gcol_done", "scol_done")]
        last_done, corr_psum, sum_done, y_done = [sem(n) for n in ("last_done", "corr_psum", "sum_done", "y_done")]

        FILL = [2 * 16, (TILES // 2 + 1) * 16]
        units = [("k", c, s) for c in range(KC) for s in range(2)] + [("q", c, s) for c in range(KC) for s in range(2)]
        token_rows = lambda t, n: t.rearrange("(a p) h -> p a h", p=P)[:, n]
        block = ctx.enter_context(nc.Block())

        @block.sync
        def _(sp):
            sp.dma_start(ctxT[:], a["ctxT"]).then_inc(got_ctx, 16)
            sp.dma_start(wkv, a["wkv"]).then_inc(got_kv, 16)
            sp.dma_start(x[:], a["x"]).then_inc(got_x, 16)
            sp.dma_start(bqk[:], a["bqk"]).then_inc(got_small, 16)
            sp.dma_start(gates[:], a["gates"].broadcast_to([P, 2])).then_inc(got_small, 16)
            sp.dma_start(w_rows, a["w_rows"]).then_inc(got_w, 16)
            for i, t in enumerate((ident, before)):
                sp.dma_start(t[:], a["consts"][:, P * i:P * i + P]).then_inc(got_const, 16)
            sp.dma_start(slotc[:], a["consts"][:, 2 * P:]).then_inc(got_const, 16)
            for i in range(2):
                sp.dma_start(bvp[:, i], a["bvp"][i:i + 1].broadcast_to([P, D])).then_inc(got_small, 16)
            sp.dma_start(gateT[:], a["gateT"]).then_inc(got_gate, 16)
            sp.wait_ge(pool_set, 1)
            sp.dma_start(table[T:ROWS].rearrange("(p a) h -> p (a h)", p=P), zeros[:]).then_inc(table_out, 16)
            for u, (what, c, s) in enumerate(units):
                dst = k_parts if what == "k" else q_parts
                sp.wait_ge(unit_lo, u + 1)
                sp.dma_start(dst[:, P * c:P * c + P, 512 * s:512 * s + 512].rearrange("r p t -> p r t"),
                             part[u % 2]).then_inc(parts_out[u % 2], 16)
                if u % 4 == 3:
                    for i in range(2):
                        sp.wait_ge(parts_out[i], 16 * (u // 2 + 1))
                    stack, order_of, got = (ks, K_PART, got_k) if what == "k" else (qs, Q_PART, got_q)
                    for r, p in enumerate(order_of):
                        sp.dma_start(stack[DH * r:DH * r + DH].rearrange("d (h t) -> d h t", h=HEADS),
                                     dst[p].rearrange("(h d) t -> d h t", d=DH)).then_inc(got, 16)
            sp.dma_start(sgu[:], a["sgu"]).then_inc(got_shared, 16)
            sp.dma_start(sdn[:, 0:2], a["sdn"][0:2 * P].rearrange("(c p) h -> p c h", p=P)).then_inc(got_shared, 16)
            sp.dma_start(sdn[0:SCH[2][1], 2], a["sdn"][2 * P:MS]).then_inc(got_shared, 16)
            sp.wait_ge(oq_done, TILES)
            sp.dma_start(tokv, a["tokv"]).then_inc(got_tokv, 16)
            sp.wait_ge(pv_psum, TILES + 2)
            for r in range(RING):
                sp.dma_start(wgu[r], a["wgu"][r]).then_inc(got_expert[r], 16)
                sp.dma_start(wdn[r], a["wdn"][r]).then_inc(got_expert[r], 16)
            for b in range(0, TILES, 2):
                sp.wait_ge(wrow_done, 1)
                for n in (b, b + 1):
                    sp.dma_start(table[P * n:P * n + P], rows[:, n]).then_inc(table_out, 16)
            with sp.Fori(0, EXPERTS // RING - 1) as lap:
                for r in range(RING):
                    sp.wait_ge(down_psum, lap * RING + r + 3)
                    sp.nop(nofuse=True)
                    for t, src in ((wgu, "wgu"), (wdn, "wdn")):
                        sp.dma_start(t[r], a[src][bass.ds(lap * RING + RING + r, 1)].squeeze(0)).then_inc(got_expert[r], 16)
            for i in range(2):
                sp.wait_ge(acc_in[i], FILL[i] + 16 * EXPERTS // 2)
            for i in range(2):
                sp.dma_start(lastrow[:, i], acc[i][LASTROW:LASTROW + EXPERTS]).then_inc(got_last, 16)
            for j in range(4):
                for i, t in enumerate((xn, xq)):
                    sp.dma_start(t[:, 2 * j:2 * j + 2], token_rows(acc[i][0:T], slice(2 * j, 2 * j + 2))).then_inc(got_acc[j], 16)
            for j in range(4):
                sp.wait_ge(y_done, j + 1)
                sp.dma_start(out[2 * j:2 * j + 2].rearrange("b p h -> p b h"), xn[:, 2 * j:2 * j + 2]).then_inc(stored, 16)
            sp.wait_ge(stored, 64)

        @block.gpsimd
        def _(pool):
            g = nc.gpsimd
            g.memset(zeros[:], 0.0).then_inc(pool_set, 1)
            pool.wait_ge(pool_set, 1)
            g.dma_start(acc[0][0:T].rearrange("(p a) h -> p a h", p=P),
                        zeros[:, 0:D].unsqueeze(1).broadcast_to([P, TILES, D])).then_inc(acc_in[0], 16)
            for i in range(2):
                g.dma_start(acc[i][T:ROWS].rearrange("(p a) h -> p (a h)", p=P), zeros[:, 0:2 * D]).then_inc(acc_in[i], 16)
            g.memset(neghalf[:], -0.5).then_inc(pool_set, 1)
            g.memset(onesb[:], 1.0).then_inc(pool_set, 1)
            g.memset(onesf[:], 1.0).then_inc(pool_set, 1)
            g.memset(vpad[0], 0.0).then_inc(pool_set, 1)
            g.memset(vpad[1], 0.0).then_inc(pool_set, 1)
            for i in range(2):
                g.memset(negmaxT[i][:], 0.0).then_inc(pool_set, 1)
            g.memset(gbest[:], MARK).then_inc(pool_set, 1)
            g.memset(gtop[:], MARK).then_inc(pool_set, 1)
            g.memset(cand[:], MARK).then_inc(pool_set, 1)
            g.memset(etop[:], MARK).then_inc(pool_set, 1)
            pool.wait_ge(pool_set, 6)
            for i in range(2):
                g.memset(vpad[i].rearrange("p (h e) -> p h e", h=HEADS)[:, :, DH:DH + 1], 1.0).then_inc(pool_set, 1)
            pool.wait_ge(got_const, 48)
            g.tensor_copy(identb[:], ident[:]).then_inc(consts_b, 1)
            g.tensor_copy(beforeb[:], before[:]).then_inc(consts_b, 1)
            g.tensor_tensor(pick[:], ident[:, 0:HEADS].unsqueeze(2).broadcast_to([P, HEADS, P]),
                            ident[:, HEADS:2 * HEADS].unsqueeze(2).broadcast_to([P, HEADS, P]), ALU.add).then_inc(consts_b, 1)
            pool.wait_ge(veps_done, 1)
            pool.wait_ge(pool_set, 2)
            g.tensor_tensor(rstd[:], veps[:], neghalf[:], ALU.pow).then_inc(rstd_done, 1)
            for u in range(len(units)):
                pool.wait_ge(unit_rest, u + 1)
                g.tensor_copy(part[u % 2][:, 1], rest[u % 2]).then_inc(unit_mid, 1)
                if u == 3:
                    pool.wait_ge(tbp_done, 1)
                    for b in range(TILES):
                        pool.wait_ge(xn_done, b + 1)
                        g.tensor_tensor(x[:, b], x[:, b], bvp[:, 1], ALU.add).then_inc(xp_done, 1)
            def stationary_values(b, u):
                pool.wait_ge(pv_psum, b + 1)
                pool.nop(nofuse=True)
                g.tensor_copy(vpad[u].rearrange("p (h e) -> p h e", h=HEADS)[:, :, 0:DH],
                              values[:, bass.ds(b * D, D)].rearrange("p (h d) -> p h d", h=HEADS)).then_inc(vpad_done, 1)

            pool.wait_ge(v_done, TILES)
            pool.wait_ge(pool_set, 14)
            with pool.Fori(0, TILES // 2) as pair:
                for u in range(2):
                    stationary_values(pair * 2 + u, u)
            for b in range(TILES):
                pool.wait_ge(y1_done, b + 1)
                if b == 0:
                    pool.wait_ge(xp_done, TILES)
                g.tensor_tensor(x[:, b], xq[:, b], x[:, b], ALU.add).then_inc(x2_done, 1)
            pool.wait_ge(veps_done, 2)
            g.tensor_tensor(rstd[:], veps[:], neghalf[:], ALU.pow).then_inc(rstd_done, 1)

            for b in range(0, TILES, 2):
                pool.wait_ge(base_done, b + 2)
                g.dma_start(token_rows(acc[1][0:T], slice(b, b + 2)), x[:, b:b + 2]).then_inc(acc_in[1], 16)

            def gather(i):
                g.indirect_dma_start(gx[i], None, table, bass.IndirectOffsetOnAxis(gcol[i][:], 0)).then_inc(got_rows[i], 16)

            pool.wait_ge(table_out, 16 * (TILES + 1))
            for e in range(GBUF):
                pool.wait_ge(gcol_done, e + 1)
                gather(e)

            def expert(e, half, r, more):
                pool.wait_ge(scol_done, e + 1)
                pool.wait_ge(orow_done, e + 3)
                pool.wait_ge(acc_in[r % 2], FILL[r % 2] + 16 * half)
                pool.nop(nofuse=True)
                g.indirect_dma_start(acc[r % 2], bass.IndirectOffsetOnAxis(scol[r % OBUF][:], 0), orow[r % OBUF], None,
                                     compute_op=ALU.add).then_inc(acc_in[r % 2], 16)
                if more:
                    pool.wait_ge(gcol_done, e + GBUF + 1)
                    pool.nop(nofuse=True)
                    gather(r % GBUF)

            with pool.Fori(0, EXPERTS // RING - 1) as lap:
                for r in range(RING):
                    expert(lap * RING + r, lap * (RING // 2) + r // 2, r, True)
            for r in range(RING):
                e = EXPERTS - RING + r
                expert(e, e // 2, r, e + GBUF < EXPERTS)

        @block.scalar
        def _(act):
            s = nc.scalar
            act.sem_inc(exp_done, 2)
            act.sem_inc(headsT_done, 2)
            act.sem_inc(orow_done, 2)
            act.wait_ge(got_small, 64)
            s.activation(tg[:], gates[:], ACT.Tanh).then_inc(tanh_done, 1)

            def unit(u):
                what, c, _ = units[u]
                col = c if what == "q" else KC + c
                act.wait_ge(unit_psum, u + 1)
                if u >= 2:
                    act.wait_ge(unit_rest, u - 1)
                s.activation(exact[u % 2], bank[u % 2][:], ACT.Identity, bias=bqk[:, col:col + 1]).then_inc(unit_act, 1)
                if u >= 2:
                    act.wait_ge(parts_out[u % 2], 16 * (u // 2))
                s.activation(part[u % 2][:, 0], bank[u % 2][:], ACT.Identity, bias=bqk[:, col:col + 1]).then_inc(unit_act, 1)

            for u in range(4):
                unit(u)
            act.wait_ge(nmr_done, 1)
            for b in range(TILES):
                s.activation(xn[:, b], x[:, b], ACT.Identity, bias=nmr[:, b:b + 1], scale=rstd[:, b:b + 1]).then_inc(xn_done, 1)
            act.wait_ge(w_psum, 1)
            s.activation(wqT[:].rearrange("p k (c o) -> p c k o", c=2), bank[4][:].rearrange("p (c k o) -> p c k o", c=2, k=KC), ACT.Copy).then_inc(wT_done, 1)
            act.wait_ge(w_psum, 2)
            s.activation(wpT[:].rearrange("p k (c o) -> p c k o", c=2), bank[5][:, 0:256].bitcast(bf16).rearrange("p (c k o) -> p c k o", c=2, k=KC), ACT.Copy).then_inc(wT_done, 1)
            for j in range(4):
                act.wait_ge(xqT_psum, j + 1)
                s.activation(xqT[:, :, 256 * j:256 * j + 256], bank[2 + j % 2][:].rearrange("p (k t) -> p k t", k=KC), ACT.Copy).then_inc(xqT_done, 1)
            for u in range(4, 8):
                unit(u)

            def negmax_across(b, u):
                act.wait_ge(nm_psum, b + 1)
                act.nop(nofuse=True)
                s.activation(negmaxT[u][0:2 * HEADS], bank[7][0:2 * HEADS, 0:TOK // 2].bitcast(bf16), ACT.Copy).then_inc(nm_done, 1)

            def heads_out(b, u):
                act.wait_ge(pv_psum, b + 3)
                act.wait_ge(heads_psum, b + 1)
                act.nop(nofuse=True)
                s.activation(headsT[u], bank[4 + u][:], ACT.Copy).then_inc(headsT_done, 1)

            def attend(b, u, more=True):
                for g in range(4):
                    act.wait_ge(st_psum, 4 * b + g + 1)
                    if g == 0:
                        act.wait_ge(pv_psum, b + 1)
                    act.nop(nofuse=True)
                    s.activation(probs[u][:, 512 * g:512 * g + 512], bank[2 + g % 2][:], ACT.Exp, scale=SCALE).then_inc(exp_done, 1)
                if more:
                    negmax_across(b + 1, 1 - u)
                heads_out(b, u)

            act.wait_ge(pool_set, 8)
            negmax_across(0, 0)
            with act.Fori(0, TILES // 2 - 1) as pair:
                for u in range(2):
                    attend(pair * 2 + u, u)
            attend(TILES - 2, 0)
            attend(TILES - 1, 1, False)

            for j in range(4):
                act.wait_ge(oT_psum, j + 1)
                if j >= 2:
                    act.wait_ge(y_psum, j - 1)
                s.activation(oT[j % 2][:], bank[j % 2][:, 0:256].bitcast(bf16).rearrange("p (k t) -> p k t", k=KC), ACT.Copy).then_inc(oT_done, 1)
            act.wait_ge(nmr_done, 2)
            for b in range(TILES):
                s.activation(rows[:, b, 0:D], x[:, b], ACT.Identity, bias=nmr[:, b:b + 1], scale=rstd[:, b:b + 1]).then_inc(h_done, 1)
                if b % 2:
                    j = b // 2
                    if j:
                        act.wait_ge(hT_psum, j)
                        s.activation(hT[:, :, 256 * (j - 1):256 * j], bank[4 + (j - 1) % 2][:].rearrange("p (k t) -> p k t", k=KC), ACT.Copy).then_inc(hT_done, 1)
            act.wait_ge(hT_psum, 4)
            s.activation(hT[:, :, 768:1024], bank[5][:].rearrange("p (k t) -> p k t", k=KC), ACT.Copy).then_inc(hT_done, 1)
            act.wait_ge(shift_done, 1)
            for b in range(TILES):
                s.activation(pexp[:, b], logit[:, b], ACT.Exp, accum_out=total[:, b:b + 1]).then_inc(pexp_done, 1)

            for u in range(6):
                act.wait_ge(sg_psum, u + 1)
                if u >= 2:
                    act.wait_ge(sact_done, u - 1)
                n = SCH[u // 2][1]
                s.activation(sgate[u % 2][0:n], bank[2 * (u % 2)][0:n], ACT.Silu).then_inc(sgate_done, 1)
            for j in range(2):
                act.wait_ge(overT_psum, j + 1)
                s.activation(overT[:, 512 * j:512 * j + 512], bank[7][0:EXPERTS], ACT.Copy).then_inc(overT_done, 1)

            def expert(e, half, r):
                p = r % 2
                act.wait_ge(up_psum, e + 3)
                act.wait_ge(hid_done, e + 1)
                act.nop(nofuse=True)
                s.activation(silu[p], bank[2 + p][0:MH, 0:MC * CAP].rearrange("p (c t) -> p c t", c=MC), ACT.Silu).then_inc(silu_done, 1)
                act.wait_ge(down_psum, e + 3)
                act.wait_ge(gw_done, e + 1)
                act.wait_ge(acc_in[p], FILL[p] + 16 * half - 16)
                act.nop(nofuse=True)
                s.activation(orow[r % OBUF], bank[4 + p][0:CAP, 0:D], ACT.Copy, scale=gw[p][:]).then_inc(orow_done, 1)

            with act.Fori(0, EXPERTS // RING - 1) as lap:
                for r in range(RING):
                    expert(lap * RING + r, lap * (RING // 2) + r // 2, r)
            for r in range(RING):
                e = EXPERTS - RING + r
                expert(e, e // 2, r)

        @block.vector
        def _(dve):
            v = nc.vector
            dve.sem_inc(norm_done, 1)
            dve.sem_inc(gxT_done, 2)
            dve.sem_inc(hid_done, 2)
            chain = [0]

            def link(ins):
                chain[0] += 1
                ins.then_inc(dve_chain, 1)
                dve.wait_ge(dve_chain, chain[0])

            def rest_of(u):
                dve.wait_ge(unit_act, 2 * u + 2)
                if u >= 2:
                    dve.wait_ge(unit_mid, u - 1)
                v.tensor_tensor(rest[u % 2], exact[u % 2], part[u % 2][:, 0], ALU.subtract).then_inc(unit_rest, 1)

            def low_of(u):
                dve.wait_ge(unit_mid, u + 1)
                dve.wait_ge(unit_rest, u + 1)
                v.tensor_tensor(part[u % 2][:, 2], rest[u % 2], part[u % 2][:, 1], ALU.subtract).then_inc(unit_lo, 1)

            def stats(b, done):
                v.bn_stats(stat[:, b], x[:, b]).then_inc(done, 1)

            def norm_scalars(done, base):
                for b in range(TILES):
                    dve.wait_ge(done, b + 1)
                    i = v.bn_aggr(mv[:, b], stat[:, b])
                    link(i)
                v.tensor_scalar(veps[:], mv[:, :, 1], EPS, None, ALU.add).then_inc(veps_done, 1)
                dve.wait_ge(rstd_done, base)
                v.scalar_tensor_tensor(out=nmr[:], in0=mv[:, :, 0], scalar=-1.0, in1=rstd[:], op0=ALU.mult, op1=ALU.mult).then_inc(nmr_done, 1)

            dve.wait_ge(got_x, 16)
            for b in range(TILES):
                stats(b, bn_done)
            norm_scalars(bn_done, 1)
            rest_of(0)
            dve.wait_ge(got_w, 16)
            link(v.tensor_reduce(wamax[:], w_rows, AX.X, ALU.max, apply_absolute_value=True))
            link(v.tensor_scalar(wsc[:], wamax[:], 1.0 / 127.0, 1e-8, ALU.mult, ALU.max))
            link(v.reciprocal(wrs[:], wsc[:]))
            low_of(0)
            rest_of(1)
            for i in range(4):
                link(v.tensor_scalar(w_fix[:, i], w_rows[:, i], wrs[:, i:i + 1], ROUND, ALU.mult, ALU.add))
            low_of(1)
            rest_of(2)
            dve.wait_ge(got_const, 48)
            for i in range(2):
                v.tensor_scalar(w_rows[:, i], w_fix[:, i], ROUND, wsc[:, i:i + 1], ALU.subtract, ALU.mult).then_inc(w_done, 1)
                v.tensor_scalar(wp_int[:, i], w_fix[:, 2 + i], ROUND, None, ALU.subtract).then_inc(w_done, 1)
                v.tensor_scalar(wdiag[:, i], ident[:], wsc[:, 2 + i:3 + i], None, ALU.mult).then_inc(w_done, 1)
            low_of(2)
            rest_of(3)
            dve.wait_ge(xn_done, TILES)
            link(v.tensor_reduce(amax[:], xn[:], AX.X, ALU.max, apply_absolute_value=True))
            low_of(3)
            link(v.tensor_scalar(qsc[:], amax[:], 1.0 / 127.0, 1e-8, ALU.mult, ALU.max))
            link(v.reciprocal(qrs[:], qsc[:]))
            for b in range(TILES):
                link(v.tensor_scalar(xn[:, b], xn[:, b], qrs[:, b:b + 1], ROUND, ALU.mult, ALU.add))
                v.tensor_scalar(xq[:, b], xn[:, b], ROUND, qsc[:, b:b + 1], ALU.subtract, ALU.mult).then_inc(xq_done, 1)
            dve.wait_ge(tanh_done, 1)
            dve.wait_ge(got_small, 64)
            v.tensor_scalar(bvp[:, 1], bvp[:, 1], tg[:, 0:1], None, ALU.mult).then_inc(tbp_done, 1)
            for b in range(TILES):
                dve.wait_ge(v_psum, b // 2 + 1)
                v.tensor_tensor(values[:, D * b:D * b + D], bank[(2, 3, 6, 7)[b // 2]][:, D * (b % 2):D * (b % 2) + D], bvp[:, 0], ALU.add).then_inc(v_done, 1)
            dve.wait_ge(w_psum, 3)
            v.tensor_scalar(wscale[:], bank[5][:, 256:512], tg[:, 0:1], None, ALU.mult).then_inc(wT_done, 1)
            for u in range(4, 8):
                rest_of(u)
                low_of(u)

            def maximum(b, u, g):
                dve.wait_ge(s_psum, 4 * b + g + 1)
                dve.nop(nofuse=True)
                v.tensor_reduce(rowmax[:, u, 4 * g:4 * g + 4], bank[g % 2][:].rearrange("p (h m) -> p h m", h=4), AX.X, ALU.max).then_inc(max_done, 1)

            def split_max(b, u):
                dve.wait_ge(max_done, 4 * b + 4)
                dve.nop(nofuse=True)
                v.tensor_scalar(negmax[:, u, 0:HEADS], rowmax[:, u], -1.0, None, ALU.mult).then_inc(split_done, 1)
                dve.wait_ge(split_done, 2 * b + 1)
                dve.nop(nofuse=True)
                v.scalar_tensor_tensor(out=negmax[:, u, HEADS:2 * HEADS], in0=rowmax[:, u], scalar=-1.0, in1=negmax[:, u, 0:HEADS],
                                       op0=ALU.mult, op1=ALU.subtract).then_inc(split_done, 1)

            heads_out = bank[6][:].rearrange("p (h e) -> p h e", e=VW)
            xq_flat = xq[:].rearrange("p b h -> p (b h)")
            xn_flat = xn[:].rearrange("p b h -> p (b h)")
            oq_flat = oq[:].rearrange("p b h -> p (b h)")
            STEPS = 5

            def finish(b, u):
                o_b = xq_flat[:, bass.ds(b * D, D)]
                r_b = xn_flat[:, bass.ds(b * D, D)]
                one = bass.ds(b, 1)
                dve.wait_ge(heads_psum, b + 3)
                dve.nop(nofuse=True)
                v.reciprocal(rden[:, u], heads_out[:, :, DH]).then_inc(att_chain, 1)
                dve.wait_ge(att_chain, STEPS * b + 1)
                dve.nop(nofuse=True)
                v.tensor_tensor(o_b.rearrange("p (h d) -> p h d", h=HEADS), heads_out[:, :, 0:DH],
                                rden[:, u].unsqueeze(2).broadcast_to([P, HEADS, DH]), ALU.mult).then_inc(norm_done, 1)
                dve.wait_ge(norm_done, b + 2)
                dve.nop(nofuse=True)
                v.tensor_reduce(oamax[:, one], o_b, AX.X, ALU.max, apply_absolute_value=True).then_inc(att_chain, 1)
                dve.wait_ge(att_chain, STEPS * b + 2)
                dve.nop(nofuse=True)
                v.tensor_scalar(osc[:, one], oamax[:, one], 1.0 / 127.0, 1e-8, ALU.mult, ALU.max).then_inc(att_chain, 1)
                dve.wait_ge(att_chain, STEPS * b + 3)
                dve.nop(nofuse=True)
                v.reciprocal(ors[:, one], osc[:, one]).then_inc(att_chain, 1)
                dve.wait_ge(att_chain, STEPS * b + 4)
                dve.nop(nofuse=True)
                v.tensor_scalar(r_b, o_b, ors[:, one], ROUND, ALU.mult, ALU.add).then_inc(att_chain, 1)
                dve.wait_ge(att_chain, STEPS * b + 5)
                dve.nop(nofuse=True)
                v.tensor_scalar(oq_flat[:, bass.ds(b * D, D)], r_b, ROUND, None, ALU.subtract).then_inc(oq_done, 1)

            def attend(b, u, more=2, first=False):
                if more:
                    maximum(b + 1, 1 - u, 1)
                if not first:
                    finish(b - 1, 1 - u)
                if more:
                    maximum(b + 1, 1 - u, 2)
                    maximum(b + 1, 1 - u, 3)
                    split_max(b + 1, 1 - u)
                if more > 1:
                    maximum(b + 2, u, 0)

            for g in range(4):
                maximum(0, 0, g)
            split_max(0, 0)
            maximum(1, 1, 0)
            attend(0, 0, first=True)
            with dve.Fori(0, LAPS) as pair:
                for u in range(2):
                    attend(pair * 2 + (1 + u), 1 - u)
            for b in range(2 * LAPS + 1, TILES):
                attend(b, b % 2, min(2, TILES - 1 - b))
            finish(TILES - 1, 1)

            for b in range(TILES):
                dve.wait_ge(y_psum, b // 2 + 1)
                v.scalar_tensor_tensor(out=xq[:, b], in0=bank[2 + b // 2 % 2][:, D * (b % 2):D * (b % 2) + D], scalar=osc[:, b:b + 1],
                                       in1=wscale[:], op0=ALU.mult, op1=ALU.mult).then_inc(y1_done, 1)
            for b in range(TILES):
                dve.wait_ge(x2_done, b + 1)
                stats(b, bn2_done)
            norm_scalars(bn2_done, 2)

            logit_bank = bank[6][:].rearrange("p (b e) -> p b e", b=TILES)
            dve.wait_ge(logit_psum, 1)
            dve.wait_ge(pool_set, 12)
            link(v.tensor_reduce(lmax[:], logit_bank, AX.X, ALU.max))
            link(v.tensor_tensor(logit, logit_bank, lmax[:].unsqueeze(2).broadcast_to([P, TILES, EXPERTS]), ALU.subtract))
            v.tensor_scalar(logit, logit, LOWEST, None, ALU.max).then_inc(shift_done, 1)
            dve.wait_ge(shift_done, 1)
            link(v.tensor_reduce(gbest[:, :, 0:GROUPS], logit.rearrange("p b (g e) -> p b g e", g=GROUPS), AX.X, ALU.max))
            for b in range(TILES):
                i = v.max(g8[:, b], gbest[:, b, 0:GROUPS])
            link(i)
            link(v.tensor_copy(gtop[:, :, 0:TOPG], g8[:, :, 0:TOPG]))
            for b in range(TILES):
                i = v.match_replace(gout[:, b], gtop[:, b], gbest[:, b], CHOSEN)
            link(i)
            link(v.tensor_scalar(gcap[:], gout[:, :, 0:GROUPS], CHOSEN, LOWEST, ALU.is_lt, ALU.mult))
            link(v.tensor_tensor(cand[:, :, 0:EXPERTS].rearrange("p b (g e) -> p b g e", g=GROUPS), logit.rearrange("p b (g e) -> p b g e", g=GROUPS),
                                 gcap[:].unsqueeze(3).broadcast_to([P, TILES, GROUPS, GSIZE]), ALU.min))
            for b in range(TILES):
                i = v.max(e8[:, b], cand[:, b, 0:EXPERTS])
            link(i)
            link(v.tensor_copy(etop[:, :, 0:TOPK], e8[:, :, 0:TOPK]))
            for b in range(TILES):
                i = v.match_replace(eout[:, b], etop[:, b], cand[:, b], CHOSEN)
            link(i)
            v.tensor_scalar(sel[:], eout[:, :, 0:EXPERTS], CHOSEN, None, ALU.is_equal).then_inc(sel_done, 1)
            dve.wait_ge(pexp_done, TILES)
            link(v.reciprocal(rtotal[:], total[:]))
            link(v.tensor_scalar(rtotal[:], rtotal[:], tg[:, 1:2], None, ALU.mult))
            link(v.tensor_tensor(pexp, pexp, rtotal[:].unsqueeze(2).broadcast_to([P, TILES, EXPERTS]), ALU.mult))
            v.scalar_tensor_tensor(out=rows[:, :, D:ROW], in0=eout[:, :, 0:EXPERTS], scalar=CHOSEN, in1=pexp,
                                   op0=ALU.is_equal, op1=ALU.mult).then_inc(wrow_done, 1)
            dve.wait_ge(selT_psum, 1)
            dve.wait_ge(got_tokv, 16)
            selT = bank[4][0:EXPERTS].bitcast(bf16)
            v.tensor_tensor(key2, selT, tokv[:, 1], ALU.mult).then_inc(key_done, 1)
            v.tensor_tensor(key, selT, tokv[:, 0], ALU.mult).then_inc(key_done, 1)
            dve.wait_ge(key_done, 2)

            def round_(r):
                link(v.max(order[:, 8 * r:8 * r + 8], key))
                if 8 * r + 8 < CAP:
                    link(v.match_replace(key, order[:, 8 * r:8 * r + 8], key, 0.0))

            def shared_hidden(u):
                c, h = u // 2, u % 2
                n = SCH[c][1]
                dve.wait_ge(sgate_done, u + 1)
                v.tensor_tensor(sact[0:n, c * T + 512 * h:c * T + 512 * h + 512], sgate[u % 2][0:n], bank[2 * (u % 2) + 1][0:n], ALU.mult).then_inc(sact_done, 1)

            def add_shared(j):
                dve.wait_ge(sd_psum, j + 1)
                for b in (2 * j, 2 * j + 1):
                    v.scalar_tensor_tensor(out=x[:, b], in0=bank[4 + j % 2][:, D * (b % 2):D * (b % 2) + D], scalar=tg[:, 1:2],
                                           in1=x[:, b], op0=ALU.mult, op1=ALU.add).then_inc(base_done, 1)

            shared_hidden(0)
            shared_hidden(1)
            link(v.tensor_reduce(last[:, 0:1], key2, AX.X, ALU.max))
            link(v.tensor_scalar(last[:, 1:2], last[:, 0:1], -1.0, T + 1.0, ALU.mult, ALU.add))
            link(v.scalar_tensor_tensor(out=last[:, 2:3], in0=last[:, 0:1], scalar=0.0, in1=last[:, 1:2], op0=ALU.is_gt, op1=ALU.mult))
            round_(0)
            dve.wait_ge(pos_psum, 1)
            dve.wait_ge(wrow_done, 1)
            v.scalar_tensor_tensor(out=over, in0=logit_bank, scalar=CAP - 1.0, in1=rows[:, :, D:ROW], op0=ALU.is_ge, op1=ALU.mult).then_inc(over_done, 1)
            for what in (1, "s2", 2, "s3", 3, 4, "s4", 5, "s5", 6, 7, "a0", 8, "a1", 9, "a2", 10, "a3", 11):
                if isinstance(what, int):
                    round_(what)
                elif what[0] == "s":
                    shared_hidden(int(what[1]))
                else:
                    add_shared(int(what[1]))
            v.tensor_copy(order[:, CAP - 1:CAP], last[:, 2:3]).then_inc(order_done, 1)
            dve.wait_ge(slot_psum, 1)
            slots = bank[7][0:CAP, 0:EXPERTS]
            v.tensor_scalar(gidx[:], slots, -1.0, float(T), ALU.mult, ALU.add).then_inc(idx_done, 1)
            dve.wait_ge(idx_done, 1)

            def to_gather(e, i):
                v.tensor_copy(gcol[i][:], gidx[:, bass.ds(e, 1)]).then_inc(gcol_done, 1)

            for e in range(GBUF):
                to_gather(e, e)
            link(v.tensor_scalar(slotv[:, 1], slots, slotc[0:CAP, 0:1], None, ALU.mult))
            link(v.scalar_tensor_tensor(out=empty[:], in0=slotv[:, 1], scalar=0.0, in1=slotc[0:CAP, 2:], op0=ALU.is_equal, op1=ALU.mult))
            link(v.tensor_scalar(slotv[:, 0], slotv[:, 1], -1.0, float(T), ALU.mult, ALU.add))
            link(v.tensor_tensor(sidx[:], slotv[:, 0], empty[:], ALU.add))

            def rows_across(e, u):
                dve.wait_ge(gT_psum, e + 1)
                dve.wait_ge(up_psum, e + 1)
                dve.nop(nofuse=True)
                v.tensor_copy(gxT[u], bank[u][:, 0:KC * CAP].rearrange("p (k t) -> p k t", k=KC)).then_inc(gxT_done, 1)

            def expert(e, lap, r, more, across):
                u = r % 2
                dve.wait_ge(silu_done, e + 1)
                dve.wait_ge(down_psum, e + 1)
                dve.nop(nofuse=True)
                v.tensor_tensor(hid[u], silu[u], bank[2 + u][0:MH, MC * CAP:2 * MC * CAP].rearrange("p (c t) -> p c t", c=MC),
                                ALU.mult).then_inc(hid_done, 1)
                dve.wait_ge(got_rows[r % GBUF], lap * (16 * RING // GBUF) + 16 * (r // GBUF + 1))
                dve.wait_ge(orow_done, e + 1)
                dve.nop(nofuse=True)
                v.tensor_scalar(gw[u][:], gx[r % GBUF][:, bass.ds(e + D, 1)], slotc[0:CAP, 0:1], slotc[0:CAP, 1:2], ALU.mult, ALU.add).then_inc(gw_done, 1)
                dve.wait_ge(acc_in[u], lap * (8 * RING) + FILL[u] + 16 * (r // 2) - 16)
                dve.nop(nofuse=True)
                v.tensor_copy(scol[r % OBUF][:], sidx[:, bass.ds(e, 1)]).then_inc(scol_done, 1)
                if more:
                    to_gather(e + GBUF, r % GBUF)
                if across:
                    rows_across(e + 2, u)

            rows_across(0, 0)
            rows_across(1, 1)
            with dve.Fori(0, EXPERTS // RING - 1) as lap:
                for r in range(RING):
                    expert(lap * RING + r, lap, r, True, True)
            for r in range(RING):
                e = EXPERTS - RING + r
                expert(e, EXPERTS // RING - 1, r, e + GBUF < EXPERTS, e + 2 < EXPERTS)

            dve.wait_ge(got_last, 32)
            v.tensor_tensor(lastrow[:, 2], lastrow[:, 0], lastrow[:, 1], ALU.add).then_inc(last_done, 1)
            for j in range(4):
                dve.wait_ge(got_acc[j], 32)
                two = xn[:, 2 * j:2 * j + 2]
                v.tensor_tensor(two, two, xq[:, 2 * j:2 * j + 2], ALU.add).then_inc(sum_done, 1)
                dve.wait_ge(sum_done, j + 1)
                dve.wait_ge(corr_psum, j + 1)
                v.tensor_tensor(two, two, bank[j][:].rearrange("p (b h) -> p b h", b=2), ALU.add).then_inc(y_done, 1)

        @block.tensor
        def _(pe):
            t = nc.tensor
            pe.sem_inc(pv_psum, 2)
            pe.sem_inc(heads_psum, 2)
            pe.sem_inc(up_psum, 2)
            pe.sem_inc(down_psum, 2)

            def unit(u):
                what, c, h = units[u]
                if u >= 2:
                    pe.wait_ge(unit_act, 2 * (u - 1))
                for k in range(KC):
                    w = wkv[:, k, P * c:P * c + P] if what == "k" else wqT[:, k, P * c:P * c + P]
                    src = ctxT if what == "k" else xqT
                    last = t.matmul(bank[u % 2][:], w, src[:, k, 512 * h:512 * h + 512], start=(k == 0), stop=(k == KC - 1))
                last.then_inc(unit_psum, 1)

            pe.wait_ge(got_ctx, 16)
            pe.wait_ge(got_kv, 16)
            for u in range(4):
                unit(u)
                for b in (2 * u, 2 * u + 1):
                    for k in range(KC):
                        last = t.matmul(bank[(2, 3, 6, 7)[u]][:, D * (b % 2):D * (b % 2) + D], ctxT[:, k, P * b:P * b + P], wkv[:, k, D:2 * D],
                                        start=(k == 0), stop=(k == KC - 1))
                last.then_inc(v_psum, 1)
            pe.wait_ge(w_done, 6)
            pe.wait_ge(got_const, 48)
            for c in range(2):
                for k in range(KC):
                    last = t.transpose(bank[4][:, 256 * c + P * k:256 * c + P * k + P], w_rows[:, c, P * k:P * k + P], ident[:])
            last.then_inc(w_psum, 1)
            pe.wait_ge(consts_b, 3)
            wp_bank = bank[5][:, 0:256].bitcast(bf16)
            for c in range(2):
                for k in range(KC):
                    last = t.transpose(wp_bank[:, 256 * c + P * k:256 * c + P * k + P], wp_int[:, c, P * k:P * k + P], identb[:])
            last.then_inc(w_psum, 1)
            pe.wait_ge(wT_done, 2)
            pe.wait_ge(pool_set, 4)
            t.matmul(bank[5][:, 256:512], onesf[:], wdiag[:].rearrange("p c o -> p (c o)"), start=True, stop=True).then_inc(w_psum, 1)
            pe.wait_ge(v_done, 4)
            for j in range(4):
                pe.wait_ge(xq_done, 2 * j + 2)
                if j >= 2:
                    pe.wait_ge(xqT_done, j - 1)
                for k in range(KC):
                    for b in (2 * j, 2 * j + 1):
                        last = t.transpose(bank[2 + j % 2][:, 256 * k + P * (b % 2):256 * k + P * (b % 2) + P], xq[:, b, P * k:P * k + P], ident[:])
                last.then_inc(xqT_psum, 1)
            pe.wait_ge(xqT_done, 4)
            for u in range(4, 8):
                unit(u)

            def scores(b, g):
                for h in range(4 * g, 4 * g + 4):
                    last = t.matmul(bank[g % 2][:, P * (h % 4):P * (h % 4) + P], qs[:, bass.ds(b * TOK + h * T, TOK)], ks[:, bass.ds(b * TOK + h * T, TOK)],
                                    start=True, stop=True)
                last.then_inc(s_psum, 1)

            def scores_t(b, g, u):
                pe.wait_ge(exp_done, 4 * b + g + 1)
                pe.nop(nofuse=True)
                for h in range(4 * g, 4 * g + 4):
                    dst = bank[2 + g % 2][:, P * (h % 4):P * (h % 4) + P]
                    t.matmul(dst, ks[:, bass.ds(b * TOK + h * T, TOK)], qs[:, bass.ds(b * TOK + h * T, TOK)], start=True, stop=False)
                    last = t.matmul(dst, pick[:, h], negmaxT[u][:], start=False, stop=True)
                last.then_inc(st_psum, 1)

            def heads_times_values(b, g, u):
                pe.wait_ge(exp_done, 4 * b + g + 3)
                if g == 0:
                    pe.wait_ge(headsT_done, b + 1)
                    pe.wait_ge(vpad_done, b + 1)
                pe.nop(nofuse=True)
                for i in range(4):
                    h = 4 * g + i
                    last = t.matmul(bank[4 + u][VW * i:VW * i + VW, TOK * g:TOK * g + TOK], vpad[u][:, VW * h:VW * h + VW], probs[u][:, TOK * h:TOK * h + TOK],
                                    start=True, stop=True)
                if g == 3:
                    last.then_inc(pv_psum, 1)

            def heads_across(b, u):
                pe.wait_ge(headsT_done, b + 3)
                pe.wait_ge(norm_done, b + 1)
                pe.nop(nofuse=True)
                for g in range(4):
                    last = t.transpose(bank[6][:, TOK * g:TOK * g + TOK], headsT[u][:, TOK * g:TOK * g + TOK], ident[:])
                last.then_inc(heads_psum, 1)

            def negmax_across(b, u):
                pe.wait_ge(split_done, 2 * b + 2)
                pe.nop(nofuse=True)
                t.transpose(bank[7][0:2 * HEADS, 0:TOK // 2].bitcast(bf16), negmax[:, u], identb[:]).then_inc(nm_psum, 1)

            def next_scores(b, g):
                pe.wait_ge(max_done, 4 * b + g - 1)
                pe.nop(nofuse=True)
                scores(b, g)

            def attend(b, u, more=2, first=False):
                for g in range(4):
                    if g == 0:
                        pe.wait_ge(nm_done, b + 1)
                    elif more:
                        next_scores(b + 1, g)
                    if g == 1 and not first:
                        heads_across(b - 1, 1 - u)
                    scores_t(b, g, u)
                    if g:
                        heads_times_values(b, g - 1, u)
                if more > 1:
                    next_scores(b + 2, 0)
                if more:
                    negmax_across(b + 1, 1 - u)
                heads_times_values(b, 3, u)

            pe.wait_ge(got_k, 128)
            pe.wait_ge(got_q, 128)
            pe.wait_ge(unit_act, 16)
            pe.wait_ge(v_done, 8)
            pe.wait_ge(wT_done, 3)
            pe.wait_ge(pool_set, 14)
            scores(0, 0)
            scores(0, 1)
            for b, g in ((0, 2), (0, 3), (1, 0)):
                pe.wait_ge(max_done, 4 * b + g - 1)
                scores(b, g)
            negmax_across(0, 0)
            attend(0, 0, first=True)
            with pe.Fori(0, LAPS) as pair:
                for u in range(2):
                    attend(pair * 2 + (1 + u), 1 - u)
            for b in range(2 * LAPS + 1, TILES):
                attend(b, b % 2, min(2, TILES - 1 - b))
            heads_across(TILES - 1, 1)

            pe.wait_ge(max_done, 4 * TILES)
            pe.wait_ge(exp_done, 4 * TILES + 2)
            for j in range(4):
                pe.wait_ge(oq_done, 2 * j + 2)
                if j >= 2:
                    pe.wait_ge(oT_done, j - 1)
                o_bank = bank[j % 2][:, 0:256].bitcast(bf16)
                for k in range(KC):
                    for b in (2 * j, 2 * j + 1):
                        last = t.transpose(o_bank[:, 256 * k + P * (b % 2):256 * k + P * (b % 2) + P], oq[:, b, P * k:P * k + P], identb[:])
                last.then_inc(oT_psum, 1)
                if j >= 2:
                    pe.wait_ge(y1_done, 2 * (j - 1))
                pe.wait_ge(oT_done, j + 1)
                for b in (2 * j, 2 * j + 1):
                    for k in range(KC):
                        last = t.matmul(bank[2 + j % 2][:, D * (b % 2):D * (b % 2) + D], oT[j % 2][:, k, P * (b % 2):P * (b % 2) + P], wpT[:, k], start=(k == 0), stop=(k == KC - 1))
                last.then_inc(y_psum, 1)
            pe.wait_ge(norm_done, TILES + 1)
            for j in range(4):
                pe.wait_ge(h_done, 2 * j + 2)
                if j >= 2:
                    pe.wait_ge(hT_done, j - 1)
                for k in range(KC):
                    for b in (2 * j, 2 * j + 1):
                        last = t.transpose(bank[4 + j % 2][:, 256 * k + P * (b % 2):256 * k + P * (b % 2) + P], rows[:, b, P * k:P * k + P], ident[:])
                last.then_inc(hT_psum, 1)
            pe.wait_ge(hT_done, 4)
            pe.wait_ge(got_gate, 16)
            for b in range(TILES):
                for k in range(KC):
                    last = t.matmul(bank[6][:, EXPERTS * b:EXPERTS * b + EXPERTS], hT[:, k, P * b:P * b + P], gateT[:, k], start=(k == 0), stop=(k == KC - 1))
            last.then_inc(logit_psum, 1)

            def shared_up(u):
                c, h = u // 2, u % 2
                m0, n = SCH[c]
                if u >= 2:
                    pe.wait_ge(sact_done, u - 1)
                for i in range(2):
                    for k in range(KC):
                        last = t.matmul(bank[2 * (u % 2) + i][0:n], sgu[:, k, i, m0:m0 + n], hT[:, k, 512 * h:512 * h + 512], start=(k == 0), stop=(k == KC - 1))
                last.then_inc(sg_psum, 1)

            pe.wait_ge(got_shared, 48)
            pe.wait_ge(y1_done, TILES)
            shared_up(0)
            shared_up(1)
            pe.wait_ge(sel_done, 1)
            selT = bank[4][0:EXPERTS].bitcast(bf16)
            for b in range(TILES):
                last = t.transpose(selT[:, P * b:P * b + P], sel[:, b], identb[:])
            last.then_inc(selT_psum, 1)
            for b in range(TILES):
                dst = bank[6][:, EXPERTS * b:EXPERTS * b + EXPERTS]
                for c in range(b):
                    t.matmul(dst, onesb[:], sel[:, c], start=(c == 0), stop=False)
                last = t.matmul(dst, beforeb[:], sel[:, b], start=(b == 0), stop=True)
            last.then_inc(pos_psum, 1)
            for u in range(2, 6):
                shared_up(u)
            pe.wait_ge(over_done, 1)
            for j in range(2):
                if j:
                    pe.wait_ge(overT_done, j)
                for b in range(4):
                    last = t.transpose(bank[7][0:EXPERTS, P * b:P * b + P], over[:, 4 * j + b], ident[:])
                last.then_inc(overT_psum, 1)
            pe.wait_ge(sact_done, 6)
            pe.wait_ge(key_done, 2)
            for j in range(4):
                if j >= 2:
                    pe.wait_ge(base_done, 2 * (j - 1))
                for b in (2 * j, 2 * j + 1):
                    for c, (m0, n) in enumerate(SCH):
                        last = t.matmul(bank[4 + j % 2][:, D * (b % 2):D * (b % 2) + D], sact[0:n, c * T + P * b:c * T + P * b + P], sdn[0:n, c], start=(c == 0), stop=(c == 2))
                last.then_inc(sd_psum, 1)
            pe.wait_ge(order_done, 1)
            pe.wait_ge(overT_done, 2)
            t.transpose(bank[7][0:CAP, 0:EXPERTS], order[:], ident[0:EXPERTS, 0:EXPERTS]).then_inc(slot_psum, 1)
            pe.wait_ge(base_done, TILES)

            def rows_across(e, lap, r):
                pe.wait_ge(got_rows[r % GBUF], lap * (16 * RING // GBUF) + 16 * (r // GBUF + 1))
                pe.wait_ge(gxT_done, e + 1)
                pe.nop(nofuse=True)
                for k in range(KC):
                    last = t.transpose(bank[r % 2][:, CAP * k:CAP * k + CAP], gx[r % GBUF][:, P * k:P * k + P], ident[0:CAP, 0:CAP])
                last.then_inc(gT_psum, 1)

            def up(e, lap, r):
                s, lap = r % RING, lap + r // RING
                pe.wait_ge(got_expert[s], lap * 32 + 32)
                pe.wait_ge(gxT_done, e + 3)
                pe.wait_ge(hid_done, e + 1)
                pe.nop(nofuse=True)
                for i in range(2):
                    for c in range(MC):
                        for k in range(KC):
                            last = t.matmul(bank[2 + r % 2][0:MH, CAP * (MC * i + c):CAP * (MC * i + c + 1)], wgu[s][:, k, i, MH * c:MH * c + MH], gxT[r % 2][:, k],
                                            start=(k == 0), stop=(k == KC - 1))
                last.then_inc(up_psum, 1)

            def down(e, r):
                pe.wait_ge(hid_done, e + 3)
                pe.wait_ge(orow_done, e + 1)
                pe.nop(nofuse=True)
                for c in range(MC):
                    last = t.matmul(bank[4 + r % 2][0:CAP, 0:D], hid[r % 2][:, c], wdn[r][:, c], start=(c == 0), stop=(c == MC - 1))
                last.then_inc(down_psum, 1)

            rows_across(0, 0, 0)
            up(0, 0, 0)
            rows_across(1, 0, 1)
            with pe.Fori(0, EXPERTS // RING - 1) as lap:
                for r in range(RING):
                    up(lap * RING + (r + 1), lap, r + 1)
                    rows_across(lap * RING + (r + 2), lap, r + 2)
                    down(lap * RING + r, r)
            lap = EXPERTS // RING - 1
            for r in range(RING):
                e = lap * RING + r
                if e + 1 < EXPERTS:
                    up(e + 1, lap, r + 1)
                if e + 2 < EXPERTS:
                    rows_across(e + 2, lap, r + 2)
                down(e, r)
            pe.wait_ge(last_done, 1)
            pe.wait_ge(hid_done, EXPERTS + 2)
            for j in range(4):
                for b in (2 * j, 2 * j + 1):
                    last = t.matmul(bank[j][:, D * (b % 2):D * (b % 2) + D], overT[:, P * b:P * b + P], lastrow[:, 2], start=True, stop=True)
                last.then_inc(corr_psum, 1)


def constants():
    slot = np.arange(P)
    notlast = np.where(slot == CAP - 1, 0.0, 1.0)
    spare = np.repeat(slot[:, None].astype(np.float64), EXPERTS, 1)
    spare[CAP - 1] = CAP + np.arange(EXPERTS)
    c = np.concatenate([np.eye(P), np.triu(np.ones((P, P)), 1), notlast[:, None], 1 - notlast[:, None], spare], 1)
    tok = np.arange(T)
    tokv = np.repeat(np.stack([T - tok, tok + 1])[None], EXPERTS, 0)
    return c.astype(np.float32), tokv.astype(np.float32)


def kernel(**inputs):
    import concourse.bacc as _bacc
    from concourse.bass_utils import run_bass_kernel_spmd as _run

    g = {k: np.asarray(v) for k, v in inputs.items()}
    n = lambda k: g["L0_" + k]
    lay = np.ascontiguousarray
    consts, tokv = constants()
    chunks = lambda t: lay(t.reshape(KC, P, -1).transpose(1, 0, 2))
    wgu = np.stack([n("ffn_Wg"), n("ffn_Wu")], 1)
    arrays = {
        "x": lay(g["x"].transpose(1, 0, 2)),
        "ctxT": chunks(g["ctx_2048"].reshape(T, D).T),
        "wkv": chunks(n("xattn_wkv").T),
        "w_rows": lay(np.concatenate([n("xattn_wq").reshape(2, P, D), n("xattn_wp").reshape(2, P, D)]).transpose(1, 0, 2)),
        "bqk": lay(np.concatenate([n("xattn_bq").reshape(2, P), n("xattn_bkv")[:D].reshape(2, P)]).T),
        "bvp": np.stack([n("xattn_bkv")[D:], n("xattn_bp")]),
        "gates": np.concatenate([g["g_xattn"], g["g_ffn"]])[None],
        "consts": consts,
        "tokv": tokv,
        "gateT": chunks(n("ffn_gate_weight").T),
        "wgu": lay(wgu.reshape(EXPERTS, 2, M, KC, P).transpose(0, 4, 3, 1, 2)),
        "wdn": lay(n("ffn_Wd").reshape(EXPERTS, D, MC, MH).transpose(0, 3, 2, 1)),
        "sgu": lay(np.stack([n("ffn_Sg"), n("ffn_Su")]).reshape(2, MS, KC, P).transpose(3, 2, 0, 1)),
        "sdn": lay(n("ffn_Sd").T),
    }
    nc = _bacc.Bacc("TRN2", target_bir_lowering=False, num_devices=1)
    a = {k: nc.dram_tensor(k + "_in", t.shape, mybir.dt.from_np(t.dtype), kind="ExternalInput").ap() for k, t in arrays.items()}
    out = nc.dram_tensor("out", (TILES, TOK, D), mybir.dt.float32, kind="ExternalOutput").ap()
    gated_block(nc, a, out)
    r = _run(nc, [{k + "_in": t for k, t in arrays.items()}], core_ids=[0])
    return r.results[0]["out"]
```

```python
import concourse.bass as bass
from concourse import mybir
from contextlib import ExitStack
import numpy as np

P = 128
TILES, TOK, D = 8, 128, 256
T = TILES * TOK
KC = D // P
HEADS, DH = 16, 16
VW = 32
PARTS = 3
Q_PART = [0, 0, 1, 0, 2, 1, 1, 2]
K_PART = [0, 1, 0, 2, 0, 1, 2, 1]
EXPERTS, GROUPS, TOPG, TOPK = 64, 8, 3, 6
GSIZE = EXPERTS // GROUPS
CAP = 96
M = 176
MR = M - P
GATE_AT = 64
UP_COLS = [(0, P), (P, P), (2 * P, GATE_AT + MR)]
WG = UP_COLS[2][0] + UP_COLS[2][1]
MS = 352
SCH = [(0, 128), (128, 128), (256, 96)]
ROW = D + EXPERTS
SPARE = T
LASTROW = T + CAP
ROWS = T + 2 * P
SD_BANK = (4, 5, 6, 3)
H_BANK = (0, 1, 4, 5)
V_BANK = (4, 6, 7, 5)
UNIT_BUF = 4
RING = 16
GBUF = 8
OBUF = 4
EPS = 1e-5
ROUND = 12582912.0
LOWEST = -87.33
MARK, CHOSEN = 1.0, 2.0
SCALE = 1.0 / float(np.sqrt(DH))


def gated_block(nc, a, out):
    f32, bf16, u32 = mybir.dt.float32, mybir.dt.bfloat16, mybir.dt.uint32
    ALU, ACT, AX = mybir.AluOpType, mybir.ActivationFunctionType, mybir.AxisListType
    ctx = ExitStack()
    with ctx:
        def sb(name, shape, dt=f32):
            return ctx.enter_context(nc.sbuf_tensor(name, shape, dt))

        def sem(name):
            return ctx.enter_context(nc.semaphore(name))

        def dram(name, shape, dt=f32):
            return nc.dram_tensor(name, shape, dt, kind="Internal").ap()

        q_parts = dram("q_parts", (PARTS, D, T), bf16)
        k_parts = dram("k_parts", (PARTS, D, T), bf16)
        table = dram("table", (ROWS, ROW))
        acc = [dram(f"acc{i}", (ROWS, D)) for i in range(2)]

        def carver(arena):
            at = [0]

            def cut(n, parts=P):
                at[0] += n
                return arena[0:parts, at[0] - n:at[0]]
            return cut

        stream = sb("stream", [P, 20 * T])
        cut = carver(stream)
        qs, ks = [cut(HEADS * T // 2).bitcast(bf16) for _ in range(2)]
        probs = [cut(HEADS * TOK) for _ in range(2)]
        cut = carver(stream)
        wgu, wdn = [], []
        for _ in range(RING):
            wgu.append(cut(KC * WG).rearrange("p (k m) -> p k m", k=KC))
            wdn.append(cut(2 * D).rearrange("p (c h) -> p c h", c=2))
        scratch = sb("scratch", [P, 10880])
        cut = carver(scratch)
        xqT = cut(KC * T).rearrange("p (k t) -> p k t", k=KC)
        w_rows, w_fix = [cut(4 * D).rearrange("p (c h) -> p c h", c=4) for _ in range(2)]
        wkv = cut(KC * 2 * D).rearrange("p (k h) -> p k h", k=KC)
        part = [cut(PARTS * 256).bitcast(bf16).rearrange("p (r t) -> p r t", r=PARTS) for _ in range(UNIT_BUF)]
        rest = [probs[1][:, 512 * i:512 * i + 512] for i in range(2)]
        values = cut(TILES * D)
        cut = carver(scratch)
        vpad = [cut(HEADS * VW) for _ in range(2)]
        headsT = [cut(4 * TOK) for _ in range(2)]
        cut = carver(scratch)
        sact = cut(3 * T)
        sgate = [cut(512) for _ in range(2)]
        key, key2, overT = [cut(T, EXPERTS) for _ in range(3)]
        logit, pexp, over = [cut(TILES * EXPERTS).rearrange("p (b e) -> p b e", b=TILES) for _ in range(3)]
        eout = cut(TILES * (EXPERTS + 8 - TOPK)).rearrange("p (b e) -> p b e", b=TILES)
        cut = carver(scratch)
        orow = [cut(D, CAP) for _ in range(OBUF)]
        gxT = [cut(KC * CAP).rearrange("p (k t) -> p k t", k=KC) for _ in range(2)]
        silu, hid = [[cut(2 * CAP).rearrange("p (c t) -> p c t", c=2) for _ in range(2)] for _ in range(2)]
        lastrow = cut(3 * D, EXPERTS).rearrange("p (i h) -> p i h", i=3)
        cut = carver(scratch[:, 7 * T:])
        gx = [cut(ROW, CAP) for _ in range(GBUF)]
        x = sb("x", [P, TILES, D])
        xn = sb("xn", [P, TILES, D])
        xq = sb("xq", [P, TILES, D])
        ctxT = sb("ctxT", [P, KC, T])
        hT = ctxT
        wp_int = sb("wp_int", [P, 2, D], bf16)
        wqT = sb("wqT", [P, KC, D])
        wpT = sb("wpT", [P, KC, D], bf16)
        bqk = sb("bqk", [P, 4])
        bvp = sb("bvp", [P, 2, D])
        gates = sb("gates", [P, 2])
        tg = sb("tg", [P, 2])
        rowmax = sb("rowmax", [P, 2, HEADS])
        negmax = sb("negmax", [P, 2, 2 * HEADS], bf16)
        negmaxT = [sb(f"negmaxT{i}", [P, TOK], bf16) for i in range(2)]
        pick = sb("pick", [P, HEADS, P], bf16)
        rden = sb("rden", [P, 2, HEADS])
        ident = sb("ident", [P, P])
        identb = sb("identb", [P, P], bf16)
        before = sb("before", [P, P])
        beforeb = sb("beforeb", [P, P], bf16)
        onesb = sb("onesb", [P, P], bf16)
        onesf = sb("onesf", [P, P])
        slotc = sb("slotc", [P, 2 + EXPERTS])
        tokv = xn[0:EXPERTS].rearrange("p b h -> p (b h)").rearrange("p (i t) -> p i t", i=2)
        zeros = sb("zeros", [P, 2 * ROW])
        stat = sb("stat", [P, TILES, 6])
        mv = sb("mv", [P, TILES, 2])
        veps = sb("veps", [P, TILES])
        neghalf = sb("neghalf", [P, TILES])
        rstd = sb("rstd", [P, TILES])
        nmr = sb("nmr", [P, TILES])
        amax = sb("amax", [P, TILES])
        qsc = sb("qsc", [P, TILES])
        qrs = sb("qrs", [P, TILES])
        oamax = sb("oamax", [P, TILES])
        osc = sb("osc", [P, TILES])
        ors = sb("ors", [P, TILES])
        wamax = sb("wamax", [P, 4])
        wsc = sb("wsc", [P, 4])
        wrs = sb("wrs", [P, 4])
        wdiag = sb("wdiag", [P, 2, P])
        wscale = sb("wscale", [P, D])
        oq = sb("oq", [P, TILES, D], bf16)
        oT = [sb(f"oT{i}", [P, KC, P], bf16) for i in range(2)]
        rows = sb("rows", [P, TILES, ROW])
        gateT = sb("gateT", [P, KC, EXPERTS])
        lmax = sb("lmax", [P, TILES])
        total = sb("total", [P, TILES])
        rtotal = sb("rtotal", [P, TILES])
        gbest = sb("gbest", [P, TILES, GROUPS + 8 - TOPG])
        gtop = sb("gtop", [P, TILES, 8])
        g8 = sb("g8", [P, TILES, 8])
        e8 = sb("e8", [P, TILES, 8])
        gout = sb("gout", [P, TILES, GROUPS + 8 - TOPG])
        gcap = sb("gcap", [P, TILES, GROUPS])
        cand = sb("cand", [P, TILES, EXPERTS + 8 - TOPK])
        etop = sb("etop", [P, TILES, 8])
        sel = sb("sel", [P, TILES, EXPERTS], bf16)
        last = sb("last", [EXPERTS, 4])
        order = sb("order", [EXPERTS, CAP])
        slotv = sb("slotv", [CAP, 2, EXPERTS])
        empty = sb("empty", [CAP, EXPERTS])
        gidx = sb("gidx", [CAP, EXPERTS], u32)
        sidx = sb("sidx", [CAP, EXPERTS], u32)
        sgu = sb("sgu", [P, KC, 2, MS])
        sdn = sb("sdn", [P, 3, D])
        gcol = [sb(f"gcol{i}", [CAP, 1], u32) for i in range(GBUF)]
        scol = [sb(f"scol{i}", [CAP, 1], u32) for i in range(OBUF)]
        gw = [sb(f"gw{i}", [CAP, 1]) for i in range(2)]
        bank = [ctx.enter_context(nc.psum_tensor(f"bank{i}", [P, 512], f32)) for i in range(8)]

        got_x, got_x2, got_w, got_w2, got_ctx, got_ctx2, got_kv, got_small, got_const, got_gate, got_tokv, got_shared = [
            sem(n) for n in ("got_x", "got_x2", "got_w", "got_w2", "got_ctx", "got_ctx2", "got_kv", "got_small", "got_const", "got_gate",
                             "got_tokv", "got_shared")]
        got_expert = [sem(f"got_expert{r}") for r in range(RING)]
        got_rows = [sem(f"got_rows{i}") for i in range(GBUF)]
        parts_out = [sem(f"parts_out{i}") for i in range(UNIT_BUF)]
        got_stack = [sem(f"got_stack{j}") for j in range(TILES // 2)]
        stack_ready = sem("stack_ready")
        table_out = sem("table_out")
        acc_in = [sem(f"acc_in{i}") for i in range(2)]
        got_last = sem("got_last")
        got_acc = [sem(f"got_acc{i}") for i in range(4)]
        stored = sem("stored")
        pool_set, dve_chain, act_chain, pool_chain = sem("pool_set"), sem("dve_chain"), sem("act_chain"), sem("pool_chain")
        tanh_done, tbp_done, xp_done = sem("tanh_done"), sem("tbp_done"), sem("xp_done")
        consts_b = sem("consts_b")
        mv_done, bn_done, bn2_done, veps_done, rstd_done, nmr_done, xn_done = [
            sem(n) for n in ("mv_done", "bn_done", "bn2_done", "veps_done", "rstd_done", "nmr_done", "xn_done")]
        xq_done, xqT_psum, xqT_done = sem("xq_done"), sem("xqT_psum"), sem("xqT_done")
        w_done, w_psum, wT_done = sem("w_done"), sem("w_psum"), sem("wT_done")
        unit_psum, unit_high, unit_rest, unit_mid, unit_lo = [
            sem(n) for n in ("unit_psum", "unit_high", "unit_rest", "unit_mid", "unit_lo")]
        v_psum, v_done = sem("v_psum"), sem("v_done")
        vpad_zero, vpad_done, headsT_done, heads_psum = sem("vpad_zero"), sem("vpad_done"), sem("headsT_done"), sem("heads_psum")
        s_psum, max_done, split_done, nm_psum, nm_done, st_psum, exp_done, pv_psum, norm_done, oq_done, att_chain, ors_done, round_done = [
            sem(n) for n in ("s_psum", "max_done", "split_done", "nm_psum", "nm_done", "st_psum", "exp_done",
                             "pv_psum", "norm_done", "oq_done", "att_chain", "ors_done", "round_done")]
        oT_psum, oT_done, y_psum, y1_done, x2_done = [
            sem(n) for n in ("oT_psum", "oT_done", "y_psum", "y1_done", "x2_done")]
        h_done, hT_psum, hT_done, logit_psum, shift_done, pexp_done = [
            sem(n) for n in ("h_done", "hT_psum", "hT_done", "logit_psum", "shift_done", "pexp_done")]
        wrow_done, sel_done, selT_psum, key_done, pos_psum, over_done, overT_psum, overT_done = [
            sem(n) for n in ("wrow_done", "sel_done", "selT_psum", "key_done", "pos_psum", "over_done",
                             "overT_psum", "overT_done")]
        order_done, slot_psum, idx_done = sem("order_done"), sem("slot_psum"), sem("idx_done")
        sg_psum, sgate_done, sact_done, sd_psum, base_done = [
            sem(n) for n in ("sg_psum", "sgate_done", "sact_done", "sd_psum", "base_done")]
        gT_psum, gxT_done, up_psum, silu_done, hid_done, down_psum, gw_done, orow_done, gcol_done, scol_done = [
            sem(n) for n in ("gT_psum", "gxT_done", "up_psum", "silu_done", "hid_done", "down_psum", "gw_done",
                             "orow_done", "gcol_done", "scol_done")]
        last_done, corr_psum, sum_done, y_done = [sem(n) for n in ("last_done", "corr_psum", "sum_done", "y_done")]

        FILL = [2 * 16, 2 * 16]
        units = [(what, c, s) for what in "kq" for s in range(2) for c in range(KC)]
        token_rows = lambda t, n: t.rearrange("(a p) h -> p a h", p=P)[:, n]
        block = ctx.enter_context(nc.Block())

        @block.sync
        def _(sp):
            sp.dma_start(x[:, 0:4], a["x"][:, 0:4]).then_inc(got_x, 16)
            sp.dma_start(x[:, 4:8], a["x"][:, 4:8]).then_inc(got_x2, 16)
            sp.dma_start(w_rows[:, 0:2], a["w_rows"][:, 0:2]).then_inc(got_w, 16)
            sp.dma_start(wkv[:, :, 0:D], a["wkv"][:, :, 0:D]).then_inc(got_kv, 16)
            sp.dma_start(ctxT[:, :, 0:512], a["ctxT"][:, :, 0:512]).then_inc(got_ctx, 16)
            sp.dma_start(ctxT[:, :, 512:T], a["ctxT"][:, :, 512:T]).then_inc(got_ctx2, 16)
            sp.dma_start(w_rows[:, 2:4], a["w_rows"][:, 2:4]).then_inc(got_w2, 16)
            sp.dma_start(wkv[:, :, D:2 * D], a["wkv"][:, :, D:2 * D]).then_inc(got_w2, 16)
            sp.dma_start(gateT[:], a["gateT"]).then_inc(got_gate, 16)
            sp.wait_ge(pool_set, 1)
            sp.dma_start(table[T:ROWS].rearrange("(p a) h -> p (a h)", p=P), zeros[:]).then_inc(table_out, 16)
            def parts_to_dram(u):
                what, c, s = units[u]
                dst = k_parts if what == "k" else q_parts
                sp.wait_ge(unit_lo, u + 1)
                sp.dma_start(dst[:, P * c:P * c + P, 512 * s:512 * s + 512].rearrange("r p t -> p r t"),
                             part[u % UNIT_BUF]).then_inc(parts_out[u % UNIT_BUF], 16)

            def stack(what, half):
                base = 0 if what == "k" else 4
                for u in (base + 2 * half, base + 2 * half + 1):
                    sp.wait_ge(parts_out[u % UNIT_BUF], 16 * (u // UNIT_BUF + 1))
                dst, src, order_of = (ks, k_parts, K_PART) if what == "k" else (qs, q_parts, Q_PART)
                for j in (2 * half, 2 * half + 1):
                    for r, p in enumerate(order_of):
                        sp.dma_start(dst[DH * r:DH * r + DH].rearrange("d (h t) -> d h t", h=HEADS)[:, :, 256 * j:256 * j + 256],
                                     src[p].rearrange("(h d) t -> d h t", d=DH)[:, :, 256 * j:256 * j + 256]).then_inc(got_stack[j], 16)

            parts_to_dram(0)
            parts_to_dram(1)
            stack("k", 0)
            for u in (2, 3, 4, 5):
                parts_to_dram(u)
            stack("q", 0)
            parts_to_dram(6)
            parts_to_dram(7)
            stack("k", 1)
            stack("q", 1)
            sp.dma_start(sgu[:], a["sgu"]).then_inc(got_shared, 16)
            sp.dma_start(sdn[:, 0:2], a["sdn"][0:2 * P].rearrange("(c p) h -> p c h", p=P)).then_inc(got_shared, 16)
            sp.dma_start(sdn[0:SCH[2][1], 2], a["sdn"][2 * P:MS]).then_inc(got_shared, 16)
            sp.wait_ge(oq_done, TILES)
            sp.dma_start(tokv, a["tokv"]).then_inc(got_tokv, 16)
            sp.wait_ge(pv_psum, TILES + 2)
            for r in range(RING):
                sp.dma_start(wgu[r], a["wgu"][r]).then_inc(got_expert[r], 16)
                sp.dma_start(wdn[r][:, 0], a["wdn"][r, 0:P]).then_inc(got_expert[r], 16)
                sp.dma_start(wdn[r][0:MR, 1], a["wdn"][r, P:M]).then_inc(got_expert[r], 16)
            for b in range(0, TILES, 2):
                sp.wait_ge(wrow_done, 1)
                for n in (b, b + 1):
                    sp.dma_start(table[P * n:P * n + P], rows[:, n]).then_inc(table_out, 16)
            with sp.Fori(0, EXPERTS // RING - 1) as lap:
                for r in range(RING):
                    sp.wait_ge(down_psum, lap * RING + r + 3)
                    sp.nop(nofuse=True)
                    e = bass.ds(lap * RING + RING + r, 1)
                    sp.dma_start(wgu[r], a["wgu"][e].squeeze(0)).then_inc(got_expert[r], 16)
                    sp.dma_start(wdn[r][:, 0], a["wdn"][e, 0:P].squeeze(0)).then_inc(got_expert[r], 16)
                    sp.dma_start(wdn[r][0:MR, 1], a["wdn"][e, P:M].squeeze(0)).then_inc(got_expert[r], 16)
            for i in range(2):
                sp.wait_ge(acc_in[i], FILL[i] + 16 * EXPERTS // 2)
            for i in range(2):
                sp.dma_start(lastrow[:, i], acc[i][LASTROW:LASTROW + EXPERTS]).then_inc(got_last, 16)
            for j in range(4):
                for i, t in enumerate((xn, xq)):
                    sp.dma_start(t[:, 2 * j:2 * j + 2], token_rows(acc[i][0:T], slice(2 * j, 2 * j + 2))).then_inc(got_acc[j], 16)
            for j in range(4):
                sp.wait_ge(y_done, j + 1)
                sp.dma_start(out[2 * j:2 * j + 2].rearrange("b p h -> p b h"), xn[:, 2 * j:2 * j + 2]).then_inc(stored, 16)
            sp.wait_ge(stored, 64)

        @block.gpsimd
        def _(pool):
            g = nc.gpsimd
            g.memset(zeros[:], 0.0).then_inc(pool_set, 1)
            g.memset(neghalf[:], -0.5).then_inc(pool_set, 1)
            g.memset(onesb[:], 1.0).then_inc(pool_set, 1)
            g.memset(onesf[:], 1.0).then_inc(pool_set, 1)
            for i in range(2):
                g.memset(negmaxT[i][:], 0.0).then_inc(pool_set, 1)
            g.memset(gbest[:], MARK).then_inc(pool_set, 1)
            g.memset(gtop[:], MARK).then_inc(pool_set, 1)
            g.memset(cand[:], MARK).then_inc(pool_set, 1)
            g.memset(etop[:], MARK).then_inc(pool_set, 1)
            pool.wait_ge(veps_done, 1)
            pool.wait_ge(pool_set, 2)
            g.tensor_tensor(rstd[:], veps[:], neghalf[:], ALU.pow).then_inc(rstd_done, 1)
            pool.wait_ge(got_const, 48)
            g.tensor_copy(identb[:], ident[:]).then_inc(consts_b, 1)
            g.tensor_copy(beforeb[:], before[:]).then_inc(consts_b, 1)
            g.tensor_tensor(pick[:], ident[:, 0:HEADS].unsqueeze(2).broadcast_to([P, HEADS, P]),
                            ident[:, HEADS:2 * HEADS].unsqueeze(2).broadcast_to([P, HEADS, P]), ALU.add).then_inc(consts_b, 1)
            pool.wait_ge(pool_set, 1)
            g.dma_start(acc[0][0:T].rearrange("(p a) h -> p a h", p=P),
                        zeros[:, 0:D].unsqueeze(1).broadcast_to([P, TILES, D])).then_inc(acc_in[0], 16)
            for i in range(2):
                g.dma_start(acc[i][T:ROWS].rearrange("(p a) h -> p (a h)", p=P), zeros[:, 0:2 * D]).then_inc(acc_in[i], 16)
            pool.wait_ge(tbp_done, 1)
            for b in range(TILES):
                pool.wait_ge(xn_done, b + 1)
                g.tensor_tensor(x[:, b], x[:, b], bvp[:, 1], ALU.add).then_inc(xp_done, 1)

            def stationary_values(b, u):
                pool.wait_ge(pv_psum, b + 1)
                g.tensor_copy(vpad[u].rearrange("p (h e) -> p h e", h=HEADS)[:, :, 0:DH],
                              values[:, bass.ds(b * D, D)].rearrange("p (h d) -> p h d", h=HEADS)).then_inc(vpad_done, 1)

            def stacks(j):
                pool.wait_ge(got_stack[j], 2 * len(Q_PART) * 16)
                pool.sem_inc(stack_ready, 1)

            def residual(m):
                pool.wait_ge(y1_done, m + 2)
                g.tensor_tensor(x[:, m], xq[:, m], x[:, m], ALU.add).then_inc(x2_done, 1)

            def heads_to_int(b):
                pool.wait_ge(ors_done, b + 1)
                g.tensor_scalar(xn[:, b], xq[:, b], ors[:, b:b + 1], ROUND, ALU.mult, ALU.add).then_inc(round_done, 1)
                pool.wait_ge(round_done, b + 1)
                g.tensor_scalar(oq[:, b], xn[:, b], ROUND, None, ALU.subtract).then_inc(oq_done, 1)

            def norm2_rstd(half):
                four = slice(4 * half, 4 * half + 4)
                pool.wait_ge(veps_done, 2 + half)
                g.tensor_tensor(rstd[:, four], veps[:, four], neghalf[:, four], ALU.pow).then_inc(rstd_done, 1)

            pool.wait_ge(unit_psum, len(units))
            for i in range(2):
                g.memset(vpad[i], 0.0).then_inc(vpad_zero, 1)
            pool.wait_ge(vpad_zero, 2)
            for i in range(2):
                g.memset(vpad[i].rearrange("p (h e) -> p h e", h=HEADS)[:, :, DH:DH + 1], 1.0).then_inc(vpad_zero, 1)
            pool.wait_ge(v_done, TILES)
            pool.wait_ge(vpad_zero, 4)
            pool.wait_ge(xp_done, TILES)
            stacks(0)
            stationary_values(0, 0)
            stationary_values(1, 1)
            stacks(1)
            stationary_values(2, 0)
            for b in range(1, TILES):
                if b == 6:
                    norm2_rstd(0)
                heads_to_int(b - 1)
                if b >= 2:
                    residual(b - 2)
                if b in (1, 3):
                    stacks((b + 3) // 2)
                if b + 2 < TILES:
                    stationary_values(b + 2, b % 2)
            residual(TILES - 2)
            residual(TILES - 1)
            norm2_rstd(1)

            def gather(i):
                g.indirect_dma_start(gx[i], None, table, bass.IndirectOffsetOnAxis(gcol[i][:], 0)).then_inc(got_rows[i], 16)

            pool.wait_ge(table_out, 16 * (TILES + 1))
            for e in range(GBUF):
                pool.wait_ge(gcol_done, e + 1)
                gather(e)
                if e == 4:
                    pool.wait_ge(base_done, TILES)
                    pool.wait_ge(acc_in[1], 16)
                    g.dma_start(token_rows(acc[1][0:T], slice(0, TILES)), x[:]).then_inc(acc_in[1], 16)

            def expert(e, half, r, more):
                pool.wait_ge(scol_done, e + 1)
                pool.wait_ge(orow_done, e + 3)
                pool.wait_ge(acc_in[r % 2], FILL[r % 2] + 16 * half)
                pool.nop(nofuse=True)
                g.indirect_dma_start(acc[r % 2], bass.IndirectOffsetOnAxis(scol[r % OBUF][:], 0), orow[r % OBUF], None,
                                     compute_op=ALU.add).then_inc(acc_in[r % 2], 16)
                if more:
                    pool.wait_ge(gcol_done, e + GBUF + 1)
                    pool.nop(nofuse=True)
                    gather(r % GBUF)

            with pool.Fori(0, EXPERTS // RING - 1) as lap:
                for r in range(RING):
                    expert(lap * RING + r, lap * (RING // 2) + r // 2, r, True)
            for r in range(RING):
                e = EXPERTS - RING + r
                expert(e, e // 2, r, e + GBUF < EXPERTS)

        @block.scalar
        def _(act):
            s = nc.scalar
            act.dma_start(bqk[:], a["bqk"]).then_inc(got_small, 16)
            act.dma_start(gates[:], a["gates"].broadcast_to([P, 2])).then_inc(got_small, 16)
            for i, t in enumerate((ident, before)):
                act.dma_start(t[:], a["consts"][:, P * i:P * i + P]).then_inc(got_const, 16)
            act.dma_start(slotc[:], a["consts"][:, 2 * P:]).then_inc(got_const, 16)
            for i in range(2):
                act.dma_start(bvp[:, i], a["bvp"][i:i + 1].broadcast_to([P, D])).then_inc(got_small, 16)
            act.sem_inc(exp_done, 2)
            act.sem_inc(headsT_done, 1)
            act.sem_inc(orow_done, 2)

            def high_of(u):
                what, c, _ = units[u]
                col = c if what == "q" else KC + c
                act.wait_ge(unit_psum, u + 1)
                if u >= UNIT_BUF:
                    act.wait_ge(parts_out[u % UNIT_BUF], 16)
                s.activation(part[u % UNIT_BUF][:, 0], bank[u % UNIT_BUF][:], ACT.Identity, bias=bqk[:, col:col + 1]).then_inc(unit_high, 1)

            def middle_of(u):
                act.wait_ge(unit_rest, u + 1)
                s.activation(part[u % UNIT_BUF][:, 1], rest[u % 2], ACT.Copy).then_inc(unit_mid, 1)

            def normalise(b):
                s.activation(xn[:, b], x[:, b], ACT.Identity, bias=nmr[:, b:b + 1], scale=rstd[:, b:b + 1]).then_inc(xn_done, 1)

            def xq_across(j):
                act.wait_ge(xqT_psum, j + 1)
                s.activation(xqT[:, :, 256 * j:256 * j + 256], bank[6 + j % 2][:].rearrange("p (k t) -> p k t", k=KC), ACT.Copy).then_inc(xqT_done, 1)

            act.wait_ge(nmr_done, 1)
            for b in range(4):
                normalise(b)
            act.wait_ge(got_small, 64)
            high_of(0)
            for b in range(4, 8):
                normalise(b)
            s.activation(tg[:], gates[:], ACT.Tanh).then_inc(tanh_done, 1)
            act.wait_ge(w_psum, 1)
            s.activation(wqT[:].rearrange("p k (c o) -> p c k o", c=2), bank[4][:].rearrange("p (c k o) -> p c k o", c=2, k=KC), ACT.Copy).then_inc(wT_done, 1)
            high_of(1)
            middle_of(0)
            xq_across(0)
            middle_of(1)
            xq_across(1)
            high_of(2)
            high_of(3)
            middle_of(2)
            middle_of(3)
            high_of(4)
            xq_across(2)
            xq_across(3)
            high_of(5)
            middle_of(4)
            middle_of(5)
            act.wait_ge(w_psum, 2)
            s.activation(wpT[:].rearrange("p k (c o) -> p c k o", c=2), bank[5][:, 0:256].bitcast(bf16).rearrange("p (c k o) -> p c k o", c=2, k=KC), ACT.Copy).then_inc(wT_done, 1)
            high_of(6)
            high_of(7)
            middle_of(6)
            middle_of(7)

            def negmax_across(b, u):
                act.wait_ge(nm_psum, b + 1)
                s.activation(negmaxT[u][0:2 * HEADS], bank[7][0:2 * HEADS, 0:TOK // 2].bitcast(bf16), ACT.Copy).then_inc(nm_done, 1)

            def heads_out(b, u):
                act.wait_ge(pv_psum, b + 3)
                act.wait_ge(heads_psum, b + 1)
                s.activation(headsT[u], bank[4][:], ACT.Copy).then_inc(headsT_done, 1)

            def heads_row(m, u):
                act.wait_ge(oT_psum, m + 1)
                s.activation(oT[u][:], bank[5][:, 0:TOK].bitcast(bf16).rearrange("p (k t) -> p k t", k=KC), ACT.Copy).then_inc(oT_done, 1)

            def second_norm(b):
                s.activation(rows[:, b, 0:D], x[:, b], ACT.Identity, bias=nmr[:, b:b + 1], scale=rstd[:, b:b + 1]).then_inc(h_done, 1)

            def h_across(j):
                act.wait_ge(hT_psum, j + 1)
                s.activation(hT[:, :, 256 * j:256 * j + 256], bank[H_BANK[j]][:].rearrange("p (k t) -> p k t", k=KC), ACT.Copy).then_inc(hT_done, 1)

            def silu_gate(u):
                act.wait_ge(sg_psum, u + 1)
                if u >= 2:
                    act.wait_ge(sact_done, u - 1)
                n = SCH[u % 3][1]
                s.activation(sgate[u % 2][0:n], bank[2 * (u % 2)][0:n], ACT.Silu).then_inc(sgate_done, 1)

            def attend(b, u, more, merge):
                for g in range(4):
                    act.wait_ge(st_psum, 4 * b + g + 1)
                    if g == 0:
                        act.wait_ge(pv_psum, b + 1)
                    s.activation(probs[u][:, 512 * g:512 * g + 512], bank[2 + g % 2][:], ACT.Exp, scale=SCALE).then_inc(exp_done, 1)
                    if merge and g == 0:
                        heads_row(b - 2, u)
                    if not more:
                        if g == 0:
                            act.wait_ge(nmr_done, 2)
                        second_norm(g)
                if more:
                    negmax_across(b + 1, 1 - u)
                heads_out(b, u)

            act.wait_ge(pool_set, 6)
            negmax_across(0, 0)
            for b in range(TILES):
                attend(b, b % 2, b + 1 < TILES, b >= 2)
            heads_row(TILES - 2, 0)
            h_across(0)
            h_across(1)
            heads_row(TILES - 1, 1)
            act.wait_ge(nmr_done, 3)
            for b in range(4, TILES):
                second_norm(b)
            h_across(2)
            h_across(3)
            silu_gate(0)
            silu_gate(1)
            act.wait_ge(shift_done, 1)
            for b in range(TILES):
                s.activation(pexp[:, b], logit[:, b], ACT.Exp, accum_out=total[:, b:b + 1]).then_inc(pexp_done, 1)
            for u in range(2, 5):
                silu_gate(u)
            for j in range(2):
                act.wait_ge(overT_psum, j + 1)
                s.activation(overT[:, 512 * j:512 * j + 512], bank[7][0:EXPERTS], ACT.Copy).then_inc(overT_done, 1)
            silu_gate(5)

            def silu_of(e, p):
                act.wait_ge(up_psum, e + 3)
                act.wait_ge(hid_done, 2 * e + 2)
                act.nop(nofuse=True)
                s.activation(silu[p][:, 0], bank[2 + p][:, 0:CAP], ACT.Silu).then_inc(silu_done, 1)
                s.activation(silu[p][0:MR, 1], bank[2 + p][GATE_AT:GATE_AT + MR, 2 * CAP:3 * CAP], ACT.Silu).then_inc(silu_done, 1)

            def weighted_rows(e, half, r):
                p = r % 2
                act.wait_ge(down_psum, e + 3)
                act.wait_ge(gw_done, e + 1)
                act.wait_ge(acc_in[p], FILL[p] + 16 * half - 16)
                act.nop(nofuse=True)
                s.activation(orow[r % OBUF], bank[4 + p][0:CAP, 0:D], ACT.Copy, scale=gw[p][:]).then_inc(orow_done, 1)

            silu_of(0, 0)
            with act.Fori(0, EXPERTS // RING - 1) as lap:
                for r in range(RING):
                    silu_of(lap * RING + (r + 1), (r + 1) % 2)
                    weighted_rows(lap * RING + r, lap * (RING // 2) + r // 2, r)
            for r in range(RING):
                e = EXPERTS - RING + r
                if e + 1 < EXPERTS:
                    silu_of(e + 1, (r + 1) % 2)
                weighted_rows(e, e // 2, r)

        @block.vector
        def _(dve):
            v = nc.vector
            dve.sem_inc(norm_done, 1)
            dve.sem_inc(y1_done, 1)
            dve.sem_inc(gxT_done, 2)
            dve.sem_inc(hid_done, 4)
            chain = [0]

            def link(ins):
                chain[0] += 1
                ins.then_inc(dve_chain, 1)
                dve.wait_ge(dve_chain, chain[0])

            def rest_of(u):
                what, c, _ = units[u]
                col = c if what == "q" else KC + c
                dve.wait_ge(unit_high, u + 1)
                if u >= 2:
                    dve.wait_ge(unit_mid, u - 1)
                    dve.wait_ge(unit_lo, u - 1)
                v.scalar_tensor_tensor(out=rest[u % 2], in0=bank[u % UNIT_BUF][:], scalar=bqk[:, col:col + 1], in1=part[u % UNIT_BUF][:, 0],
                                       op0=ALU.add, op1=ALU.subtract).then_inc(unit_rest, 1)

            def low_of(u):
                dve.wait_ge(unit_mid, u + 1)
                v.tensor_tensor(part[u % UNIT_BUF][:, 2], rest[u % 2], part[u % UNIT_BUF][:, 1], ALU.subtract).then_inc(unit_lo, 1)

            def stats(b, done):
                v.bn_stats(stat[:, b], x[:, b]).then_inc(done, 1)

            def norm_scalars(done, base, meanwhile=lambda: None):
                for b in range(TILES):
                    dve.wait_ge(done, b + 1)
                    i = v.bn_aggr(mv[:, b], stat[:, b])
                link(i)
                v.tensor_scalar(veps[:], mv[:, :, 1], EPS, None, ALU.add).then_inc(veps_done, 1)
                meanwhile()
                dve.wait_ge(rstd_done, base)
                v.scalar_tensor_tensor(out=nmr[:], in0=mv[:, :, 0], scalar=-1.0, in1=rstd[:], op0=ALU.mult, op1=ALU.mult).then_inc(nmr_done, 1)

            def fix_weights(i):
                link(v.tensor_reduce(wamax[:, i:i + 2], w_rows[:, i:i + 2], AX.X, ALU.max, apply_absolute_value=True))
                link(v.tensor_scalar(wsc[:, i:i + 2], wamax[:, i:i + 2], 1.0 / 127.0, 1e-8, ALU.mult, ALU.max))
                link(v.reciprocal(wrs[:, i:i + 2], wsc[:, i:i + 2]))
                for j in (i, i + 1):
                    last = v.tensor_scalar(w_fix[:, j], w_rows[:, j], wrs[:, j:j + 1], ROUND, ALU.mult, ALU.add)
                link(last)

            def wq_fixed():
                dve.wait_ge(got_w, 16)
                fix_weights(0)
                for i in range(2):
                    v.tensor_scalar(w_rows[:, i], w_fix[:, i], ROUND, wsc[:, i:i + 1], ALU.subtract, ALU.mult).then_inc(w_done, 1)

            def quantise(half):
                tiles = range(4 * half, 4 * half + 4)
                four = slice(4 * half, 4 * half + 4)
                for b in tiles:
                    dve.wait_ge(xn_done, b + 1)
                    i = v.tensor_reduce(amax[:, b:b + 1], xn[:, b], AX.X, ALU.max, apply_absolute_value=True)
                link(i)
                link(v.tensor_scalar(qsc[:, four], amax[:, four], 1.0 / 127.0, 1e-8, ALU.mult, ALU.max))
                link(v.reciprocal(qrs[:, four], qsc[:, four]))
                for b in tiles:
                    i = v.tensor_scalar(xn[:, b], xn[:, b], qrs[:, b:b + 1], ROUND, ALU.mult, ALU.add)
                    if b % 2:
                        link(i)
                        for n in (b - 1, b):
                            v.tensor_scalar(xq[:, n], xn[:, n], ROUND, qsc[:, n:n + 1], ALU.subtract, ALU.mult).then_inc(xq_done, 1)

            dve.wait_ge(got_x, 16)
            for b in range(4):
                stats(b, bn_done)
            dve.wait_ge(got_x2, 16)
            for b in range(4, TILES):
                stats(b, bn_done)
            norm_scalars(bn_done, 1, wq_fixed)
            quantise(0)
            dve.wait_ge(got_small, 64)
            rest_of(0)
            rest_of(1)
            low_of(0)
            low_of(1)
            quantise(1)
            rest_of(2)
            rest_of(3)
            low_of(2)
            low_of(3)
            dve.wait_ge(tanh_done, 1)
            v.tensor_scalar(bvp[:, 1], bvp[:, 1], tg[:, 0:1], None, ALU.mult).then_inc(tbp_done, 1)
            dve.wait_ge(got_w2, 32)
            fix_weights(2)
            dve.wait_ge(got_const, 48)
            for i in range(2):
                v.tensor_scalar(wp_int[:, i], w_fix[:, 2 + i], ROUND, None, ALU.subtract).then_inc(w_done, 1)
                v.tensor_scalar(wdiag[:, i], ident[:], wsc[:, 2 + i:3 + i], None, ALU.mult).then_inc(w_done, 1)
            rest_of(4)
            rest_of(5)
            low_of(4)
            low_of(5)
            rest_of(6)
            rest_of(7)
            low_of(6)
            low_of(7)
            for b in range(TILES):
                if b == 6:
                    dve.wait_ge(w_psum, 3)
                    v.tensor_scalar(wscale[:], bank[5][:, 256:512], tg[:, 0:1], None, ALU.mult).then_inc(wT_done, 1)
                dve.wait_ge(v_psum, b // 2 + 1)
                v.tensor_tensor(values[:, D * b:D * b + D], bank[V_BANK[b // 2]][:, D * (b % 2):D * (b % 2) + D], bvp[:, 0], ALU.add).then_inc(v_done, 1)

            def maximum(b, u, g):
                dve.wait_ge(s_psum, 4 * b + g + 1)
                v.tensor_reduce(rowmax[:, u, 4 * g:4 * g + 4], bank[g % 2][:].rearrange("p (h m) -> p h m", h=4), AX.X, ALU.max).then_inc(max_done, 1)

            def split_max(b, u):
                dve.wait_ge(max_done, 4 * b + 4)
                v.tensor_scalar(negmax[:, u, 0:HEADS], rowmax[:, u], -1.0, None, ALU.mult).then_inc(split_done, 1)
                dve.wait_ge(split_done, 2 * b + 1)
                v.scalar_tensor_tensor(out=negmax[:, u, HEADS:2 * HEADS], in0=rowmax[:, u], scalar=-1.0, in1=negmax[:, u, 0:HEADS],
                                       op0=ALU.mult, op1=ALU.subtract).then_inc(split_done, 1)

            heads_out = bank[6][:].rearrange("p (h e) -> p h e", e=VW)
            xq_flat = xq[:].rearrange("p b h -> p (b h)")
            STEPS = 3

            def heads_normalised(b, u):
                dve.wait_ge(heads_psum, b + 3)
                v.reciprocal(rden[:, u], heads_out[:, :, DH]).then_inc(att_chain, 1)
                dve.wait_ge(att_chain, STEPS * b + 1)
                v.tensor_tensor(xq_flat[:, bass.ds(b * D, D)].rearrange("p (h d) -> p h d", h=HEADS), heads_out[:, :, 0:DH],
                                rden[:, u].unsqueeze(2).broadcast_to([P, HEADS, DH]), ALU.mult).then_inc(norm_done, 1)

            def heads_scale(b):
                one = bass.ds(b, 1)
                dve.wait_ge(norm_done, b + 2)
                v.tensor_reduce(oamax[:, one], xq_flat[:, bass.ds(b * D, D)], AX.X, ALU.max, apply_absolute_value=True).then_inc(att_chain, 1)
                dve.wait_ge(att_chain, STEPS * b + 2)
                v.tensor_scalar(osc[:, one], oamax[:, one], 1.0 / 127.0, 1e-8, ALU.mult, ALU.max).then_inc(att_chain, 1)

            def heads_rscale(b):
                one = bass.ds(b, 1)
                dve.wait_ge(att_chain, STEPS * b + 3)
                v.reciprocal(ors[:, one], osc[:, one]).then_inc(ors_done, 1)

            x_flat = x[:].rearrange("p b h -> p (b h)")
            stat_flat = stat[:].rearrange("p b i -> p (b i)")

            def project(m):
                dve.wait_ge(y_psum, m + 1)
                v.scalar_tensor_tensor(out=xq_flat[:, bass.ds(m * D, D)], in0=bank[5][:, D:2 * D], scalar=osc[:, bass.ds(m, 1)],
                                       in1=wscale[:], op0=ALU.mult, op1=ALU.mult).then_inc(y1_done, 1)

            def stats2(m):
                dve.wait_ge(x2_done, m + 1)
                v.bn_stats(stat_flat[:, bass.ds(m * 6, 6)], x_flat[:, bass.ds(m * D, D)]).then_inc(bn2_done, 1)

            def norm2_veps(half):
                four = slice(4 * half, 4 * half + 4)
                for b in range(4 * half, 4 * half + 4):
                    dve.wait_ge(bn2_done, b + 1)
                    v.bn_aggr(mv[:, b], stat[:, b]).then_inc(mv_done, 1)
                dve.wait_ge(mv_done, 4 * half + 4)
                v.tensor_scalar(veps[:, four], mv[:, four, 1], EPS, None, ALU.add).then_inc(veps_done, 1)

            def norm2_nmr(half):
                four = slice(4 * half, 4 * half + 4)
                dve.wait_ge(rstd_done, 2 + half)
                v.scalar_tensor_tensor(out=nmr[:, four], in0=mv[:, four, 0], scalar=-1.0, in1=rstd[:, four], op0=ALU.mult, op1=ALU.mult).then_inc(nmr_done, 1)

            def shared_hidden(u):
                h, c = u // 3, u % 3
                n = SCH[c][1]
                dve.wait_ge(sgate_done, u + 1)
                v.tensor_tensor(sact[0:n, c * T + 512 * h:c * T + 512 * h + 512], sgate[u % 2][0:n], bank[2 * (u % 2) + 1][0:n], ALU.mult).then_inc(sact_done, 1)

            def attend(b, u, more, before):
                if more:
                    maximum(b + 1, 1 - u, 1)
                if before:
                    heads_normalised(b - 1, 1 - u)
                if more:
                    maximum(b + 1, 1 - u, 2)
                if before:
                    heads_scale(b - 1)
                if before > 1:
                    project(b - 2)
                if before:
                    heads_rscale(b - 1)
                if more:
                    maximum(b + 1, 1 - u, 3)
                    split_max(b + 1, 1 - u)
                if more > 1:
                    maximum(b + 2, u, 0)
                if before > 1:
                    stats2(b - 2)

            for g in range(4):
                maximum(0, 0, g)
            split_max(0, 0)
            maximum(1, 1, 0)
            for b in range(TILES):
                if b == TILES - 2:
                    norm2_veps(0)
                elif b == TILES - 1:
                    norm2_nmr(0)
                attend(b, b % 2, min(2, TILES - 1 - b), min(2, b))
            b = TILES - 1
            heads_normalised(b, 1)
            heads_scale(b)
            heads_rscale(b)
            dve.wait_ge(ors_done, b + 1)
            v.tensor_scalar(xn[:, b], xq[:, b], ors[:, b:b + 1], ROUND, ALU.mult, ALU.add).then_inc(round_done, 1)
            dve.wait_ge(round_done, b + 1)
            v.tensor_scalar(oq[:, b], xn[:, b], ROUND, None, ALU.subtract).then_inc(oq_done, 1)
            for m in (TILES - 2, TILES - 1):
                project(m)
                stats2(m)
            norm2_veps(1)
            norm2_nmr(1)
            shared_hidden(0)

            logit_bank, pos_bank = [bank[i][:].rearrange("p (b e) -> p b e", b=TILES) for i in (7, 6)]
            dve.wait_ge(logit_psum, 2)
            dve.wait_ge(pool_set, 10)
            link(v.tensor_reduce(lmax[:], logit_bank, AX.X, ALU.max))
            link(v.tensor_tensor(logit, logit_bank, lmax[:].unsqueeze(2).broadcast_to([P, TILES, EXPERTS]), ALU.subtract))
            v.tensor_scalar(logit, logit, LOWEST, None, ALU.max).then_inc(shift_done, 1)
            shared_hidden(1)
            dve.wait_ge(shift_done, 1)
            link(v.tensor_reduce(gbest[:, :, 0:GROUPS], logit.rearrange("p b (g e) -> p b g e", g=GROUPS), AX.X, ALU.max))
            for b in range(TILES):
                i = v.max(g8[:, b], gbest[:, b, 0:GROUPS])
            link(i)
            link(v.tensor_copy(gtop[:, :, 0:TOPG], g8[:, :, 0:TOPG]))
            for b in range(TILES):
                i = v.match_replace(gout[:, b], gtop[:, b], gbest[:, b], CHOSEN)
            link(i)
            link(v.tensor_scalar(gcap[:], gout[:, :, 0:GROUPS], CHOSEN, LOWEST, ALU.is_lt, ALU.mult))
            link(v.tensor_tensor(cand[:, :, 0:EXPERTS].rearrange("p b (g e) -> p b g e", g=GROUPS), logit.rearrange("p b (g e) -> p b g e", g=GROUPS),
                                 gcap[:].unsqueeze(3).broadcast_to([P, TILES, GROUPS, GSIZE]), ALU.min))
            for b in range(TILES):
                i = v.max(e8[:, b], cand[:, b, 0:EXPERTS])
            link(i)
            link(v.tensor_copy(etop[:, :, 0:TOPK], e8[:, :, 0:TOPK]))
            for b in range(TILES):
                i = v.match_replace(eout[:, b], etop[:, b], cand[:, b], CHOSEN)
            link(i)
            v.tensor_scalar(sel[:], eout[:, :, 0:EXPERTS], CHOSEN, None, ALU.is_equal).then_inc(sel_done, 1)
            shared_hidden(2)
            dve.wait_ge(pexp_done, TILES)
            link(v.reciprocal(rtotal[:], total[:]))
            link(v.tensor_scalar(rtotal[:], rtotal[:], tg[:, 1:2], None, ALU.mult))
            link(v.tensor_tensor(pexp, pexp, rtotal[:].unsqueeze(2).broadcast_to([P, TILES, EXPERTS]), ALU.mult))
            v.scalar_tensor_tensor(out=rows[:, :, D:ROW], in0=eout[:, :, 0:EXPERTS], scalar=CHOSEN, in1=pexp,
                                   op0=ALU.is_equal, op1=ALU.mult).then_inc(wrow_done, 1)
            dve.wait_ge(selT_psum, 1)
            dve.wait_ge(got_tokv, 16)
            selT = bank[4][0:EXPERTS].bitcast(bf16)
            v.tensor_tensor(key2, selT, tokv[:, 1], ALU.mult).then_inc(key_done, 1)
            v.tensor_tensor(key, selT, tokv[:, 0], ALU.mult).then_inc(key_done, 1)
            dve.wait_ge(key_done, 2)

            def round_(r):
                link(v.max(order[:, 8 * r:8 * r + 8], key))
                if 8 * r + 8 < CAP:
                    link(v.match_replace(key, order[:, 8 * r:8 * r + 8], key, 0.0))

            def add_shared(j):
                dve.wait_ge(sd_psum, 4 - j)
                for b in (2 * j, 2 * j + 1):
                    v.scalar_tensor_tensor(out=x[:, b], in0=bank[SD_BANK[j]][:, D * (b % 2):D * (b % 2) + D], scalar=tg[:, 1:2],
                                           in1=x[:, b], op0=ALU.mult, op1=ALU.add).then_inc(base_done, 1)

            link(v.tensor_reduce(last[:, 0:1], key2, AX.X, ALU.max))
            link(v.tensor_scalar(last[:, 1:2], last[:, 0:1], -1.0, T + 1.0, ALU.mult, ALU.add))
            link(v.scalar_tensor_tensor(out=last[:, 2:3], in0=last[:, 0:1], scalar=0.0, in1=last[:, 1:2], op0=ALU.is_gt, op1=ALU.mult))
            round_(0)
            shared_hidden(3)
            dve.wait_ge(pos_psum, 1)
            dve.wait_ge(wrow_done, 1)
            v.scalar_tensor_tensor(out=over, in0=pos_bank, scalar=CAP - 1.0, in1=rows[:, :, D:ROW], op0=ALU.is_ge, op1=ALU.mult).then_inc(over_done, 1)
            for r in range(1, CAP // 8):
                round_(r)
                if r in (3, 5):
                    shared_hidden(4 + (r == 5))
            v.tensor_copy(order[:, CAP - 1:CAP], last[:, 2:3]).then_inc(order_done, 1)
            dve.wait_ge(slot_psum, 1)
            slots = bank[7][0:CAP, 0:EXPERTS]
            v.tensor_scalar(gidx[:], slots, -1.0, float(T), ALU.mult, ALU.add).then_inc(idx_done, 1)
            dve.wait_ge(idx_done, 1)

            def to_gather(e, i):
                v.tensor_copy(gcol[i][:], gidx[:, bass.ds(e, 1)]).then_inc(gcol_done, 1)

            for e in range(GBUF):
                to_gather(e, e)
            link(v.tensor_scalar(slotv[:, 1], slots, slotc[0:CAP, 0:1], None, ALU.mult))
            link(v.scalar_tensor_tensor(out=empty[:], in0=slotv[:, 1], scalar=0.0, in1=slotc[0:CAP, 2:], op0=ALU.is_equal, op1=ALU.mult))
            link(v.tensor_scalar(slotv[:, 0], slotv[:, 1], -1.0, float(T), ALU.mult, ALU.add))
            link(v.tensor_tensor(sidx[:], slotv[:, 0], empty[:], ALU.add))
            for j in (3, 2, 1):
                add_shared(j)

            def rows_across(e, u):
                dve.wait_ge(gT_psum, e + 1)
                dve.wait_ge(up_psum, e + 1)
                dve.nop(nofuse=True)
                v.tensor_copy(gxT[u], bank[u][:, 0:KC * CAP].rearrange("p (k t) -> p k t", k=KC)).then_inc(gxT_done, 1)

            def expert(e, lap, r, more, across):
                u = r % 2
                dve.wait_ge(silu_done, 2 * e + 2)
                dve.wait_ge(down_psum, e + 1)
                dve.nop(nofuse=True)
                v.tensor_tensor(hid[u][:, 0], silu[u][:, 0], bank[2 + u][:, CAP:2 * CAP], ALU.mult).then_inc(hid_done, 1)
                v.tensor_tensor(hid[u][0:MR, 1], silu[u][0:MR, 1], bank[2 + u][0:MR, 2 * CAP:3 * CAP], ALU.mult).then_inc(hid_done, 1)
                if across:
                    rows_across(e + 2, u)
                dve.wait_ge(got_rows[r % GBUF], lap * (16 * RING // GBUF) + 16 * (r // GBUF + 1))
                dve.wait_ge(orow_done, e + 1)
                dve.nop(nofuse=True)
                v.tensor_scalar(gw[u][:], gx[r % GBUF][:, bass.ds(e + D, 1)], slotc[0:CAP, 0:1], slotc[0:CAP, 1:2], ALU.mult, ALU.add).then_inc(gw_done, 1)
                dve.wait_ge(acc_in[u], lap * (8 * RING) + FILL[u] + 16 * (r // 2) - 16)
                dve.nop(nofuse=True)
                v.tensor_copy(scol[r % OBUF][:], sidx[:, bass.ds(e, 1)]).then_inc(scol_done, 1)
                if more:
                    to_gather(e + GBUF, r % GBUF)

            rows_across(0, 0)
            add_shared(0)
            rows_across(1, 1)
            with dve.Fori(0, EXPERTS // RING - 1) as lap:
                for r in range(RING):
                    expert(lap * RING + r, lap, r, True, True)
            for r in range(RING):
                e = EXPERTS - RING + r
                expert(e, EXPERTS // RING - 1, r, e + GBUF < EXPERTS, e + 2 < EXPERTS)

            dve.wait_ge(got_last, 32)
            v.tensor_tensor(lastrow[:, 2], lastrow[:, 0], lastrow[:, 1], ALU.add).then_inc(last_done, 1)
            for j in range(4):
                dve.wait_ge(got_acc[j], 32)
                two = xn[:, 2 * j:2 * j + 2]
                v.tensor_tensor(two, two, xq[:, 2 * j:2 * j + 2], ALU.add).then_inc(sum_done, 1)
                dve.wait_ge(sum_done, j + 1)
                dve.wait_ge(corr_psum, j + 1)
                v.tensor_tensor(two, two, bank[j][:].rearrange("p (b h) -> p b h", b=2), ALU.add).then_inc(y_done, 1)

        @block.tensor
        def _(pe):
            t = nc.tensor
            pe.sem_inc(pv_psum, 2)
            pe.sem_inc(heads_psum, 2)
            pe.sem_inc(up_psum, 2)
            pe.sem_inc(down_psum, 2)

            def unit(u):
                what, c, h = units[u]
                if u >= UNIT_BUF:
                    pe.wait_ge(unit_rest, u - UNIT_BUF + 1)
                for k in range(KC):
                    w = wkv[:, k, P * c:P * c + P] if what == "k" else wqT[:, k, P * c:P * c + P]
                    src = ctxT if what == "k" else xqT
                    last = t.matmul(bank[u % UNIT_BUF][:], w, src[:, k, 512 * h:512 * h + 512], start=(k == 0), stop=(k == KC - 1))
                last.then_inc(unit_psum, 1)

            def xq_across(j):
                pe.wait_ge(xq_done, 2 * j + 2)
                if j >= 2:
                    pe.wait_ge(xqT_done, j - 1)
                for k in range(KC):
                    for b in (2 * j, 2 * j + 1):
                        last = t.transpose(bank[6 + j % 2][:, 256 * k + P * (b % 2):256 * k + P * (b % 2) + P], xq[:, b, P * k:P * k + P], ident[:])
                last.then_inc(xqT_psum, 1)

            pe.wait_ge(got_kv, 16)
            pe.wait_ge(got_ctx, 16)
            unit(0)
            unit(1)
            pe.wait_ge(got_ctx2, 16)
            unit(2)
            unit(3)
            pe.wait_ge(w_done, 2)
            pe.wait_ge(got_const, 48)
            for c in range(2):
                for k in range(KC):
                    last = t.transpose(bank[4][:, 256 * c + P * k:256 * c + P * k + P], w_rows[:, c, P * k:P * k + P], ident[:])
            last.then_inc(w_psum, 1)
            for half in range(2):
                xq_across(2 * half)
                xq_across(2 * half + 1)
                pe.wait_ge(wT_done, 1)
                pe.wait_ge(xqT_done, 2 * half + 2)
                unit(4 + 2 * half)
                unit(5 + 2 * half)
            def values_of(j):
                for b in (2 * j, 2 * j + 1):
                    for k in range(KC):
                        last = t.matmul(bank[V_BANK[j]][:, D * (b % 2):D * (b % 2) + D], ctxT[:, k, P * b:P * b + P], wkv[:, k, D:2 * D],
                                        start=(k == 0), stop=(k == KC - 1))
                last.then_inc(v_psum, 1)

            pe.wait_ge(w_done, 6)
            pe.wait_ge(consts_b, 3)
            wp_bank = bank[5][:, 0:256].bitcast(bf16)
            for c in range(2):
                for k in range(KC):
                    last = t.transpose(wp_bank[:, 256 * c + P * k:256 * c + P * k + P], wp_int[:, c, P * k:P * k + P], identb[:])
            last.then_inc(w_psum, 1)
            pe.wait_ge(got_w2, 32)
            for j in range(3):
                if j == 1:
                    pe.wait_ge(xqT_done, 4)
                values_of(j)
            pe.wait_ge(wT_done, 2)
            pe.wait_ge(pool_set, 4)
            t.matmul(bank[5][:, 256:512], onesf[:], wdiag[:].rearrange("p c o -> p (c o)"), start=True, stop=True).then_inc(w_psum, 1)
            pe.wait_ge(wT_done, 3)
            values_of(3)

            def scores(b, g):
                for h in range(4 * g, 4 * g + 4):
                    last = t.matmul(bank[g % 2][:, P * (h % 4):P * (h % 4) + P], qs[:, bass.ds(b * TOK + h * T, TOK)], ks[:, bass.ds(b * TOK + h * T, TOK)],
                                    start=True, stop=True)
                last.then_inc(s_psum, 1)

            def scores_t(b, g, u):
                pe.wait_ge(exp_done, 4 * b + g + 1)
                for h in range(4 * g, 4 * g + 4):
                    dst = bank[2 + g % 2][:, P * (h % 4):P * (h % 4) + P]
                    t.matmul(dst, ks[:, bass.ds(b * TOK + h * T, TOK)], qs[:, bass.ds(b * TOK + h * T, TOK)], start=True, stop=False)
                    last = t.matmul(dst, pick[:, h], negmaxT[u][:], start=False, stop=True)
                last.then_inc(st_psum, 1)

            def heads_times_values(b, g, u):
                pe.wait_ge(exp_done, 4 * b + g + 3)
                if g == 0:
                    pe.wait_ge(headsT_done, b + 1)
                    pe.wait_ge(vpad_done, b + 1)
                for i in range(4):
                    h = 4 * g + i
                    last = t.matmul(bank[4][VW * i:VW * i + VW, TOK * g:TOK * g + TOK], vpad[u][:, VW * h:VW * h + VW], probs[u][:, TOK * h:TOK * h + TOK],
                                    start=True, stop=True)
                if g == 3:
                    last.then_inc(pv_psum, 1)

            def heads_across(b, u):
                pe.wait_ge(headsT_done, b + 2)
                pe.wait_ge(norm_done, b + 1)
                for g in range(4):
                    last = t.transpose(bank[6][:, TOK * g:TOK * g + TOK], headsT[u][:, TOK * g:TOK * g + TOK], ident[:])
                last.then_inc(heads_psum, 1)

            def negmax_across(b, u):
                pe.wait_ge(split_done, 2 * b + 2)
                t.transpose(bank[7][0:2 * HEADS, 0:TOK // 2].bitcast(bf16), negmax[:, u], identb[:]).then_inc(nm_psum, 1)

            def next_scores(b, g):
                pe.wait_ge(max_done, 4 * b + g - 1)
                scores(b, g)

            def heads_row(m, u):
                pe.wait_ge(oq_done, m + 1)
                pe.wait_ge(y1_done, m + 1)
                for k in range(KC):
                    last = t.transpose(bank[5][:, 0:TOK].bitcast(bf16)[:, P * k:P * k + P], oq_flat[:, bass.ds(m * D + P * k, P)], identb[:])
                last.then_inc(oT_psum, 1)

            def project(m, u):
                pe.wait_ge(oT_done, m + 1)
                for k in range(KC):
                    last = t.matmul(bank[5][:, D:2 * D], oT[u][:, k], wpT[:, k], start=(k == 0), stop=(k == KC - 1))
                last.then_inc(y_psum, 1)

            def attend(b, u, more, before):
                for g in range(4):
                    if g == 0:
                        pe.wait_ge(nm_done, b + 1)
                    elif g < 3 and more:
                        next_scores(b + 1, g + 1)
                    elif g == 3 and more > 1:
                        if u == 0:
                            pe.wait_ge(stack_ready, b // 2 + 2)
                        next_scores(b + 2, 0)
                    if g == 1 and before:
                        heads_across(b - 1, 1 - u)
                    scores_t(b, g, u)
                    if g == 0 and before > 1:
                        heads_row(b - 2, u)
                    if g == 2 and before > 1:
                        project(b - 2, u)
                    if g:
                        heads_times_values(b, g - 1, u)
                if more > 1:
                    next_scores(b + 2, 1)
                if more:
                    negmax_across(b + 1, 1 - u)
                heads_times_values(b, 3, u)

            oq_flat = oq[:].rearrange("p b h -> p (b h)")
            pe.wait_ge(unit_rest, 8)
            pe.wait_ge(v_done, 8)
            pe.wait_ge(wT_done, 3)
            pe.wait_ge(stack_ready, 1)
            pe.wait_ge(pool_set, 6)
            scores(0, 0)
            scores(0, 1)
            for b, g in ((0, 2), (0, 3), (1, 0), (1, 1)):
                pe.wait_ge(max_done, 4 * b + g - 1)
                scores(b, g)
            negmax_across(0, 0)
            for b in range(TILES):
                attend(b, b % 2, min(2, TILES - 1 - b), min(2, b))

            def h_across(j):
                pe.wait_ge(h_done, 2 * j + 2)
                for k in range(KC):
                    for b in (2 * j, 2 * j + 1):
                        last = t.transpose(bank[H_BANK[j]][:, 256 * k + P * (b % 2):256 * k + P * (b % 2) + P], rows[:, b, P * k:P * k + P], ident[:])
                last.then_inc(hT_psum, 1)

            def logits(half):
                pe.wait_ge(hT_done, 2 * half + 2)
                for b in range(4 * half, 4 * half + 4):
                    for k in range(KC):
                        last = t.matmul(bank[7][:, EXPERTS * b:EXPERTS * b + EXPERTS], hT[:, k, P * b:P * b + P], gateT[:, k], start=(k == 0), stop=(k == KC - 1))
                last.then_inc(logit_psum, 1)

            def shared_up(u):
                h, c = u // 3, u % 3
                m0, n = SCH[c]
                if u >= 2:
                    pe.wait_ge(sact_done, u - 1)
                for i in range(2):
                    for k in range(KC):
                        last = t.matmul(bank[2 * (u % 2) + i][0:n], sgu[:, k, i, m0:m0 + n], hT[:, k, 512 * h:512 * h + 512], start=(k == 0), stop=(k == KC - 1))
                last.then_inc(sg_psum, 1)

            heads_row(TILES - 2, 0)
            pe.wait_ge(max_done, 4 * TILES)
            pe.wait_ge(exp_done, 4 * TILES + 2)
            h_across(0)
            h_across(1)
            heads_across(TILES - 1, 1)
            project(TILES - 2, 0)
            pe.wait_ge(got_gate, 16)
            logits(0)
            heads_row(TILES - 1, 1)
            project(TILES - 1, 1)
            pe.wait_ge(got_shared, 48)
            shared_up(0)
            pe.wait_ge(headsT_done, TILES + 1)
            pe.wait_ge(y1_done, TILES + 1)
            h_across(2)
            h_across(3)
            logits(1)
            shared_up(1)
            shared_up(2)
            pe.wait_ge(norm_done, TILES + 1)
            pe.wait_ge(sel_done, 1)
            selT = bank[4][0:EXPERTS].bitcast(bf16)
            for b in range(TILES):
                last = t.transpose(selT[:, P * b:P * b + P], sel[:, b], identb[:])
            last.then_inc(selT_psum, 1)
            for b in range(TILES):
                dst = bank[6][:, EXPERTS * b:EXPERTS * b + EXPERTS]
                for c in range(b):
                    t.matmul(dst, onesb[:], sel[:, c], start=(c == 0), stop=False)
                last = t.matmul(dst, beforeb[:], sel[:, b], start=(b == 0), stop=True)
            last.then_inc(pos_psum, 1)
            shared_up(3)
            shared_up(4)
            pe.wait_ge(over_done, 1)
            for j in range(2):
                if j:
                    pe.wait_ge(overT_done, j)
                for b in range(4):
                    last = t.transpose(bank[7][0:EXPERTS, P * b:P * b + P], over[:, 4 * j + b], ident[:])
                last.then_inc(overT_psum, 1)
            shared_up(5)
            pe.wait_ge(sact_done, 6)
            pe.wait_ge(key_done, 2)

            def shared_down(j):
                for b in (2 * j, 2 * j + 1):
                    for c, (m0, n) in enumerate(SCH):
                        last = t.matmul(bank[SD_BANK[j]][:, D * (b % 2):D * (b % 2) + D], sact[0:n, c * T + P * b:c * T + P * b + P], sdn[0:n, c], start=(c == 0), stop=(c == 2))
                last.then_inc(sd_psum, 1)

            shared_down(3)
            shared_down(2)
            pe.wait_ge(order_done, 1)
            pe.wait_ge(overT_done, 2)
            t.transpose(bank[7][0:CAP, 0:EXPERTS], order[:], ident[0:EXPERTS, 0:EXPERTS]).then_inc(slot_psum, 1)
            shared_down(1)
            shared_down(0)

            def rows_across(e, lap, r):
                pe.wait_ge(got_rows[r % GBUF], lap * (16 * RING // GBUF) + 16 * (r // GBUF + 1))
                pe.wait_ge(gxT_done, e + 1)
                pe.nop(nofuse=True)
                for k in range(KC):
                    last = t.transpose(bank[r % 2][:, CAP * k:CAP * k + CAP], gx[r % GBUF][:, P * k:P * k + P], ident[0:CAP, 0:CAP])
                last.then_inc(gT_psum, 1)

            def up(e, lap, r):
                s, lap = r % RING, lap + r // RING
                pe.wait_ge(got_expert[s], lap * 48 + 48)
                pe.wait_ge(gxT_done, e + 3)
                pe.wait_ge(hid_done, 2 * e + 2)
                pe.nop(nofuse=True)
                for i, (c0, n) in enumerate(UP_COLS):
                    for k in range(KC):
                        last = t.matmul(bank[2 + r % 2][0:n, CAP * i:CAP * i + CAP], wgu[s][:, k, c0:c0 + n], gxT[r % 2][:, k],
                                        start=(k == 0), stop=(k == KC - 1))
                last.then_inc(up_psum, 1)

            def down(e, r):
                pe.wait_ge(hid_done, 2 * e + 6)
                pe.wait_ge(orow_done, e + 1)
                pe.nop(nofuse=True)
                for c, n in enumerate((P, MR)):
                    last = t.matmul(bank[4 + r % 2][0:CAP, 0:D], hid[r % 2][0:n, c], wdn[r][0:n, c], start=(c == 0), stop=(c == 1))
                last.then_inc(down_psum, 1)

            rows_across(0, 0, 0)
            rows_across(1, 0, 1)
            up(0, 0, 0)
            pe.wait_ge(base_done, TILES)
            with pe.Fori(0, EXPERTS // RING - 1) as lap:
                for r in range(RING):
                    up(lap * RING + (r + 1), lap, r + 1)
                    rows_across(lap * RING + (r + 2), lap, r + 2)
                    down(lap * RING + r, r)
            lap = EXPERTS // RING - 1
            for r in range(RING):
                e = lap * RING + r
                if e + 1 < EXPERTS:
                    up(e + 1, lap, r + 1)
                if e + 2 < EXPERTS:
                    rows_across(e + 2, lap, r + 2)
                down(e, r)
            pe.wait_ge(last_done, 1)
            pe.wait_ge(hid_done, 2 * EXPERTS + 4)
            for j in range(4):
                for b in (2 * j, 2 * j + 1):
                    last = t.matmul(bank[j][:, D * (b % 2):D * (b % 2) + D], overT[:, P * b:P * b + P], lastrow[:, 2], start=True, stop=True)
                last.then_inc(corr_psum, 1)


def constants():
    slot = np.arange(P)
    notlast = np.where(slot == CAP - 1, 0.0, 1.0)
    spare = np.repeat(slot[:, None].astype(np.float64), EXPERTS, 1)
    spare[CAP - 1] = CAP + np.arange(EXPERTS)
    c = np.concatenate([np.eye(P), np.triu(np.ones((P, P)), 1), notlast[:, None], 1 - notlast[:, None], spare], 1)
    tok = np.arange(T)
    tokv = np.repeat(np.stack([T - tok, tok + 1])[None], EXPERTS, 0)
    return c.astype(np.float32), tokv.astype(np.float32)


def kernel(**inputs):
    import concourse.bacc as _bacc
    from concourse.bass_utils import run_bass_kernel_spmd as _run

    g = {k: np.asarray(v) for k, v in inputs.items()}
    n = lambda k: g["L0_" + k]
    lay = np.ascontiguousarray
    consts, tokv = constants()
    chunks = lambda t: lay(t.reshape(KC, P, -1).transpose(1, 0, 2))
    wg, wu = n("ffn_Wg"), n("ffn_Wu")
    gap = np.zeros((EXPERTS, GATE_AT - MR, D), wg.dtype)
    wgu = np.concatenate([wg[:, :P], wu[:, :P], wu[:, P:], gap, wg[:, P:]], 1)
    arrays = {
        "x": lay(g["x"].transpose(1, 0, 2)),
        "ctxT": chunks(g["ctx_2048"].reshape(T, D).T),
        "wkv": chunks(n("xattn_wkv").T),
        "w_rows": lay(np.concatenate([n("xattn_wq").reshape(2, P, D), n("xattn_wp").reshape(2, P, D)]).transpose(1, 0, 2)),
        "bqk": lay(np.concatenate([n("xattn_bq").reshape(2, P), n("xattn_bkv")[:D].reshape(2, P)]).T),
        "bvp": np.stack([n("xattn_bkv")[D:], n("xattn_bp")]),
        "gates": np.concatenate([g["g_xattn"], g["g_ffn"]])[None],
        "consts": consts,
        "tokv": tokv,
        "gateT": chunks(n("ffn_gate_weight").T),
        "wgu": lay(wgu.reshape(EXPERTS, WG, KC, P).transpose(0, 3, 2, 1)),
        "wdn": lay(n("ffn_Wd").transpose(0, 2, 1)),
        "sgu": lay(np.stack([n("ffn_Sg"), n("ffn_Su")]).reshape(2, MS, KC, P).transpose(3, 2, 0, 1)),
        "sdn": lay(n("ffn_Sd").T),
    }
    nc = _bacc.Bacc("TRN2", target_bir_lowering=False, num_devices=1)
    a = {k: nc.dram_tensor(k + "_in", t.shape, mybir.dt.from_np(t.dtype), kind="ExternalInput").ap() for k, t in arrays.items()}
    out = nc.dram_tensor("out", (TILES, TOK, D), mybir.dt.float32, kind="ExternalOutput").ap()
    gated_block(nc, a, out)
    r = _run(nc, [{k + "_in": t for k, t in arrays.items()}], core_ids=[0])
    return r.results[0]["out"]
```

```python
import concourse.bass as bass
from concourse import mybir
from contextlib import ExitStack
import numpy as np

P = 128
TILES, TOK, D = 8, 128, 256
T = TILES * TOK
HALF = T // 2
KC = D // P
HEADS, DH = 16, 16
VW = 32
PARTS = 3
Q_PART = [0, 0, 1, 0, 2, 1, 1, 2]
K_PART = [0, 1, 0, 2, 0, 1, 2, 1]
EXPERTS, GROUPS, TOPG, TOPK = 64, 8, 3, 6
GSIZE = EXPERTS // GROUPS
CAP = 96
M = 176
MR = M - P
GATE_AT = 64
UP_COLS = [(0, P), (P, P), (2 * P, GATE_AT + MR)]
WG = UP_COLS[2][0] + UP_COLS[2][1]
MS = 352
SCH = [(0, 128), (128, 128), (256, 96)]
ROW = D + EXPERTS
SPARE = T
LASTROW = T + CAP
ROWS = T + 2 * P
LOGIT_BANK = (7, 6)
SD_BANK = (4, 5, 6, 3)
SD_ORDER = (1, 0, 3, 2)
NORM2 = ((0, 4), (4, 7), (7, 8))
H_BANK = (0, 1, 4, 5)
V_BANK = (4, 6, 7, 4)
UNIT_BUF = 4
RING = 16
GBUF = 8
OBUF = 4
EPS = 1e-5
ROUND = 12582912.0
LOWEST = -87.33
MARK, CHOSEN = 1.0, 2.0
SCALE = 1.0 / float(np.sqrt(DH))


def gated_block(nc, a, out):
    f32, bf16, u32 = mybir.dt.float32, mybir.dt.bfloat16, mybir.dt.uint32
    ALU, ACT, AX = mybir.AluOpType, mybir.ActivationFunctionType, mybir.AxisListType
    ctx = ExitStack()
    with ctx:
        def sb(name, shape, dt=f32):
            return ctx.enter_context(nc.sbuf_tensor(name, shape, dt))

        def sem(name):
            return ctx.enter_context(nc.semaphore(name))

        def dram(name, shape, dt=f32):
            return nc.dram_tensor(name, shape, dt, kind="Internal").ap()

        q_parts = dram("q_parts", (PARTS, D, T), bf16)
        k_parts = dram("k_parts", (PARTS, D, T), bf16)
        table = dram("table", (ROWS, ROW))
        acc = [dram(f"acc{i}", (ROWS, D)) for i in range(2)]

        def carver(arena):
            at = [0]

            def cut(n, parts=P):
                at[0] += n
                return arena[0:parts, at[0] - n:at[0]]
            return cut

        stream = sb("stream", [P, 20 * T])
        cut = carver(stream)
        qs, ks = [cut(HEADS * T // 2).bitcast(bf16) for _ in range(2)]
        probs = [cut(HEADS * TOK) for _ in range(2)]
        cut = carver(stream)
        wgu, wdn = [], []
        for _ in range(RING):
            wgu.append(cut(KC * WG).rearrange("p (k m) -> p k m", k=KC))
            wdn.append(cut(2 * D).rearrange("p (c h) -> p c h", c=2))
        scratch = sb("scratch", [P, 10880])
        cut = carver(scratch)
        xqT = cut(KC * T).rearrange("p (k t) -> p k t", k=KC)
        w_rows, w_fix = [cut(4 * D).rearrange("p (c h) -> p c h", c=4) for _ in range(2)]
        wkv = cut(KC * 2 * D).rearrange("p (k h) -> p k h", k=KC)
        part = [cut(PARTS * 256).bitcast(bf16).rearrange("p (r t) -> p r t", r=PARTS) for _ in range(UNIT_BUF)]
        rest = [probs[1][:, 512 * i:512 * i + 512] for i in range(2)]
        values = cut(TILES * D)
        cut = carver(scratch)
        vpad = [cut(HEADS * VW) for _ in range(2)]
        headsT = [cut(4 * TOK) for _ in range(2)]
        cut = carver(scratch)
        sact = cut(3 * T)
        sgate = [cut(512) for _ in range(2)]
        key, key2 = [cut(HALF) for _ in range(2)]
        lists = cut(2 * EXPERTS, CAP)
        first, once = [cut(CAP, CAP) for _ in range(2)]
        slots = cut(EXPERTS, CAP)
        cut(T - 3 * EXPERTS - 2 * CAP)
        overT = cut(T, EXPERTS)
        logit, pexp, over = [cut(TILES * EXPERTS).rearrange("p (b e) -> p b e", b=TILES) for _ in range(3)]
        eout = cut(TILES * (EXPERTS + 8 - TOPK)).rearrange("p (b e) -> p b e", b=TILES)
        sup = [cut(512) for _ in range(2)]
        cut = carver(scratch)
        orow = [cut(D, CAP) for _ in range(OBUF)]
        gxT = [cut(KC * CAP).rearrange("p (k t) -> p k t", k=KC) for _ in range(2)]
        silu, hid = [[cut(2 * CAP).rearrange("p (c t) -> p c t", c=2) for _ in range(2)] for _ in range(2)]
        lastrow = cut(3 * D, EXPERTS).rearrange("p (i h) -> p i h", i=3)
        cut = carver(scratch[:, 7 * T:])
        gx = [cut(ROW, CAP) for _ in range(GBUF)]
        x = sb("x", [P, TILES, D])
        xn = sb("xn", [P, TILES, D])
        xq = sb("xq", [P, TILES, D])
        ctxT = sb("ctxT", [P, KC, T])
        hT = ctxT
        wp_int = sb("wp_int", [P, 2, D], bf16)
        wqT = sb("wqT", [P, KC, D])
        wpT = sb("wpT", [P, KC, D], bf16)
        bqk = sb("bqk", [P, 4])
        bvp = sb("bvp", [P, 2, D])
        gates = sb("gates", [P, 2])
        tg = sb("tg", [P, 2])
        rowmax = sb("rowmax", [P, 2, HEADS])
        negmax = sb("negmax", [P, 2, 2 * HEADS], bf16)
        negmaxT = [sb(f"negmaxT{i}", [P, TOK], bf16) for i in range(2)]
        pick = sb("pick", [P, HEADS, P], bf16)
        rden = sb("rden", [P, 2, HEADS])
        ident = sb("ident", [P, P])
        identb = sb("identb", [P, P], bf16)
        before = sb("before", [P, P])
        beforeb = sb("beforeb", [P, P], bf16)
        onesb = sb("onesb", [P, P], bf16)
        onesf = sb("onesf", [P, P])
        slotc = sb("slotc", [P, 2 + EXPERTS])
        tokv = xn[:, 0:4].rearrange("p b h -> p (b h)").rearrange("p (i t) -> p i t", i=2)
        zeros = sb("zeros", [P, 2 * ROW])
        stat = sb("stat", [P, TILES, 6])
        mv = sb("mv", [P, TILES, 2])
        veps = sb("veps", [P, TILES])
        neghalf = sb("neghalf", [P, TILES])
        rstd = sb("rstd", [P, TILES])
        nmr = sb("nmr", [P, TILES])
        amax = sb("amax", [P, TILES])
        qsc = sb("qsc", [P, TILES])
        qrs = sb("qrs", [P, TILES])
        oamax = sb("oamax", [P, TILES])
        osc = sb("osc", [P, TILES])
        ors = sb("ors", [P, TILES])
        wamax = sb("wamax", [P, 4])
        wsc = sb("wsc", [P, 4])
        wrs = sb("wrs", [P, 4])
        wdiag = sb("wdiag", [P, 2, P])
        wscale = sb("wscale", [P, D])
        oq = sb("oq", [P, TILES, D], bf16)
        oT = [sb(f"oT{i}", [P, KC, P], bf16) for i in range(2)]
        rows = sb("rows", [P, TILES, ROW])
        gateT = sb("gateT", [P, KC, EXPERTS])
        lmax = sb("lmax", [P, TILES])
        total = sb("total", [P, TILES])
        rtotal = sb("rtotal", [P, TILES])
        gbest = sb("gbest", [P, TILES, GROUPS + 8 - TOPG])
        gtop = sb("gtop", [P, TILES, 8])
        g8 = sb("g8", [P, TILES, 8])
        e8 = sb("e8", [P, TILES, 8])
        gout = sb("gout", [P, TILES, GROUPS + 8 - TOPG])
        gcap = sb("gcap", [P, TILES, GROUPS])
        cand = sb("cand", [P, TILES, EXPERTS + 8 - TOPK])
        etop = sb("etop", [P, TILES, 8])
        sel = sb("sel", [P, TILES, EXPERTS], bf16)
        last = sb("last", [P, 4])
        order = sb("order", [2 * EXPERTS, CAP])
        reverse = sb("reverse", [CAP, CAP])
        slotv = sb("slotv", [CAP, 2, EXPERTS])
        empty = sb("empty", [CAP, EXPERTS])
        gidx = sb("gidx", [CAP, EXPERTS], u32)
        sidx = sb("sidx", [CAP, EXPERTS], u32)
        sgu = sb("sgu", [P, KC, 2, MS])
        sdn = sb("sdn", [P, 3, D])
        gcol = [sb(f"gcol{i}", [CAP, 1], u32) for i in range(GBUF)]
        scol = [sb(f"scol{i}", [CAP, 1], u32) for i in range(OBUF)]
        gw = [sb(f"gw{i}", [CAP, 1]) for i in range(2)]
        bank = [ctx.enter_context(nc.psum_tensor(f"bank{i}", [P, 512], f32)) for i in range(8)]

        got_x, got_x2, got_w, got_w2, got_ctx, got_ctx2, got_kv, got_small, got_const, got_gate, got_tokv, got_shared, got_reverse = [
            sem(n) for n in ("got_x", "got_x2", "got_w", "got_w2", "got_ctx", "got_ctx2", "got_kv", "got_small", "got_const", "got_gate",
                             "got_tokv", "got_shared", "got_reverse")]
        got_expert = [sem(f"got_expert{r}") for r in range(RING)]
        got_rows = [sem(f"got_rows{i}") for i in range(GBUF)]
        parts_out = [sem(f"parts_out{i}") for i in range(UNIT_BUF)]
        got_stack = [sem(f"got_stack{j}") for j in range(TILES // 2)]
        stack_ready = sem("stack_ready")
        table_out = sem("table_out")
        acc_in = [sem(f"acc_in{i}") for i in range(2)]
        got_last = sem("got_last")
        got_acc = [sem(f"got_acc{i}") for i in range(4)]
        stored = sem("stored")
        pool_set, dve_chain, act_chain, pool_chain = sem("pool_set"), sem("dve_chain"), sem("act_chain"), sem("pool_chain")
        tanh_done, tbp_done, xp_done = sem("tanh_done"), sem("tbp_done"), sem("xp_done")
        consts_b = sem("consts_b")
        mv_done, bn_done, bn2_done, veps_done, rstd_done, nmr_done, xn_done = [
            sem(n) for n in ("mv_done", "bn_done", "bn2_done", "veps_done", "rstd_done", "nmr_done", "xn_done")]
        xq_done, xqT_psum, xqT_done = sem("xq_done"), sem("xqT_psum"), sem("xqT_done")
        w_done, w_psum, wT_done = sem("w_done"), sem("w_psum"), sem("wT_done")
        unit_psum, unit_high, unit_rest, unit_mid, unit_lo = [
            sem(n) for n in ("unit_psum", "unit_high", "unit_rest", "unit_mid", "unit_lo")]
        v_psum, v_done = sem("v_psum"), sem("v_done")
        vpad_zero, vpad_done, headsT_done, heads_psum = sem("vpad_zero"), sem("vpad_done"), sem("headsT_done"), sem("heads_psum")
        s_psum, max_done, split_done, nm_psum, nm_done, st_psum, exp_done, pv_psum, norm_done, oq_done, att_chain, ors_done, round_done = [
            sem(n) for n in ("s_psum", "max_done", "split_done", "nm_psum", "nm_done", "st_psum", "exp_done",
                             "pv_psum", "norm_done", "oq_done", "att_chain", "ors_done", "round_done")]
        oT_psum, oT_done, y_psum, y1_done, x2_done = [
            sem(n) for n in ("oT_psum", "oT_done", "y_psum", "y1_done", "x2_done")]
        h_done, hT_psum, hT_done, logit_psum, shift_done, pexp_done = [
            sem(n) for n in ("h_done", "hT_psum", "hT_done", "logit_psum", "shift_done", "pexp_done")]
        wrow_done, sel_done, selT_psum, key_done, pos_psum, over_done, overT_psum, overT_done = [
            sem(n) for n in ("wrow_done", "sel_done", "selT_psum", "key_done", "pos_psum", "over_done",
                             "overT_psum", "overT_done")]
        selS_done, key_made = sem("selS_done"), sem("key_made")
        slotc_done, lists_done, lists_psum = sem("slotc_done"), sem("lists_done"), sem("lists_psum")
        order_done, slot_psum, idx_done = sem("order_done"), sem("slot_psum"), sem("idx_done")
        sup_done = sem("sup_done")
        sg_psum, sgate_done, sact_done, sd_psum, base_done = [
            sem(n) for n in ("sg_psum", "sgate_done", "sact_done", "sd_psum", "base_done")]
        gT_psum, gxT_done, up_psum, silu_done, hid_done, down_psum, gw_done, orow_done, gcol_done, scol_done = [
            sem(n) for n in ("gT_psum", "gxT_done", "up_psum", "silu_done", "hid_done", "down_psum", "gw_done",
                             "orow_done", "gcol_done", "scol_done")]
        last_done, corr_psum, sum_done, y_done = [sem(n) for n in ("last_done", "corr_psum", "sum_done", "y_done")]

        FILL = [2 * 16, 2 * 16]
        units = [("k", 0, 0), ("k", 1, 0), ("k", 0, 1), ("q", 0, 0), ("q", 1, 0), ("k", 1, 1), ("q", 0, 1), ("q", 1, 1)]
        token_rows = lambda t, n: t.rearrange("(a p) h -> p a h", p=P)[:, n]
        block = ctx.enter_context(nc.Block())

        @block.sync
        def _(sp):
            sp.dma_start(x[:, 0:4], a["x"][:, 0:4]).then_inc(got_x, 16)
            sp.dma_start(x[:, 4:8], a["x"][:, 4:8]).then_inc(got_x2, 16)
            sp.dma_start(w_rows[:, 0:2], a["w_rows"][:, 0:2]).then_inc(got_w, 16)
            sp.dma_start(wkv[:, :, 0:D], a["wkv"][:, :, 0:D]).then_inc(got_kv, 16)
            sp.dma_start(ctxT[:, :, 0:512], a["ctxT"][:, :, 0:512]).then_inc(got_ctx, 16)
            sp.dma_start(ctxT[:, :, 512:T], a["ctxT"][:, :, 512:T]).then_inc(got_ctx2, 16)
            sp.dma_start(w_rows[:, 2:4], a["w_rows"][:, 2:4]).then_inc(got_w2, 16)
            sp.dma_start(wkv[:, :, D:2 * D], a["wkv"][:, :, D:2 * D]).then_inc(got_w2, 16)
            sp.dma_start(gateT[:], a["gateT"]).then_inc(got_gate, 16)
            sp.dma_start(reverse[:], a["reverse"]).then_inc(got_reverse, 16)
            sp.wait_ge(pool_set, 1)
            sp.dma_start(table[T:ROWS].rearrange("(p a) h -> p (a h)", p=P), zeros[:]).then_inc(table_out, 16)
            def parts_to_dram(u):
                what, c, s = units[u]
                dst = k_parts if what == "k" else q_parts
                sp.wait_ge(unit_lo, u + 1)
                sp.dma_start(dst[:, P * c:P * c + P, 512 * s:512 * s + 512].rearrange("r p t -> p r t"),
                             part[u % UNIT_BUF]).then_inc(parts_out[u % UNIT_BUF], 16)

            def stack(what, j):
                for u, (w, _, half) in enumerate(units):
                    if w == what and half == j // 2:
                        sp.wait_ge(parts_out[u % UNIT_BUF], 16 * (u // UNIT_BUF + 1))
                dst, src, order_of = (ks, k_parts, K_PART) if what == "k" else (qs, q_parts, Q_PART)
                for r, p in enumerate(order_of):
                    sp.dma_start(dst[DH * r:DH * r + DH].rearrange("d (h t) -> d h t", h=HEADS)[:, :, 256 * j:256 * j + 256],
                                 src[p].rearrange("(h d) t -> d h t", d=DH)[:, :, 256 * j:256 * j + 256]).then_inc(got_stack[j], 16)

            for step in (0, 1, ("k", 0), 3, 4, 2, ("q", 0), 5, ("k", 1), ("q", 1), 6, 7, ("k", 2), ("q", 2), ("k", 3), ("q", 3)):
                if isinstance(step, int):
                    parts_to_dram(step)
                else:
                    stack(*step)
            sp.dma_start(sgu[:], a["sgu"]).then_inc(got_shared, 16)
            sp.dma_start(sdn[:, 0:2], a["sdn"][0:2 * P].rearrange("(c p) h -> p c h", p=P)).then_inc(got_shared, 16)
            sp.dma_start(sdn[0:SCH[2][1], 2], a["sdn"][2 * P:MS]).then_inc(got_shared, 16)
            sp.wait_ge(oq_done, TILES)
            sp.dma_start(tokv, a["tokv"]).then_inc(got_tokv, 16)
            sp.wait_ge(pv_psum, TILES + 2)
            for r in range(RING):
                sp.dma_start(wgu[r], a["wgu"][r]).then_inc(got_expert[r], 16)
                sp.dma_start(wdn[r][:, 0], a["wdn"][r, 0:P]).then_inc(got_expert[r], 16)
                sp.dma_start(wdn[r][0:MR, 1], a["wdn"][r, P:M]).then_inc(got_expert[r], 16)
            for b in range(0, TILES, 2):
                sp.wait_ge(wrow_done, 1 + b // 4)
                for n in (b, b + 1):
                    sp.dma_start(table[P * n:P * n + P], rows[:, n]).then_inc(table_out, 16)
            with sp.Fori(0, EXPERTS // RING - 1) as lap:
                for r in range(RING):
                    sp.wait_ge(down_psum, lap * RING + r + 3)
                    sp.nop(nofuse=True)
                    e = bass.ds(lap * RING + RING + r, 1)
                    sp.dma_start(wgu[r], a["wgu"][e].squeeze(0)).then_inc(got_expert[r], 16)
                    sp.dma_start(wdn[r][:, 0], a["wdn"][e, 0:P].squeeze(0)).then_inc(got_expert[r], 16)
                    sp.dma_start(wdn[r][0:MR, 1], a["wdn"][e, P:M].squeeze(0)).then_inc(got_expert[r], 16)
            for i in range(2):
                sp.wait_ge(acc_in[i], FILL[i] + 16 * EXPERTS // 2)
            for i in range(2):
                sp.dma_start(lastrow[:, i], acc[i][LASTROW:LASTROW + EXPERTS]).then_inc(got_last, 16)
            for j in range(4):
                for i, t in enumerate((xn, xq)):
                    sp.dma_start(t[:, 2 * j:2 * j + 2], token_rows(acc[i][0:T], slice(2 * j, 2 * j + 2))).then_inc(got_acc[j], 16)
            for j in range(4):
                sp.wait_ge(y_done, j + 1)
                sp.dma_start(out[2 * j:2 * j + 2].rearrange("b p h -> p b h"), xn[:, 2 * j:2 * j + 2]).then_inc(stored, 16)
            sp.wait_ge(stored, 64)

        @block.gpsimd
        def _(pool):
            g = nc.gpsimd
            g.memset(zeros[:], 0.0).then_inc(pool_set, 1)
            g.memset(neghalf[:], -0.5).then_inc(pool_set, 1)
            g.memset(onesb[:], 1.0).then_inc(pool_set, 1)
            g.memset(onesf[:], 1.0).then_inc(pool_set, 1)
            for i in range(2):
                g.memset(negmaxT[i][:], 0.0).then_inc(pool_set, 1)
            g.memset(gbest[:], MARK).then_inc(pool_set, 1)
            g.memset(gtop[:], MARK).then_inc(pool_set, 1)
            g.memset(cand[:], MARK).then_inc(pool_set, 1)
            g.memset(etop[:], MARK).then_inc(pool_set, 1)
            pool.wait_ge(veps_done, 1)
            pool.wait_ge(pool_set, 2)
            g.tensor_tensor(rstd[:], veps[:], neghalf[:], ALU.pow).then_inc(rstd_done, 1)
            pool.wait_ge(got_const, 48)
            g.tensor_copy(identb[:], ident[:]).then_inc(consts_b, 1)
            g.tensor_copy(beforeb[:], before[:]).then_inc(consts_b, 1)
            g.tensor_tensor(pick[:], ident[:, 0:HEADS].unsqueeze(2).broadcast_to([P, HEADS, P]),
                            ident[:, HEADS:2 * HEADS].unsqueeze(2).broadcast_to([P, HEADS, P]), ALU.add).then_inc(consts_b, 1)
            pool.wait_ge(tbp_done, 1)
            for b in range(TILES):
                pool.wait_ge(xn_done, b + 1)
                g.tensor_tensor(x[:, b], x[:, b], bvp[:, 1], ALU.add).then_inc(xp_done, 1)

            def stationary_values(b, u):
                pool.wait_ge(v_done, b + 1)
                pool.wait_ge(pv_psum, b + 1)
                g.tensor_copy(vpad[u].rearrange("p (h e) -> p h e", h=HEADS)[:, :, 0:DH],
                              values[:, bass.ds(b * D, D)].rearrange("p (h d) -> p h d", h=HEADS)).then_inc(vpad_done, 1)

            def stacks(j):
                pool.wait_ge(got_stack[j], 2 * len(Q_PART) * 16)
                pool.sem_inc(stack_ready, 1)

            def residual(m):
                pool.wait_ge(y1_done, m + 2)
                g.tensor_tensor(x[:, m], xq[:, m], x[:, m], ALU.add).then_inc(x2_done, 1)

            def heads_to_int(b):
                pool.wait_ge(ors_done, b + 1)
                g.tensor_scalar(xn[:, b], xq[:, b], ors[:, b:b + 1], ROUND, ALU.mult, ALU.add).then_inc(round_done, 1)
                pool.wait_ge(round_done, b + 1)
                g.tensor_scalar(oq[:, b], xn[:, b], ROUND, None, ALU.subtract).then_inc(oq_done, 1)

            def norm2_rstd(i):
                n = slice(*NORM2[i])
                pool.wait_ge(veps_done, 2 + i)
                g.tensor_tensor(rstd[:, n], veps[:, n], neghalf[:, n], ALU.pow).then_inc(rstd_done, 1)

            pool.wait_ge(unit_psum, len(units))
            for i in range(2):
                g.memset(vpad[i], 0.0).then_inc(vpad_zero, 1)
            pool.wait_ge(vpad_zero, 2)
            for i in range(2):
                g.memset(vpad[i].rearrange("p (h e) -> p h e", h=HEADS)[:, :, DH:DH + 1], 1.0).then_inc(vpad_zero, 1)
            stacks(0)
            pool.wait_ge(vpad_zero, 4)
            pool.wait_ge(xp_done, TILES)
            stationary_values(0, 0)
            stationary_values(1, 1)
            stacks(1)
            stationary_values(2, 0)
            for b in range(1, TILES):
                if b == 6:
                    norm2_rstd(0)
                heads_to_int(b - 1)
                if b >= 2:
                    residual(b - 2)
                if b in (1, 3):
                    stacks((b + 3) // 2)
                if b + 2 < TILES:
                    stationary_values(b + 2, b % 2)
            pool.wait_ge(pool_set, 1)
            g.dma_start(acc[0][0:T].rearrange("(p a) h -> p a h", p=P),
                        zeros[:, 0:D].unsqueeze(1).broadcast_to([P, TILES, D])).then_inc(acc_in[0], 16)
            for i in range(2):
                g.dma_start(acc[i][T:ROWS].rearrange("(p a) h -> p (a h)", p=P), zeros[:, 0:2 * D]).then_inc(acc_in[i], 16)
            residual(TILES - 2)
            norm2_rstd(1)
            residual(TILES - 1)
            norm2_rstd(2)
            def shared_hidden(u):
                h, c = u // 3, u % 3
                n = SCH[c][1]
                pool.wait_ge(sgate_done, u + 1)
                pool.wait_ge(sup_done, u + 1)
                g.tensor_tensor(sact[0:n, c * T + 512 * h:c * T + 512 * h + 512], sgate[u % 2][0:n], sup[u % 2][0:n], ALU.mult).then_inc(sact_done, 1)

            for u in range(3):
                shared_hidden(u)
            for i, t in enumerate((first, once)):
                g.tensor_tensor(t, ident[0:CAP, 0:CAP], slotc[0:CAP, i:i + 1].broadcast_to([CAP, CAP]), ALU.mult).then_inc(slotc_done, 1)
            pool.wait_ge(got_tokv, 16)
            pool.wait_ge(selS_done, 1)
            g.tensor_tensor(key2, key2, tokv[:, 1], ALU.mult).then_inc(key_done, 1)
            for u in range(3, 6):
                shared_hidden(u)

            def gather(i):
                g.indirect_dma_start(gx[i], None, table, bass.IndirectOffsetOnAxis(gcol[i][:], 0)).then_inc(got_rows[i], 16)

            pool.wait_ge(table_out, 16 * (TILES + 1))
            for e in range(GBUF):
                pool.wait_ge(gcol_done, e + 1)
                gather(e)
                if e == 4:
                    pool.wait_ge(base_done, TILES)
                    pool.wait_ge(acc_in[1], 16)
                    g.dma_start(token_rows(acc[1][0:T], slice(0, TILES)), x[:]).then_inc(acc_in[1], 16)

            def expert(e, half, r, more):
                pool.wait_ge(scol_done, e + 1)
                pool.wait_ge(orow_done, e + 3)
                pool.wait_ge(acc_in[r % 2], FILL[r % 2] + 16 * half)
                pool.nop(nofuse=True)
                g.indirect_dma_start(acc[r % 2], bass.IndirectOffsetOnAxis(scol[r % OBUF][:], 0), orow[r % OBUF], None,
                                     compute_op=ALU.add).then_inc(acc_in[r % 2], 16)
                if more:
                    pool.wait_ge(gcol_done, e + GBUF + 1)
                    pool.nop(nofuse=True)
                    gather(r % GBUF)

            with pool.Fori(0, EXPERTS // RING - 1) as lap:
                for r in range(RING):
                    expert(lap * RING + r, lap * (RING // 2) + r // 2, r, True)
            for r in range(RING):
                e = EXPERTS - RING + r
                expert(e, e // 2, r, e + GBUF < EXPERTS)

        @block.scalar
        def _(act):
            s = nc.scalar
            act.dma_start(bqk[:], a["bqk"]).then_inc(got_small, 16)
            act.dma_start(gates[:], a["gates"].broadcast_to([P, 2])).then_inc(got_small, 16)
            for i, t in enumerate((ident, before)):
                act.dma_start(t[:], a["consts"][:, P * i:P * i + P]).then_inc(got_const, 16)
            act.dma_start(slotc[:], a["consts"][:, 2 * P:]).then_inc(got_const, 16)
            for i in range(2):
                act.dma_start(bvp[:, i], a["bvp"][i:i + 1].broadcast_to([P, D])).then_inc(got_small, 16)
            act.sem_inc(exp_done, 2)
            act.sem_inc(headsT_done, 1)
            act.sem_inc(orow_done, 2)

            def high_of(u):
                what, c, _ = units[u]
                col = c if what == "q" else KC + c
                act.wait_ge(unit_psum, u + 1)
                if u >= UNIT_BUF:
                    act.wait_ge(parts_out[u % UNIT_BUF], 16)
                s.activation(part[u % UNIT_BUF][:, 0], bank[u % UNIT_BUF][:], ACT.Identity, bias=bqk[:, col:col + 1]).then_inc(unit_high, 1)

            def middle_of(u):
                act.wait_ge(unit_rest, u + 1)
                s.activation(part[u % UNIT_BUF][:, 1], rest[u % 2], ACT.Copy).then_inc(unit_mid, 1)

            def normalise(b):
                s.activation(xn[:, b], x[:, b], ACT.Identity, bias=nmr[:, b:b + 1], scale=rstd[:, b:b + 1]).then_inc(xn_done, 1)

            def xq_across(j):
                act.wait_ge(xqT_psum, j + 1)
                s.activation(xqT[:, :, 256 * j:256 * j + 256], bank[6 + j % 2][:].rearrange("p (k t) -> p k t", k=KC), ACT.Copy).then_inc(xqT_done, 1)

            act.wait_ge(nmr_done, 1)
            for b in range(4):
                normalise(b)
            act.wait_ge(got_small, 64)
            high_of(0)
            for b in range(4, 8):
                normalise(b)
            high_of(1)
            act.wait_ge(w_psum, 1)
            s.activation(wqT[:].rearrange("p k (c o) -> p c k o", c=2), bank[4][:].rearrange("p (c k o) -> p c k o", c=2, k=KC), ACT.Copy).then_inc(wT_done, 1)
            xq_across(0)
            xq_across(1)
            s.activation(tg[:], gates[:], ACT.Tanh).then_inc(tanh_done, 1)
            middle_of(0)
            middle_of(1)
            high_of(2)
            high_of(3)
            xq_across(2)
            xq_across(3)
            middle_of(2)
            middle_of(3)
            high_of(4)
            middle_of(4)
            high_of(5)
            middle_of(5)
            high_of(6)
            middle_of(6)
            high_of(7)
            middle_of(7)
            act.wait_ge(w_psum, 2)
            s.activation(wpT[:].rearrange("p k (c o) -> p c k o", c=2), bank[5][:, 0:256].bitcast(bf16).rearrange("p (c k o) -> p c k o", c=2, k=KC), ACT.Copy).then_inc(wT_done, 1)

            def negmax_across(b, u):
                act.wait_ge(nm_psum, b + 1)
                s.activation(negmaxT[u][0:2 * HEADS], bank[7][0:2 * HEADS, 0:TOK // 2].bitcast(bf16), ACT.Copy).then_inc(nm_done, 1)

            def heads_out(b, u):
                act.wait_ge(pv_psum, b + 3)
                act.wait_ge(heads_psum, b + 1)
                s.activation(headsT[u], bank[4][:], ACT.Copy).then_inc(headsT_done, 1)

            def heads_row(m, u):
                act.wait_ge(oT_psum, m + 1)
                s.activation(oT[u][:], bank[5][:, 0:TOK].bitcast(bf16).rearrange("p (k t) -> p k t", k=KC), ACT.Copy).then_inc(oT_done, 1)

            def second_norm(b):
                s.activation(rows[:, b, 0:D], x[:, b], ACT.Identity, bias=nmr[:, b:b + 1], scale=rstd[:, b:b + 1]).then_inc(h_done, 1)

            def h_across(j):
                act.wait_ge(hT_psum, j + 1)
                s.activation(hT[:, :, 256 * j:256 * j + 256], bank[H_BANK[j]][:].rearrange("p (k t) -> p k t", k=KC), ACT.Copy).then_inc(hT_done, 1)

            def silu_gate(u):
                act.wait_ge(sg_psum, u + 1)
                if u >= 2:
                    act.wait_ge(sact_done, u - 1)
                n = SCH[u % 3][1]
                s.activation(sgate[u % 2][0:n], bank[2 * (u % 2)][0:n], ACT.Silu).then_inc(sgate_done, 1)
                s.activation(sup[u % 2][0:n], bank[2 * (u % 2) + 1][0:n], ACT.Copy).then_inc(sup_done, 1)

            def attend(b, u, more, merge):
                for g in range(4):
                    act.wait_ge(st_psum, 4 * b + g + 1)
                    if g == 0:
                        act.wait_ge(pv_psum, b + 1)
                    s.activation(probs[u][:, 512 * g:512 * g + 512], bank[2 + g % 2][:], ACT.Exp, scale=SCALE).then_inc(exp_done, 1)
                    if merge and g == 0:
                        heads_row(b - 2, u)
                    if not more:
                        if g == 0:
                            act.wait_ge(nmr_done, 2)
                        second_norm(g)
                if more:
                    negmax_across(b + 1, 1 - u)
                heads_out(b, u)

            act.wait_ge(pool_set, 6)
            negmax_across(0, 0)
            for b in range(TILES):
                attend(b, b % 2, b + 1 < TILES, b >= 2)
            heads_row(TILES - 2, 0)
            h_across(0)
            h_across(1)
            heads_row(TILES - 1, 1)

            def exponentials(half):
                act.wait_ge(shift_done, half + 1)
                for b in range(4 * half, 4 * half + 4):
                    s.activation(pexp[:, b], logit[:, b], ACT.Exp, accum_out=total[:, b:b + 1]).then_inc(pexp_done, 1)

            act.wait_ge(nmr_done, 3)
            for b in range(4, 7):
                second_norm(b)
            exponentials(0)
            h_across(2)
            act.wait_ge(nmr_done, 4)
            second_norm(7)
            h_across(3)
            exponentials(1)
            silu_gate(0)
            silu_gate(1)
            act.wait_ge(selT_psum, 1)
            act.wait_ge(key_made, 1)
            s.activation(key2, bank[4][:, 0:HALF // 2].bitcast(bf16), ACT.Copy).then_inc(selS_done, 1)
            silu_gate(2)
            silu_gate(3)
            silu_gate(4)
            for j in range(2):
                act.wait_ge(overT_psum, j + 1)
                s.activation(overT[:, 512 * j:512 * j + 512], bank[7][0:EXPERTS], ACT.Copy).then_inc(overT_done, 1)
            silu_gate(5)

            def silu_of(e, p):
                act.wait_ge(up_psum, e + 3)
                act.wait_ge(hid_done, 2 * e + 2)
                act.nop(nofuse=True)
                s.activation(silu[p][:, 0], bank[2 + p][:, 0:CAP], ACT.Silu).then_inc(silu_done, 1)
                s.activation(silu[p][0:MR, 1], bank[2 + p][GATE_AT:GATE_AT + MR, 2 * CAP:3 * CAP], ACT.Silu).then_inc(silu_done, 1)

            def weighted_rows(e, half, r):
                p = r % 2
                act.wait_ge(down_psum, e + 3)
                act.wait_ge(gw_done, e + 1)
                act.wait_ge(acc_in[p], FILL[p] + 16 * half - 16)
                act.nop(nofuse=True)
                s.activation(orow[r % OBUF], bank[4 + p][0:CAP, 0:D], ACT.Copy, scale=gw[p][:]).then_inc(orow_done, 1)

            silu_of(0, 0)
            with act.Fori(0, EXPERTS // RING - 1) as lap:
                for r in range(RING):
                    silu_of(lap * RING + (r + 1), (r + 1) % 2)
                    weighted_rows(lap * RING + r, lap * (RING // 2) + r // 2, r)
            for r in range(RING):
                e = EXPERTS - RING + r
                if e + 1 < EXPERTS:
                    silu_of(e + 1, (r + 1) % 2)
                weighted_rows(e, e // 2, r)

        @block.vector
        def _(dve):
            v = nc.vector
            dve.sem_inc(norm_done, 1)
            dve.sem_inc(y1_done, 1)
            dve.sem_inc(gxT_done, 2)
            dve.sem_inc(hid_done, 4)
            chain = [0]

            def link(ins):
                chain[0] += 1
                ins.then_inc(dve_chain, 1)
                dve.wait_ge(dve_chain, chain[0])

            def rest_of(u):
                what, c, _ = units[u]
                col = c if what == "q" else KC + c
                dve.wait_ge(unit_high, u + 1)
                if u >= 2:
                    dve.wait_ge(unit_mid, u - 1)
                    dve.wait_ge(unit_lo, u - 1)
                v.scalar_tensor_tensor(out=rest[u % 2], in0=bank[u % UNIT_BUF][:], scalar=bqk[:, col:col + 1], in1=part[u % UNIT_BUF][:, 0],
                                       op0=ALU.add, op1=ALU.subtract).then_inc(unit_rest, 1)

            def low_of(u):
                dve.wait_ge(unit_mid, u + 1)
                v.tensor_tensor(part[u % UNIT_BUF][:, 2], rest[u % 2], part[u % UNIT_BUF][:, 1], ALU.subtract).then_inc(unit_lo, 1)

            def stats(b, done):
                v.bn_stats(stat[:, b], x[:, b]).then_inc(done, 1)

            def norm_scalars(done, base, meanwhile=lambda: None):
                for b in range(TILES):
                    dve.wait_ge(done, b + 1)
                    i = v.bn_aggr(mv[:, b], stat[:, b])
                link(i)
                v.tensor_scalar(veps[:], mv[:, :, 1], EPS, None, ALU.add).then_inc(veps_done, 1)
                meanwhile()
                dve.wait_ge(rstd_done, base)
                v.scalar_tensor_tensor(out=nmr[:], in0=mv[:, :, 0], scalar=-1.0, in1=rstd[:], op0=ALU.mult, op1=ALU.mult).then_inc(nmr_done, 1)

            def fix_weights(i):
                link(v.tensor_reduce(wamax[:, i:i + 2], w_rows[:, i:i + 2], AX.X, ALU.max, apply_absolute_value=True))
                link(v.tensor_scalar(wsc[:, i:i + 2], wamax[:, i:i + 2], 1.0 / 127.0, 1e-8, ALU.mult, ALU.max))
                link(v.reciprocal(wrs[:, i:i + 2], wsc[:, i:i + 2]))
                for j in (i, i + 1):
                    last = v.tensor_scalar(w_fix[:, j], w_rows[:, j], wrs[:, j:j + 1], ROUND, ALU.mult, ALU.add)
                link(last)

            def wq_fixed():
                dve.wait_ge(got_w, 16)
                fix_weights(0)
                for i in range(2):
                    v.tensor_scalar(w_rows[:, i], w_fix[:, i], ROUND, wsc[:, i:i + 1], ALU.subtract, ALU.mult).then_inc(w_done, 1)

            def token_scales(half):
                tiles = range(4 * half, 4 * half + 4)
                four = slice(4 * half, 4 * half + 4)
                for b in tiles:
                    dve.wait_ge(xn_done, b + 1)
                    i = v.tensor_reduce(amax[:, b:b + 1], xn[:, b], AX.X, ALU.max, apply_absolute_value=True)
                link(i)
                link(v.tensor_scalar(qsc[:, four], amax[:, four], 1.0 / 127.0, 1e-8, ALU.mult, ALU.max))
                link(v.reciprocal(qrs[:, four], qsc[:, four]))

            def quantise(half):
                for b in range(4 * half, 4 * half + 4):
                    i = v.tensor_scalar(xn[:, b], xn[:, b], qrs[:, b:b + 1], ROUND, ALU.mult, ALU.add)
                    if b % 2:
                        link(i)
                        for n in (b - 1, b):
                            v.tensor_scalar(xq[:, n], xn[:, n], ROUND, qsc[:, n:n + 1], ALU.subtract, ALU.mult).then_inc(xq_done, 1)

            dve.wait_ge(got_x, 16)
            for b in range(4):
                stats(b, bn_done)
            dve.wait_ge(got_x2, 16)
            for b in range(4, TILES):
                stats(b, bn_done)
            norm_scalars(bn_done, 1, wq_fixed)
            def values_of(j):
                dve.wait_ge(v_psum, j + 1)
                for b in (2 * j, 2 * j + 1):
                    v.tensor_tensor(values[:, D * b:D * b + D], bank[V_BANK[j]][:, D * (b % 2):D * (b % 2) + D], bvp[:, 0], ALU.add).then_inc(v_done, 1)

            token_scales(0)
            quantise(0)
            dve.wait_ge(got_small, 64)
            rest_of(0)
            rest_of(1)
            token_scales(1)
            low_of(0)
            low_of(1)
            quantise(1)
            dve.wait_ge(tanh_done, 1)
            v.tensor_scalar(bvp[:, 1], bvp[:, 1], tg[:, 0:1], None, ALU.mult).then_inc(tbp_done, 1)
            rest_of(2)
            rest_of(3)
            low_of(2)
            rest_of(4)
            low_of(3)
            low_of(4)
            dve.wait_ge(got_w2, 32)
            fix_weights(2)
            dve.wait_ge(got_const, 48)
            for i in range(2):
                v.tensor_scalar(wp_int[:, i], w_fix[:, 2 + i], ROUND, None, ALU.subtract).then_inc(w_done, 1)
                v.tensor_scalar(wdiag[:, i], ident[:], wsc[:, 2 + i:3 + i], None, ALU.mult).then_inc(w_done, 1)
            values_of(0)
            rest_of(5)
            low_of(5)
            values_of(1)
            rest_of(6)
            low_of(6)
            values_of(2)
            rest_of(7)
            values_of(3)
            low_of(7)

            def maximum(b, u, g):
                dve.wait_ge(s_psum, 4 * b + g + 1)
                v.tensor_reduce(rowmax[:, u, 4 * g:4 * g + 4], bank[g % 2][:].rearrange("p (h m) -> p h m", h=4), AX.X, ALU.max).then_inc(max_done, 1)

            def split_max(b, u):
                dve.wait_ge(max_done, 4 * b + 4)
                v.tensor_scalar(negmax[:, u, 0:HEADS], rowmax[:, u], -1.0, None, ALU.mult).then_inc(split_done, 1)
                dve.wait_ge(split_done, 2 * b + 1)
                v.scalar_tensor_tensor(out=negmax[:, u, HEADS:2 * HEADS], in0=rowmax[:, u], scalar=-1.0, in1=negmax[:, u, 0:HEADS],
                                       op0=ALU.mult, op1=ALU.subtract).then_inc(split_done, 1)

            heads_out = bank[6][:].rearrange("p (h e) -> p h e", e=VW)
            xq_flat = xq[:].rearrange("p b h -> p (b h)")
            STEPS = 3

            def heads_normalised(b, u):
                dve.wait_ge(heads_psum, b + 3)
                v.reciprocal(rden[:, u], heads_out[:, :, DH]).then_inc(att_chain, 1)
                dve.wait_ge(att_chain, STEPS * b + 1)
                v.tensor_tensor(xq_flat[:, bass.ds(b * D, D)].rearrange("p (h d) -> p h d", h=HEADS), heads_out[:, :, 0:DH],
                                rden[:, u].unsqueeze(2).broadcast_to([P, HEADS, DH]), ALU.mult).then_inc(norm_done, 1)

            def heads_scale(b):
                one = bass.ds(b, 1)
                dve.wait_ge(norm_done, b + 2)
                v.tensor_reduce(oamax[:, one], xq_flat[:, bass.ds(b * D, D)], AX.X, ALU.max, apply_absolute_value=True).then_inc(att_chain, 1)
                dve.wait_ge(att_chain, STEPS * b + 2)
                v.tensor_scalar(osc[:, one], oamax[:, one], 1.0 / 127.0, 1e-8, ALU.mult, ALU.max).then_inc(att_chain, 1)

            def heads_rscale(b):
                one = bass.ds(b, 1)
                dve.wait_ge(att_chain, STEPS * b + 3)
                v.reciprocal(ors[:, one], osc[:, one]).then_inc(ors_done, 1)

            x_flat = x[:].rearrange("p b h -> p (b h)")
            stat_flat = stat[:].rearrange("p b i -> p (b i)")

            def project(m):
                dve.wait_ge(y_psum, m + 1)
                v.scalar_tensor_tensor(out=xq_flat[:, bass.ds(m * D, D)], in0=bank[5][:, D:2 * D], scalar=osc[:, bass.ds(m, 1)],
                                       in1=wscale[:], op0=ALU.mult, op1=ALU.mult).then_inc(y1_done, 1)

            def stats2(m):
                dve.wait_ge(x2_done, m + 1)
                v.bn_stats(stat_flat[:, bass.ds(m * 6, 6)], x_flat[:, bass.ds(m * D, D)]).then_inc(bn2_done, 1)

            def norm2_veps(i):
                n = slice(*NORM2[i])
                for b in range(*NORM2[i]):
                    dve.wait_ge(bn2_done, b + 1)
                    v.bn_aggr(mv[:, b], stat[:, b]).then_inc(mv_done, 1)
                dve.wait_ge(mv_done, NORM2[i][1])
                v.tensor_scalar(veps[:, n], mv[:, n, 1], EPS, None, ALU.add).then_inc(veps_done, 1)

            def norm2_nmr(i):
                n = slice(*NORM2[i])
                dve.wait_ge(rstd_done, 2 + i)
                v.scalar_tensor_tensor(out=nmr[:, n], in0=mv[:, n, 0], scalar=-1.0, in1=rstd[:, n], op0=ALU.mult, op1=ALU.mult).then_inc(nmr_done, 1)

            def four(half):
                return slice(4 * half, 4 * half + 4)

            def shift_logits(half):
                n = four(half)
                from_bank = bank[LOGIT_BANK[half]][:].rearrange("p (b e) -> p b e", b=TILES)[:, n]
                dve.wait_ge(logit_psum, 2 * half + 2)
                link(v.tensor_reduce(lmax[:, n], from_bank, AX.X, ALU.max))
                link(v.tensor_tensor(logit[:, n], from_bank, lmax[:, n].unsqueeze(2).broadcast_to([P, 4, EXPERTS]), ALU.subtract))
                v.tensor_scalar(logit[:, n], logit[:, n], LOWEST, None, ALU.max).then_inc(shift_done, 1)

            def best_groups(half):
                n = four(half)
                dve.wait_ge(shift_done, half + 1)
                link(v.tensor_reduce(gbest[:, n, 0:GROUPS], logit[:, n].rearrange("p b (g e) -> p b g e", g=GROUPS), AX.X, ALU.max))
                for b in range(4 * half, 4 * half + 4):
                    i = v.max(g8[:, b], gbest[:, b, 0:GROUPS])
                link(i)
                link(v.tensor_copy(gtop[:, n, 0:TOPG], g8[:, n, 0:TOPG]))

            def candidates(half):
                n = four(half)
                for b in range(4 * half, 4 * half + 4):
                    i = v.match_replace(gout[:, b], gtop[:, b], gbest[:, b], CHOSEN)
                link(i)
                link(v.tensor_scalar(gcap[:, n], gout[:, n, 0:GROUPS], CHOSEN, LOWEST, ALU.is_lt, ALU.mult))
                link(v.tensor_tensor(cand[:, n, 0:EXPERTS].rearrange("p b (g e) -> p b g e", g=GROUPS), logit[:, n].rearrange("p b (g e) -> p b g e", g=GROUPS),
                                     gcap[:, n].unsqueeze(3).broadcast_to([P, 4, GROUPS, GSIZE]), ALU.min))

            def best_experts(half):
                n = four(half)
                for b in range(4 * half, 4 * half + 4):
                    i = v.max(e8[:, b], cand[:, b, 0:EXPERTS])
                link(i)
                link(v.tensor_copy(etop[:, n, 0:TOPK], e8[:, n, 0:TOPK]))
                for b in range(4 * half, 4 * half + 4):
                    i = v.match_replace(eout[:, b], etop[:, b], cand[:, b], CHOSEN)
                link(i)
                v.tensor_scalar(sel[:, n], eout[:, n, 0:EXPERTS], CHOSEN, None, ALU.is_equal).then_inc(sel_done, 1)

            def weights(half):
                n = four(half)
                dve.wait_ge(pexp_done, 4 * half + 4)
                link(v.reciprocal(rtotal[:, n], total[:, n]))
                link(v.tensor_scalar(rtotal[:, n], rtotal[:, n], tg[:, 1:2], None, ALU.mult))
                link(v.tensor_tensor(pexp[:, n], pexp[:, n], rtotal[:, n].unsqueeze(2).broadcast_to([P, 4, EXPERTS]), ALU.mult))
                v.scalar_tensor_tensor(out=rows[:, n, D:ROW], in0=eout[:, n, 0:EXPERTS], scalar=CHOSEN, in1=pexp[:, n],
                                       op0=ALU.is_equal, op1=ALU.mult).then_inc(wrow_done, 1)

            def attend(b, u, more, before):
                if more:
                    maximum(b + 1, 1 - u, 1)
                if before:
                    heads_normalised(b - 1, 1 - u)
                if more:
                    maximum(b + 1, 1 - u, 2)
                if before:
                    heads_scale(b - 1)
                if before > 1:
                    project(b - 2)
                if before:
                    heads_rscale(b - 1)
                if more:
                    maximum(b + 1, 1 - u, 3)
                    split_max(b + 1, 1 - u)
                if more > 1:
                    maximum(b + 2, u, 0)
                if before > 1:
                    stats2(b - 2)

            for g in range(4):
                maximum(0, 0, g)
            split_max(0, 0)
            dve.wait_ge(w_psum, 3)
            v.tensor_scalar(wscale[:], bank[5][:, 256:512], tg[:, 0:1], None, ALU.mult).then_inc(wT_done, 1)
            maximum(1, 1, 0)
            for b in range(TILES):
                if b == TILES - 2:
                    norm2_veps(0)
                elif b == TILES - 1:
                    norm2_nmr(0)
                attend(b, b % 2, min(2, TILES - 1 - b), min(2, b))
            b = TILES - 1
            heads_normalised(b, 1)
            heads_scale(b)
            heads_rscale(b)
            dve.wait_ge(ors_done, b + 1)
            v.tensor_scalar(xn[:, b], xq[:, b], ors[:, b:b + 1], ROUND, ALU.mult, ALU.add).then_inc(round_done, 1)
            dve.wait_ge(round_done, b + 1)
            v.tensor_scalar(oq[:, b], xn[:, b], ROUND, None, ALU.subtract).then_inc(oq_done, 1)
            dve.wait_ge(pool_set, 10)
            project(TILES - 2)
            stats2(TILES - 2)
            norm2_veps(1)
            project(TILES - 1)
            norm2_nmr(1)
            shift_logits(0)
            stats2(TILES - 1)
            norm2_veps(2)
            best_groups(0)
            norm2_nmr(2)
            candidates(0)
            best_experts(0)
            weights(0)
            shift_logits(1)
            best_groups(1)
            candidates(1)
            best_experts(1)
            weights(1)
            pos_bank = bank[6][:].rearrange("p (b e) -> p b e", b=TILES)
            dve.wait_ge(selT_psum, 1)
            dve.wait_ge(got_tokv, 16)
            v.tensor_tensor(key, bank[4][:, 0:HALF // 2].bitcast(bf16), tokv[:, 0], ALU.mult).then_inc(key_made, 1)
            dve.wait_ge(key_made, 1)

            def round_(r):
                link(v.max(order[:, 8 * r:8 * r + 8], key))
                if 8 * r + 8 < CAP:
                    link(v.match_replace(key, order[:, 8 * r:8 * r + 8], key, 0.0))

            def add_shared(j):
                dve.wait_ge(sd_psum, SD_ORDER.index(j) + 1)
                for b in (2 * j, 2 * j + 1):
                    v.scalar_tensor_tensor(out=x[:, b], in0=bank[SD_BANK[j]][:, D * (b % 2):D * (b % 2) + D], scalar=tg[:, 1:2],
                                           in1=x[:, b], op0=ALU.mult, op1=ALU.add).then_inc(base_done, 1)

            round_(0)
            dve.wait_ge(pos_psum, 1)
            dve.wait_ge(wrow_done, 2)
            v.scalar_tensor_tensor(out=over, in0=pos_bank, scalar=CAP - 1.0, in1=rows[:, :, D:ROW], op0=ALU.is_ge, op1=ALU.mult).then_inc(over_done, 1)
            for r in range(1, CAP // 8):
                round_(r)
                if r == 4:
                    dve.wait_ge(key_done, 1)
                    link(v.tensor_reduce(last[:, 0:1], key2, AX.X, ALU.max))
                    link(v.tensor_scalar(last[:, 1:2], last[:, 0:1], -1.0, T + 1.0, ALU.mult, ALU.add))
                    link(v.scalar_tensor_tensor(out=last[:, 2:3], in0=last[:, 0:1], scalar=0.0, in1=last[:, 1:2], op0=ALU.is_gt, op1=ALU.mult))
            v.tensor_copy(order[:, CAP - 1:CAP], last[:, 2:3]).then_inc(order_done, 1)
            dve.wait_ge(lists_psum, 1)
            v.tensor_copy(lists, bank[7][0:CAP, 0:2 * EXPERTS]).then_inc(lists_done, 1)
            dve.wait_ge(slot_psum, 1)
            choice, other = [bank[7][0:CAP, 256 + EXPERTS * i:256 + EXPERTS * (i + 1)] for i in range(2)]
            link(v.tensor_copy(slots, choice))
            link(v.scalar_tensor_tensor(out=empty[:], in0=slots, scalar=0.0, in1=other, op0=ALU.is_equal, op1=ALU.mult))
            link(v.tensor_tensor(slots, slots, empty[:], ALU.add))
            v.tensor_scalar(gidx[:], slots, -1.0, float(T), ALU.mult, ALU.add).then_inc(idx_done, 1)
            dve.wait_ge(idx_done, 1)

            def to_gather(e, i):
                v.tensor_copy(gcol[i][:], gidx[:, bass.ds(e, 1)]).then_inc(gcol_done, 1)

            for e in range(GBUF):
                to_gather(e, e)
            link(v.tensor_scalar(slotv[:, 1], slots, slotc[0:CAP, 0:1], None, ALU.mult))
            link(v.scalar_tensor_tensor(out=empty[:], in0=slotv[:, 1], scalar=0.0, in1=slotc[0:CAP, 2:], op0=ALU.is_equal, op1=ALU.mult))
            link(v.tensor_scalar(slotv[:, 0], slotv[:, 1], -1.0, float(T), ALU.mult, ALU.add))
            link(v.tensor_tensor(sidx[:], slotv[:, 0], empty[:], ALU.add))
            for j in SD_ORDER[:3]:
                add_shared(j)

            def rows_across(e, u):
                dve.wait_ge(gT_psum, e + 1)
                dve.wait_ge(up_psum, e + 1)
                dve.nop(nofuse=True)
                v.tensor_copy(gxT[u], bank[u][:, 0:KC * CAP].rearrange("p (k t) -> p k t", k=KC)).then_inc(gxT_done, 1)

            def expert(e, lap, r, more, across):
                u = r % 2
                dve.wait_ge(silu_done, 2 * e + 2)
                dve.wait_ge(down_psum, e + 1)
                dve.nop(nofuse=True)
                v.tensor_tensor(hid[u][:, 0], silu[u][:, 0], bank[2 + u][:, CAP:2 * CAP], ALU.mult).then_inc(hid_done, 1)
                v.tensor_tensor(hid[u][0:MR, 1], silu[u][0:MR, 1], bank[2 + u][0:MR, 2 * CAP:3 * CAP], ALU.mult).then_inc(hid_done, 1)
                if across:
                    rows_across(e + 2, u)
                dve.wait_ge(got_rows[r % GBUF], lap * (16 * RING // GBUF) + 16 * (r // GBUF + 1))
                dve.wait_ge(orow_done, e + 1)
                dve.nop(nofuse=True)
                v.tensor_scalar(gw[u][:], gx[r % GBUF][:, bass.ds(e + D, 1)], slotc[0:CAP, 0:1], slotc[0:CAP, 1:2], ALU.mult, ALU.add).then_inc(gw_done, 1)
                dve.wait_ge(acc_in[u], lap * (8 * RING) + FILL[u] + 16 * (r // 2) - 16)
                dve.nop(nofuse=True)
                v.tensor_copy(scol[r % OBUF][:], sidx[:, bass.ds(e, 1)]).then_inc(scol_done, 1)
                if more:
                    to_gather(e + GBUF, r % GBUF)

            rows_across(0, 0)
            add_shared(SD_ORDER[3])
            rows_across(1, 1)
            with dve.Fori(0, EXPERTS // RING - 1) as lap:
                for r in range(RING):
                    expert(lap * RING + r, lap, r, True, True)
            for r in range(RING):
                e = EXPERTS - RING + r
                expert(e, EXPERTS // RING - 1, r, e + GBUF < EXPERTS, e + 2 < EXPERTS)

            dve.wait_ge(got_last, 32)
            v.tensor_tensor(lastrow[:, 2], lastrow[:, 0], lastrow[:, 1], ALU.add).then_inc(last_done, 1)
            for j in range(4):
                dve.wait_ge(got_acc[j], 32)
                two = xn[:, 2 * j:2 * j + 2]
                v.tensor_tensor(two, two, xq[:, 2 * j:2 * j + 2], ALU.add).then_inc(sum_done, 1)
                dve.wait_ge(sum_done, j + 1)
                dve.wait_ge(corr_psum, j + 1)
                v.tensor_tensor(two, two, bank[j][:].rearrange("p (b h) -> p b h", b=2), ALU.add).then_inc(y_done, 1)

        @block.tensor
        def _(pe):
            t = nc.tensor
            pe.sem_inc(pv_psum, 2)
            pe.sem_inc(heads_psum, 2)
            pe.sem_inc(up_psum, 2)
            pe.sem_inc(down_psum, 2)

            def unit(u):
                what, c, h = units[u]
                if u >= UNIT_BUF:
                    pe.wait_ge(unit_rest, u - UNIT_BUF + 1)
                for k in range(KC):
                    w = wkv[:, k, P * c:P * c + P] if what == "k" else wqT[:, k, P * c:P * c + P]
                    src = ctxT if what == "k" else xqT
                    last = t.matmul(bank[u % UNIT_BUF][:], w, src[:, k, 512 * h:512 * h + 512], start=(k == 0), stop=(k == KC - 1))
                last.then_inc(unit_psum, 1)

            def values_of(j):
                for b in (2 * j, 2 * j + 1):
                    for k in range(KC):
                        last = t.matmul(bank[V_BANK[j]][:, D * (b % 2):D * (b % 2) + D], ctxT[:, k, P * b:P * b + P], wkv[:, k, D:2 * D],
                                        start=(k == 0), stop=(k == KC - 1))
                last.then_inc(v_psum, 1)

            def xq_across(j):
                pe.wait_ge(xq_done, 2 * j + 2)
                if j >= 2:
                    pe.wait_ge(xqT_done, j - 1)
                for k in range(KC):
                    for b in (2 * j, 2 * j + 1):
                        last = t.transpose(bank[6 + j % 2][:, 256 * k + P * (b % 2):256 * k + P * (b % 2) + P], xq[:, b, P * k:P * k + P], ident[:])
                last.then_inc(xqT_psum, 1)

            pe.wait_ge(got_kv, 16)
            pe.wait_ge(got_ctx, 16)
            unit(0)
            unit(1)
            pe.wait_ge(w_done, 2)
            pe.wait_ge(got_const, 48)
            for c in range(2):
                for k in range(KC):
                    last = t.transpose(bank[4][:, 256 * c + P * k:256 * c + P * k + P], w_rows[:, c, P * k:P * k + P], ident[:])
            last.then_inc(w_psum, 1)
            xq_across(0)
            xq_across(1)
            pe.wait_ge(got_ctx2, 16)
            unit(2)
            pe.wait_ge(wT_done, 1)
            pe.wait_ge(xqT_done, 2)
            unit(3)
            unit(4)
            xq_across(2)
            xq_across(3)
            unit(5)
            pe.wait_ge(got_w2, 32)
            values_of(0)
            pe.wait_ge(xqT_done, 4)
            unit(6)
            unit(7)

            pe.wait_ge(w_done, 6)
            pe.wait_ge(consts_b, 3)
            wp_bank = bank[5][:, 0:256].bitcast(bf16)
            for c in range(2):
                for k in range(KC):
                    last = t.transpose(wp_bank[:, 256 * c + P * k:256 * c + P * k + P], wp_int[:, c, P * k:P * k + P], identb[:])
            last.then_inc(w_psum, 1)
            values_of(1)
            values_of(2)
            pe.wait_ge(v_done, 2)
            values_of(3)

            def scores(b, g):
                for h in range(4 * g, 4 * g + 4):
                    last = t.matmul(bank[g % 2][:, P * (h % 4):P * (h % 4) + P], qs[:, bass.ds(b * TOK + h * T, TOK)], ks[:, bass.ds(b * TOK + h * T, TOK)],
                                    start=True, stop=True)
                last.then_inc(s_psum, 1)

            def scores_t(b, g, u):
                pe.wait_ge(exp_done, 4 * b + g + 1)
                for h in range(4 * g, 4 * g + 4):
                    dst = bank[2 + g % 2][:, P * (h % 4):P * (h % 4) + P]
                    t.matmul(dst, ks[:, bass.ds(b * TOK + h * T, TOK)], qs[:, bass.ds(b * TOK + h * T, TOK)], start=True, stop=False)
                    last = t.matmul(dst, pick[:, h], negmaxT[u][:], start=False, stop=True)
                last.then_inc(st_psum, 1)

            def heads_times_values(b, g, u):
                pe.wait_ge(exp_done, 4 * b + g + 3)
                if g == 0:
                    pe.wait_ge(headsT_done, b + 1)
                    pe.wait_ge(vpad_done, b + 1)
                for i in range(4):
                    h = 4 * g + i
                    last = t.matmul(bank[4][VW * i:VW * i + VW, TOK * g:TOK * g + TOK], vpad[u][:, VW * h:VW * h + VW], probs[u][:, TOK * h:TOK * h + TOK],
                                    start=True, stop=True)
                if g == 3:
                    last.then_inc(pv_psum, 1)

            def heads_across(b, u):
                pe.wait_ge(headsT_done, b + 2)
                pe.wait_ge(norm_done, b + 1)
                for g in range(4):
                    last = t.transpose(bank[6][:, TOK * g:TOK * g + TOK], headsT[u][:, TOK * g:TOK * g + TOK], ident[:])
                last.then_inc(heads_psum, 1)

            def negmax_across(b, u):
                pe.wait_ge(split_done, 2 * b + 2)
                t.transpose(bank[7][0:2 * HEADS, 0:TOK // 2].bitcast(bf16), negmax[:, u], identb[:]).then_inc(nm_psum, 1)

            def next_scores(b, g):
                pe.wait_ge(max_done, 4 * b + g - 1)
                scores(b, g)

            def heads_row(m, u):
                pe.wait_ge(oq_done, m + 1)
                pe.wait_ge(y1_done, m + 1)
                for k in range(KC):
                    last = t.transpose(bank[5][:, 0:TOK].bitcast(bf16)[:, P * k:P * k + P], oq_flat[:, bass.ds(m * D + P * k, P)], identb[:])
                last.then_inc(oT_psum, 1)

            def project(m, u):
                pe.wait_ge(oT_done, m + 1)
                for k in range(KC):
                    last = t.matmul(bank[5][:, D:2 * D], oT[u][:, k], wpT[:, k], start=(k == 0), stop=(k == KC - 1))
                last.then_inc(y_psum, 1)

            def attend(b, u, more, before):
                for g in range(4):
                    if g == 0:
                        pe.wait_ge(nm_done, b + 1)
                    elif g < 3 and more:
                        next_scores(b + 1, g + 1)
                    elif g == 3 and more > 1:
                        if u == 0:
                            pe.wait_ge(stack_ready, b // 2 + 2)
                        next_scores(b + 2, 0)
                    if g == 1 and before:
                        heads_across(b - 1, 1 - u)
                    scores_t(b, g, u)
                    if g == 0 and before > 1:
                        heads_row(b - 2, u)
                    if g == 2 and before > 1:
                        project(b - 2, u)
                    if g:
                        heads_times_values(b, g - 1, u)
                if more > 1:
                    next_scores(b + 2, 1)
                if more:
                    negmax_across(b + 1, 1 - u)
                heads_times_values(b, 3, u)

            oq_flat = oq[:].rearrange("p b h -> p (b h)")
            pe.wait_ge(unit_rest, 8)
            pe.wait_ge(stack_ready, 1)
            scores(0, 0)
            scores(0, 1)
            pe.wait_ge(wT_done, 2)
            pe.wait_ge(pool_set, 4)
            t.matmul(bank[5][:, 256:512], onesf[:], wdiag[:].rearrange("p c o -> p (c o)"), start=True, stop=True).then_inc(w_psum, 1)
            for b, g in ((0, 2), (0, 3), (1, 0), (1, 1)):
                pe.wait_ge(max_done, 4 * b + g - 1)
                scores(b, g)
            pe.wait_ge(v_done, TILES)
            negmax_across(0, 0)
            pe.wait_ge(wT_done, 3)
            for b in range(TILES):
                attend(b, b % 2, min(2, TILES - 1 - b), min(2, b))

            def h_across(j):
                pe.wait_ge(h_done, 2 * j + 2)
                for k in range(KC):
                    for b in (2 * j, 2 * j + 1):
                        last = t.transpose(bank[H_BANK[j]][:, 256 * k + P * (b % 2):256 * k + P * (b % 2) + P], rows[:, b, P * k:P * k + P], ident[:])
                last.then_inc(hT_psum, 1)

            def logits(j):
                pe.wait_ge(hT_done, j + 1)
                half = j // 2
                for b in (2 * j, 2 * j + 1):
                    for k in range(KC):
                        last = t.matmul(bank[LOGIT_BANK[half]][:, EXPERTS * b:EXPERTS * b + EXPERTS], hT[:, k, P * b:P * b + P], gateT[:, k], start=(k == 0), stop=(k == KC - 1))
                last.then_inc(logit_psum, 1)

            def shared_up(u, which=(0, 1)):
                h, c = u // 3, u % 3
                m0, n = SCH[c]
                if u >= 2:
                    pe.wait_ge(sup_done, u - 1)
                for i in which:
                    for k in range(KC):
                        last = t.matmul(bank[2 * (u % 2) + i][0:n], sgu[:, k, i, m0:m0 + n], hT[:, k, 512 * h:512 * h + 512], start=(k == 0), stop=(k == KC - 1))
                if 1 in which:
                    last.then_inc(sg_psum, 1)

            heads_across(TILES - 1, 1)
            heads_row(TILES - 2, 0)
            pe.wait_ge(max_done, 4 * TILES)
            pe.wait_ge(exp_done, 4 * TILES + 2)
            h_across(0)
            h_across(1)
            project(TILES - 2, 0)
            pe.wait_ge(got_gate, 16)
            logits(0)
            logits(1)
            heads_row(TILES - 1, 1)
            project(TILES - 1, 1)
            pe.wait_ge(got_shared, 48)
            shared_up(0)
            pe.wait_ge(headsT_done, TILES + 1)
            pe.wait_ge(y1_done, TILES + 1)
            h_across(2)
            pe.wait_ge(norm_done, TILES + 1)
            logits(2)
            h_across(3)
            logits(3)
            shared_up(1)
            shared_up(2, (0,))
            pe.wait_ge(sel_done, 2)
            selT = bank[4][:, 0:HALF // 2].bitcast(bf16)
            for b in range(TILES):
                half = b // 4
                last = t.transpose(selT[EXPERTS * half:EXPERTS * (half + 1), P * (b % 4):P * (b % 4) + P], sel[:, b], identb[:])
            last.then_inc(selT_psum, 1)
            for b in range(TILES):
                dst = bank[6][:, EXPERTS * b:EXPERTS * b + EXPERTS]
                for c in range(b):
                    t.matmul(dst, onesb[:], sel[:, c], start=(c == 0), stop=False)
                last = t.matmul(dst, beforeb[:], sel[:, b], start=(b == 0), stop=True)
            last.then_inc(pos_psum, 1)
            def shared_down(j):
                for b in (2 * j, 2 * j + 1):
                    for c, (m0, n) in enumerate(SCH):
                        last = t.matmul(bank[SD_BANK[j]][:, D * (b % 2):D * (b % 2) + D], sact[0:n, c * T + P * b:c * T + P * b + P], sdn[0:n, c], start=(c == 0), stop=(c == 2))
                last.then_inc(sd_psum, 1)

            shared_up(2, (1,))
            shared_up(3)
            shared_up(4)
            pe.wait_ge(over_done, 1)
            for j in range(2):
                if j:
                    pe.wait_ge(sact_done, 3)
                    shared_down(1)
                    pe.wait_ge(overT_done, j)
                for b in range(4):
                    last = t.transpose(bank[7][0:EXPERTS, P * b:P * b + P], over[:, 4 * j + b], ident[:])
                last.then_inc(overT_psum, 1)
            shared_up(5)
            pe.wait_ge(key_made, 1)
            pe.wait_ge(selS_done, 1)
            shared_down(0)
            pe.wait_ge(order_done, 1)
            pe.wait_ge(overT_done, 2)
            t.transpose(bank[7][0:CAP, 0:2 * EXPERTS], order[:], ident[:]).then_inc(lists_psum, 1)
            pe.wait_ge(lists_done, 1)
            pe.wait_ge(slotc_done, 2)
            pe.wait_ge(got_reverse, 16)
            of_first, of_second = lists[:, 0:EXPERTS], lists[:, EXPERTS:2 * EXPERTS]
            for i, (w, src, w_last, src_last) in enumerate(((first, of_first, once, of_second), (reverse[:], of_second, once, of_first))):
                dst = bank[7][0:CAP, 256 + EXPERTS * i:256 + EXPERTS * (i + 1)]
                t.matmul(dst, w, src, start=True, stop=False)
                last = t.matmul(dst, w_last, src_last, start=False, stop=True)
            last.then_inc(slot_psum, 1)
            pe.wait_ge(sact_done, 6)
            shared_down(3)
            shared_down(2)

            def rows_across(e, lap, r):
                pe.wait_ge(got_rows[r % GBUF], lap * (16 * RING // GBUF) + 16 * (r // GBUF + 1))
                pe.wait_ge(gxT_done, e + 1)
                pe.nop(nofuse=True)
                for k in range(KC):
                    last = t.transpose(bank[r % 2][:, CAP * k:CAP * k + CAP], gx[r % GBUF][:, P * k:P * k + P], ident[0:CAP, 0:CAP])
                last.then_inc(gT_psum, 1)

            def up(e, lap, r):
                s, lap = r % RING, lap + r // RING
                pe.wait_ge(got_expert[s], lap * 48 + 48)
                pe.wait_ge(gxT_done, e + 3)
                pe.wait_ge(hid_done, 2 * e + 2)
                pe.nop(nofuse=True)
                for i, (c0, n) in enumerate(UP_COLS):
                    for k in range(KC):
                        last = t.matmul(bank[2 + r % 2][0:n, CAP * i:CAP * i + CAP], wgu[s][:, k, c0:c0 + n], gxT[r % 2][:, k],
                                        start=(k == 0), stop=(k == KC - 1))
                last.then_inc(up_psum, 1)

            def down(e, r):
                pe.wait_ge(hid_done, 2 * e + 6)
                pe.wait_ge(orow_done, e + 1)
                pe.nop(nofuse=True)
                for c, n in enumerate((P, MR)):
                    last = t.matmul(bank[4 + r % 2][0:CAP, 0:D], hid[r % 2][0:n, c], wdn[r][0:n, c], start=(c == 0), stop=(c == 1))
                last.then_inc(down_psum, 1)

            rows_across(0, 0, 0)
            rows_across(1, 0, 1)
            up(0, 0, 0)
            pe.wait_ge(base_done, TILES)
            with pe.Fori(0, EXPERTS // RING - 1) as lap:
                for r in range(RING):
                    up(lap * RING + (r + 1), lap, r + 1)
                    rows_across(lap * RING + (r + 2), lap, r + 2)
                    down(lap * RING + r, r)
            lap = EXPERTS // RING - 1
            for r in range(RING):
                e = lap * RING + r
                if e + 1 < EXPERTS:
                    up(e + 1, lap, r + 1)
                if e + 2 < EXPERTS:
                    rows_across(e + 2, lap, r + 2)
                down(e, r)
            pe.wait_ge(last_done, 1)
            pe.wait_ge(hid_done, 2 * EXPERTS + 4)
            for j in range(4):
                for b in (2 * j, 2 * j + 1):
                    last = t.matmul(bank[j][:, D * (b % 2):D * (b % 2) + D], overT[:, P * b:P * b + P], lastrow[:, 2], start=True, stop=True)
                last.then_inc(corr_psum, 1)


def constants():
    slot = np.arange(P)
    notlast = np.where(slot == CAP - 1, 0.0, 1.0)
    spare = np.repeat(slot[:, None].astype(np.float64), EXPERTS, 1)
    spare[CAP - 1] = CAP + np.arange(EXPERTS)
    c = np.concatenate([np.eye(P), np.triu(np.ones((P, P)), 1), notlast[:, None], 1 - notlast[:, None], spare], 1)
    tok = np.arange(T).reshape(2, 1, HALF)
    tokv = np.repeat(np.stack([T - tok, tok + 1], 2), EXPERTS, 1).reshape(P, 2, HALF)
    reverse = np.zeros((CAP, CAP))
    reverse[:CAP - 1, :CAP - 1] = np.eye(CAP - 1)[::-1]
    return c.astype(np.float32), tokv.astype(np.float32), reverse.astype(np.float32)


def kernel(**inputs):
    import concourse.bacc as _bacc
    from concourse.bass_utils import run_bass_kernel_spmd as _run

    g = {k: np.asarray(v) for k, v in inputs.items()}
    n = lambda k: g["L0_" + k]
    lay = np.ascontiguousarray
    consts, tokv, reverse = constants()
    chunks = lambda t: lay(t.reshape(KC, P, -1).transpose(1, 0, 2))
    wg, wu = n("ffn_Wg"), n("ffn_Wu")
    gap = np.zeros((EXPERTS, GATE_AT - MR, D), wg.dtype)
    wgu = np.concatenate([wg[:, :P], wu[:, :P], wu[:, P:], gap, wg[:, P:]], 1)
    arrays = {
        "x": lay(g["x"].transpose(1, 0, 2)),
        "ctxT": chunks(g["ctx_2048"].reshape(T, D).T),
        "wkv": chunks(n("xattn_wkv").T),
        "w_rows": lay(np.concatenate([n("xattn_wq").reshape(2, P, D), n("xattn_wp").reshape(2, P, D)]).transpose(1, 0, 2)),
        "bqk": lay(np.concatenate([n("xattn_bq").reshape(2, P), n("xattn_bkv")[:D].reshape(2, P)]).T),
        "bvp": np.stack([n("xattn_bkv")[D:], n("xattn_bp")]),
        "gates": np.concatenate([g["g_xattn"], g["g_ffn"]])[None],
        "consts": consts,
        "tokv": tokv,
        "reverse": reverse,
        "gateT": chunks(n("ffn_gate_weight").T),
        "wgu": lay(wgu.reshape(EXPERTS, WG, KC, P).transpose(0, 3, 2, 1)),
        "wdn": lay(n("ffn_Wd").transpose(0, 2, 1)),
        "sgu": lay(np.stack([n("ffn_Sg"), n("ffn_Su")]).reshape(2, MS, KC, P).transpose(3, 2, 0, 1)),
        "sdn": lay(n("ffn_Sd").T),
    }
    nc = _bacc.Bacc("TRN2", target_bir_lowering=False, num_devices=1)
    a = {k: nc.dram_tensor(k + "_in", t.shape, mybir.dt.from_np(t.dtype), kind="ExternalInput").ap() for k, t in arrays.items()}
    out = nc.dram_tensor("out", (TILES, TOK, D), mybir.dt.float32, kind="ExternalOutput").ap()
    gated_block(nc, a, out)
    r = _run(nc, [{k + "_in": t for k, t in arrays.items()}], core_ids=[0])
    return r.results[0]["out"]
```
